# Optimizing a Trainium2 kernel written in Bass

```python
import numpy as np
import jax
import jax.numpy as jnp

def _softmax(x, axis=-1):
    return jax.nn.softmax(x, axis=axis)

def _gelu(x):
    return jax.nn.gelu(x, approximate=True)

def _silu(x):
    return jax.nn.silu(x)

def _sigmoid(x):
    return jax.nn.sigmoid(x)

def _layernorm(x, axis=-1, eps=1e-05):
    m = jnp.mean(x, axis=axis, keepdims=True)
    v = jnp.var(x, axis=axis, keepdims=True)
    return (x - m) / jnp.sqrt(v + eps)

def _scatter_add(tgt, idx, src, axis=0):
    return tgt.at[idx].add(src)

def _segment_sum(src, seg, n):
    return jax.ops.segment_sum(src, seg, n)
kernel_name = 'mk_gnn_resnorm_d4_gnn_r32_239dbd'

def setup_inputs(seed: int=0):
    np.random.seed(seed)
    _w = jnp.asarray

    def _rec_inputs():
        import jax
        import jax.numpy as jnp
        _gk = jax.random.key(seed)
        x = -0.000202 + 1 * jax.random.normal(jax.random.fold_in(_gk, 1), (3125, 128), jnp.float32)
        src = jax.random.randint(jax.random.fold_in(_gk, 2), (50000,), 0, 3125, jnp.int32)
        dst = jnp.minimum((3125 * jax.random.uniform(jax.random.fold_in(_gk, 3), (50000,)) ** 2.0).astype(jnp.int32), 99999)
        _o = jnp.argsort(dst, stable=True)
        src = src[_o]
        dst = dst[_o]
        edge_type_8 = jax.random.randint(jax.random.fold_in(_gk, 13), (50000,), 0, 8, jnp.int32)
        node_type_8 = jax.random.randint(jax.random.fold_in(_gk, 14), (3125,), 0, 8, jnp.int32)
        return (x, src, dst, edge_type_8, node_type_8)
    x, src, dst, edge_type_8, node_type_8 = _rec_inputs()

    def _L0_gnn_setup():
        import jax, jax.numpy as jnp
        import numpy as np
        N = 50000
        E = 12500
        HID = 128
        H = 8
        HS = HID // H
        TN = 8
        R = 8
        L = 2
        OUT = 128
        EPS = 1e-05
        SQRT_D = float(np.sqrt(HS))

        def typed_linear(x, types, W):
            out = jnp.zeros((x.shape[0], W.shape[-1]), x.dtype)
            for t in range(W.shape[0]):
                out = out + jnp.where((types == t)[:, None], x @ W[t], 0.0)
            return out

        def rel_apply(h, etype, W):
            out = jnp.zeros_like(h)
            for r in range(W.shape[1]):
                out = out + jnp.where((etype == r)[:, None, None], jnp.einsum('ehi,hio->eho', h, W[:, r]), 0.0)
            return out

        def gt_layer(x, src, dst, ntype, etype, Wk, Wq, Wv, Wa, pri, Watt, Wmsg, skip, g, b):
            n = x.shape[0]
            k = typed_linear(x, ntype, Wk).reshape(n, H, HS)
            q = typed_linear(x, ntype, Wq).reshape(n, H, HS)
            v = typed_linear(x, ntype, Wv).reshape(n, H, HS)
            k_j, q_i, v_j = (k[src], q[dst], v[src])
            kw = rel_apply(k_j, etype, Watt)
            a = (kw * q_i).sum(-1) * pri[:, etype].T / SQRT_D
            amax = jax.ops.segment_max(a, dst, num_segments=n)
            ex = jnp.exp(a - amax[dst])
            den = jax.ops.segment_sum(ex, dst, num_segments=n)
            alpha = ex / (den[dst] + 1e-16)
            m = rel_apply(v_j, etype, Wmsg)
            agg = jax.ops.segment_sum(alpha[..., None] * m, dst, num_segments=n)
            out = jax.nn.silu(typed_linear(agg.reshape(n, HID), ntype, Wa))
            al = jax.nn.sigmoid(skip[ntype])[:, None]
            out = out * al + x * (1.0 - al)
            mu = out.mean(-1, keepdims=True)
            var = ((out - mu) ** 2).mean(-1, keepdims=True)
            return (out - mu) / jnp.sqrt(var + EPS) * g + b
        key = jax.random.key(seed)
        ks = jax.random.split(key, 12)
        s = 1.0 / np.sqrt(HID)
        sh = 1.0 / np.sqrt(HS)
        return {'x': jax.random.normal(ks[0], (N, HID), jnp.float32), 'edge_index': jax.random.randint(ks[1], (2, E), 0, N, dtype=jnp.int32), 'ntype': jax.random.randint(ks[2], (N,), 0, TN, dtype=jnp.int32), 'etype': jax.random.randint(ks[3], (E,), 0, R, dtype=jnp.int32), 'Wk': jax.random.normal(ks[4], (L, TN, HID, HID), jnp.float32) * s, 'Wq': jax.random.normal(ks[5], (L, TN, HID, HID), jnp.float32) * s, 'Wv': jax.random.normal(ks[6], (L, TN, HID, HID), jnp.float32) * s, 'Wa': jax.random.normal(ks[7], (L, TN, HID, HID), jnp.float32) * s, 'pri': jnp.ones((L, H, R), jnp.float32), 'Watt': jax.random.normal(ks[8], (L, H, R, HS, HS), jnp.float32) * sh, 'Wmsg': jax.random.normal(ks[9], (L, H, R, HS, HS), jnp.float32) * sh, 'skip': jnp.ones((L, TN), jnp.float32), 'ln_g': jnp.ones((L, HID), jnp.float32), 'ln_b': jnp.zeros((L, HID), jnp.float32), 'Wff': jax.random.normal(ks[10], (HID, OUT), jnp.float32) * s, 'bff': jnp.zeros((OUT,), jnp.float32)}
    _L0_gnn_all = _L0_gnn_setup()
    _L0_gnn_in = {k: v for k, v in _L0_gnn_all.items() if k in ('Wk', 'Wq', 'Wv', 'Wa', 'pri', 'Watt', 'Wmsg', 'skip', 'ln_g', 'ln_b', 'Wff', 'bff')}
    del _L0_gnn_all

    def _L1_gnn_setup():
        import jax, jax.numpy as jnp
        import numpy as np
        N_NODES = 3125
        N_EDGES = 50000
        HIDDEN = 128
        key = jax.random.key(seed)
        ks = jax.random.split(key, 7)
        s = 1.0 / np.sqrt(HIDDEN)
        user_states = jax.random.normal(ks[0], (N_NODES, HIDDEN), dtype=jnp.float32)
        edge_src = jax.random.randint(ks[1], (N_EDGES,), 0, N_NODES)
        edge_dst = jax.random.randint(ks[2], (N_EDGES,), 0, N_NODES)
        W_self = jax.random.uniform(ks[3], (HIDDEN, HIDDEN), minval=-s, maxval=s, dtype=jnp.float32)
        b_self = jax.random.uniform(ks[4], (HIDDEN,), minval=-s, maxval=s, dtype=jnp.float32)
        W_neigh = jax.random.uniform(ks[5], (HIDDEN, HIDDEN), minval=-s, maxval=s, dtype=jnp.float32)
        b_neigh = jax.random.uniform(ks[6], (HIDDEN,), minval=-s, maxval=s, dtype=jnp.float32)
        return {'user_states': user_states, 'edge_src': edge_src, 'edge_dst': edge_dst, 'W_self': W_self, 'b_self': b_self, 'W_neigh': W_neigh, 'b_neigh': b_neigh}
    _L1_gnn_all = _L1_gnn_setup()
    _L1_gnn_in = {k: v for k, v in _L1_gnn_all.items() if k in ('W_self', 'b_self', 'W_neigh', 'b_neigh')}
    del _L1_gnn_all

    def _L2_gnn_setup():
        import jax, jax.numpy as jnp
        import numpy as np
        N = 3125
        E = 18750
        D_IN = 128
        D = 128
        L = 3

        def gru_cell(m, h, w_ih, w_hh, b_ih, b_hh):
            gi = m @ w_ih.T + b_ih
            gh = h @ w_hh.T + b_hh
            ir, iz, inn = jnp.split(gi, 3, axis=-1)
            hr, hz, hn = jnp.split(gh, 3, axis=-1)
            r = jax.nn.sigmoid(ir + hr)
            z = jax.nn.sigmoid(iz + hz)
            n = jnp.tanh(inn + r * hn)
            return (1.0 - z) * n + z * h
        key = jax.random.key(seed)
        ks = jax.random.split(key, 10)
        s = 1.0 / np.sqrt(D)
        x = jax.random.normal(ks[0], (N, D_IN), dtype=jnp.float32)
        edge_index = jax.random.randint(ks[1], (2, E), 0, N, dtype=jnp.int64)
        lin_w = jax.random.normal(ks[2], (D, D_IN), dtype=jnp.float32) * (1.0 / np.sqrt(D_IN))
        lin_b = jnp.zeros((D,), dtype=jnp.float32)
        weight = jax.random.normal(ks[3], (L, D, D), dtype=jnp.float32) * s
        w_ih = jax.random.normal(ks[4], (3 * D, D), dtype=jnp.float32) * s
        w_hh = jax.random.normal(ks[5], (3 * D, D), dtype=jnp.float32) * s
        b_ih = jnp.zeros((3 * D,), dtype=jnp.float32)
        b_hh = jnp.zeros((3 * D,), dtype=jnp.float32)
        return {'x': x, 'lin_w': lin_w, 'lin_b': lin_b, 'weight': weight, 'w_ih': w_ih, 'w_hh': w_hh, 'b_ih': b_ih, 'b_hh': b_hh, 'edge_index': edge_index}
    _L2_gnn_all = _L2_gnn_setup()
    _L2_gnn_in = {k: v for k, v in _L2_gnn_all.items() if k in ('lin_w', 'lin_b', 'weight', 'w_ih', 'w_hh', 'b_ih', 'b_hh')}
    del _L2_gnn_all

    def _L3_gnn_setup():
        import jax, jax.numpy as jnp
        import numpy as np
        NEG_SLOPE = 0.2
        N_NODES = 50000

        def gat_conv(x, src, dst, W, a_src, a_dst, b, n_nodes):
            H, C = a_src.shape
            h = (x @ W).reshape(-1, H, C)
            s_src = jnp.sum(h * a_src[None], axis=-1)
            s_dst = jnp.sum(h * a_dst[None], axis=-1)
            e = jax.nn.leaky_relu(s_src[src] + s_dst[dst], NEG_SLOPE)
            m = jax.ops.segment_max(e, dst, num_segments=n_nodes)
            w = jnp.exp(e - m[dst])
            denom = jax.ops.segment_sum(w, dst, num_segments=n_nodes)
            alpha = w / denom[dst]
            out = jax.ops.segment_sum(alpha[:, :, None] * h[src], dst, num_segments=n_nodes)
            return out
        key = jax.random.key(seed)
        ks = jax.random.split(key, 12)
        N, F_in, Hid, H, F_out = (N_NODES, 128, 64, 4, 128)
        E = 25000
        x = jax.random.normal(ks[0], (N, F_in), dtype=jnp.float32)
        edge_index = jax.random.randint(ks[1], (2, E), 0, N, dtype=jnp.int64)
        sc = 0.1
        return {'x': x, 'edge_index': edge_index, 'W1': jax.random.normal(ks[2], (F_in, H * Hid), dtype=jnp.float32) * sc, 'att_src1': jax.random.normal(ks[3], (H, Hid), dtype=jnp.float32) * sc, 'att_dst1': jax.random.normal(ks[4], (H, Hid), dtype=jnp.float32) * sc, 'b1': jnp.zeros((H * Hid,), dtype=jnp.float32), 'W2': jax.random.normal(ks[5], (H * Hid, F_out), dtype=jnp.float32) * sc, 'att_src2': jax.random.normal(ks[6], (1, F_out), dtype=jnp.float32) * sc, 'att_dst2': jax.random.normal(ks[7], (1, F_out), dtype=jnp.float32) * sc, 'b2': jnp.zeros((F_out,), dtype=jnp.float32)}
    _L3_gnn_all = _L3_gnn_setup()
    _L3_gnn_in = {k: v for k, v in _L3_gnn_all.items() if k in ('W1', 'att_src1', 'att_dst1', 'b1', 'W2', 'att_src2', 'att_dst2', 'b2')}
    del _L3_gnn_all
    return {'x': x, 'src': src, 'dst': dst, 'edge_type_8': edge_type_8, 'node_type_8': node_type_8, 'L0_gnn_Wk': _L0_gnn_in['Wk'], 'L0_gnn_Wq': _L0_gnn_in['Wq'], 'L0_gnn_Wv': _L0_gnn_in['Wv'], 'L0_gnn_Wa': _L0_gnn_in['Wa'], 'L0_gnn_pri': _L0_gnn_in['pri'], 'L0_gnn_Watt': _L0_gnn_in['Watt'], 'L0_gnn_Wmsg': _L0_gnn_in['Wmsg'], 'L0_gnn_skip': _L0_gnn_in['skip'], 'L0_gnn_ln_g': _L0_gnn_in['ln_g'], 'L0_gnn_ln_b': _L0_gnn_in['ln_b'], 'L0_gnn_Wff': _L0_gnn_in['Wff'], 'L0_gnn_bff': _L0_gnn_in['bff'], 'L1_gnn_W_self': _L1_gnn_in['W_self'], 'L1_gnn_b_self': _L1_gnn_in['b_self'], 'L1_gnn_W_neigh': _L1_gnn_in['W_neigh'], 'L1_gnn_b_neigh': _L1_gnn_in['b_neigh'], 'L2_gnn_lin_w': _L2_gnn_in['lin_w'], 'L2_gnn_lin_b': _L2_gnn_in['lin_b'], 'L2_gnn_weight': _L2_gnn_in['weight'], 'L2_gnn_w_ih': _L2_gnn_in['w_ih'], 'L2_gnn_w_hh': _L2_gnn_in['w_hh'], 'L2_gnn_b_ih': _L2_gnn_in['b_ih'], 'L2_gnn_b_hh': _L2_gnn_in['b_hh'], 'L3_gnn_W1': _L3_gnn_in['W1'], 'L3_gnn_att_src1': _L3_gnn_in['att_src1'], 'L3_gnn_att_dst1': _L3_gnn_in['att_dst1'], 'L3_gnn_b1': _L3_gnn_in['b1'], 'L3_gnn_W2': _L3_gnn_in['W2'], 'L3_gnn_att_src2': _L3_gnn_in['att_src2'], 'L3_gnn_att_dst2': _L3_gnn_in['att_dst2'], 'L3_gnn_b2': _L3_gnn_in['b2']}

def reference(x, src, dst, edge_type_8, node_type_8, L0_gnn_Wk, L0_gnn_Wq, L0_gnn_Wv, L0_gnn_Wa, L0_gnn_pri, L0_gnn_Watt, L0_gnn_Wmsg, L0_gnn_skip, L0_gnn_ln_g, L0_gnn_ln_b, L0_gnn_Wff, L0_gnn_bff, L1_gnn_W_self, L1_gnn_b_self, L1_gnn_W_neigh, L1_gnn_b_neigh, L2_gnn_lin_w, L2_gnn_lin_b, L2_gnn_weight, L2_gnn_w_ih, L2_gnn_w_hh, L2_gnn_b_ih, L2_gnn_b_hh, L3_gnn_W1, L3_gnn_att_src1, L3_gnn_att_dst1, L3_gnn_b1, L3_gnn_W2, L3_gnn_att_src2, L3_gnn_att_dst2, L3_gnn_b2):
    import jax
    import jax.numpy as jnp

    def _L0_gnn_ref(x, edge_index, ntype, etype, Wk, Wq, Wv, Wa, pri, Watt, Wmsg, skip, ln_g, ln_b, Wff, bff):
        import jax, jax.numpy as jnp
        import numpy as np
        N = 50000
        E = 12500
        HID = 128
        H = 8
        HS = HID // H
        TN = 8
        R = 8
        L = 2
        OUT = 128
        EPS = 1e-05
        SQRT_D = float(np.sqrt(HS))

        def typed_linear(x, types, W):
            out = jnp.zeros((x.shape[0], W.shape[-1]), x.dtype)
            for t in range(W.shape[0]):
                out = out + jnp.where((types == t)[:, None], x @ W[t], 0.0)
            return out

        def rel_apply(h, etype, W):
            out = jnp.zeros_like(h)
            for r in range(W.shape[1]):
                out = out + jnp.where((etype == r)[:, None, None], jnp.einsum('ehi,hio->eho', h, W[:, r]), 0.0)
            return out

        def gt_layer(x, src, dst, ntype, etype, Wk, Wq, Wv, Wa, pri, Watt, Wmsg, skip, g, b):
            n = x.shape[0]
            k = typed_linear(x, ntype, Wk).reshape(n, H, HS)
            q = typed_linear(x, ntype, Wq).reshape(n, H, HS)
            v = typed_linear(x, ntype, Wv).reshape(n, H, HS)
            k_j, q_i, v_j = (k[src], q[dst], v[src])
            kw = rel_apply(k_j, etype, Watt)
            a = (kw * q_i).sum(-1) * pri[:, etype].T / SQRT_D
            amax = jax.ops.segment_max(a, dst, num_segments=n)
            ex = jnp.exp(a - amax[dst])
            den = jax.ops.segment_sum(ex, dst, num_segments=n)
            alpha = ex / (den[dst] + 1e-16)
            m = rel_apply(v_j, etype, Wmsg)
            agg = jax.ops.segment_sum(alpha[..., None] * m, dst, num_segments=n)
            out = jax.nn.silu(typed_linear(agg.reshape(n, HID), ntype, Wa))
            al = jax.nn.sigmoid(skip[ntype])[:, None]
            out = out * al + x * (1.0 - al)
            mu = out.mean(-1, keepdims=True)
            var = ((out - mu) ** 2).mean(-1, keepdims=True)
            return (out - mu) / jnp.sqrt(var + EPS) * g + b
        src, dst = (edge_index[0], edge_index[1])
        emb = x
        for l in range(L):
            emb = gt_layer(emb, src, dst, ntype, etype, Wk[l], Wq[l], Wv[l], Wa[l], pri[l], Watt[l], Wmsg[l], skip[l], ln_g[l], ln_b[l])
        return emb @ Wff + bff

    def _L1_gnn_ref(user_states, edge_src, edge_dst, W_self, b_self, W_neigh, b_neigh):
        import jax, jax.numpy as jnp
        import numpy as np
        N_NODES = 3125
        N_EDGES = 50000
        HIDDEN = 128
        n = user_states.shape[0]
        neigh_sum = jax.ops.segment_sum(user_states[edge_dst], edge_src, num_segments=n)
        counts = jax.ops.segment_sum(jnp.ones((edge_src.shape[0],), dtype=user_states.dtype), edge_src, num_segments=n)
        neigh_mean = neigh_sum / jnp.maximum(counts, 1.0)[:, None]
        neigh_msg = neigh_mean @ W_neigh.T + b_neigh
        neigh_msg = jnp.where(counts[:, None] > 0, neigh_msg, jnp.zeros_like(neigh_msg))
        self_msg = user_states @ W_self.T + b_self
        return jax.nn.relu(self_msg + neigh_msg)

    def _L2_gnn_ref(x, lin_w, lin_b, weight, w_ih, w_hh, b_ih, b_hh, edge_index):
        import jax, jax.numpy as jnp
        import numpy as np
        N = 3125
        E = 18750
        D_IN = 128
        D = 128
        L = 3

        def gru_cell(m, h, w_ih, w_hh, b_ih, b_hh):
            gi = m @ w_ih.T + b_ih
            gh = h @ w_hh.T + b_hh
            ir, iz, inn = jnp.split(gi, 3, axis=-1)
            hr, hz, hn = jnp.split(gh, 3, axis=-1)
            r = jax.nn.sigmoid(ir + hr)
            z = jax.nn.sigmoid(iz + hz)
            n = jnp.tanh(inn + r * hn)
            return (1.0 - z) * n + z * h
        h = x @ lin_w.T + lin_b
        src, dst = (edge_index[0], edge_index[1])
        n_nodes = h.shape[0]
        for i in range(weight.shape[0]):
            m = h @ weight[i]
            agg = jax.ops.segment_sum(m[src], dst, num_segments=n_nodes)
            h = gru_cell(agg, h, w_ih, w_hh, b_ih, b_hh)
        return h

    def _L3_gnn_ref(x, edge_index, W1, att_src1, att_dst1, b1, W2, att_src2, att_dst2, b2):
        import jax, jax.numpy as jnp
        import numpy as np
        NEG_SLOPE = 0.2
        N_NODES = 50000

        def gat_conv(x, src, dst, W, a_src, a_dst, b, n_nodes):
            H, C = a_src.shape
            h = (x @ W).reshape(-1, H, C)
            s_src = jnp.sum(h * a_src[None], axis=-1)
            s_dst = jnp.sum(h * a_dst[None], axis=-1)
            e = jax.nn.leaky_relu(s_src[src] + s_dst[dst], NEG_SLOPE)
            m = jax.ops.segment_max(e, dst, num_segments=n_nodes)
            w = jnp.exp(e - m[dst])
            denom = jax.ops.segment_sum(w, dst, num_segments=n_nodes)
            alpha = w / denom[dst]
            out = jax.ops.segment_sum(alpha[:, :, None] * h[src], dst, num_segments=n_nodes)
            return out
        N = x.shape[0]
        loops = jnp.arange(N, dtype=edge_index.dtype)
        src = jnp.concatenate([edge_index[0], loops])
        dst = jnp.concatenate([edge_index[1], loops])
        h1 = gat_conv(x, src, dst, W1, att_src1, att_dst1, b1, N)
        h1 = h1.reshape(N, -1) + b1
        h1 = jax.nn.elu(h1)
        h2 = gat_conv(h1, src, dst, W2, att_src2, att_dst2, b2, N)
        out = h2[:, 0, :] + b2
        return out
    edge_index = jnp.stack([src, dst])
    x = _layernorm(x + _L0_gnn_ref(x, edge_index, node_type_8, edge_type_8, L0_gnn_Wk, L0_gnn_Wq, L0_gnn_Wv, L0_gnn_Wa, L0_gnn_pri, L0_gnn_Watt, L0_gnn_Wmsg, L0_gnn_skip, L0_gnn_ln_g, L0_gnn_ln_b, L0_gnn_Wff, L0_gnn_bff), axis=-1)
    x = _layernorm(x + _L1_gnn_ref(x, src, dst, L1_gnn_W_self, L1_gnn_b_self, L1_gnn_W_neigh, L1_gnn_b_neigh), axis=-1)
    x = _layernorm(x + _L2_gnn_ref(x, L2_gnn_lin_w, L2_gnn_lin_b, L2_gnn_weight, L2_gnn_w_ih, L2_gnn_w_hh, L2_gnn_b_ih, L2_gnn_b_hh, edge_index), axis=-1)
    x = _layernorm(x + _L3_gnn_ref(x, edge_index, L3_gnn_W1, L3_gnn_att_src1, L3_gnn_att_dst1, L3_gnn_b1, L3_gnn_W2, L3_gnn_att_src2, L3_gnn_att_dst2, L3_gnn_b2), axis=-1)
    return x

_drawn_inputs = setup_inputs


def setup_inputs(seed=0):
    import zlib

    import numpy as np

    out = dict(_drawn_inputs(seed))
    spreads = {'L0_gnn_pri': (1.0, 0.2),
     'L0_gnn_skip': (1.0, 0.2),
     'L0_gnn_ln_g': (1.0, 0.2),
     'L0_gnn_ln_b': (0.0, 0.1),
     'L0_gnn_bff': (0.0, 0.1),
     'L2_gnn_lin_b': (0.0, 0.1),
     'L2_gnn_b_ih': (0.0, 0.1),
     'L2_gnn_b_hh': (0.0, 0.1),
     'L3_gnn_b1': (0.0, 0.1),
     'L3_gnn_b2': (0.0, 0.1)}
    factors = {'L3_gnn_att_dst2': 8.0}
    for name, (base, spread) in spreads.items():
        noise = np.random.default_rng([zlib.crc32(name.encode()), seed]).standard_normal(out[name].shape)
        drawn = base * np.exp(spread * noise) if base else spread * noise
        out[name] = jnp.asarray(drawn.astype(out[name].dtype))
    for name, factor in factors.items():
        out[name] = (out[name] * factor).astype(out[name].dtype)
    return out
```

```python
from contextlib import ExitStack, contextmanager

import numpy as np

import concourse.bass as bass
from concourse import mybir

F32 = mybir.dt.float32
F16 = mybir.dt.float16
BF16 = mybir.dt.bfloat16
I32 = mybir.dt.int32
ALU = mybir.AluOpType
ACT = mybir.ActivationFunctionType
AX = mybir.AxisListType
ds = bass.ds

P = 128
D = 128
BIG = 3.0e38
LN_EPS = 1e-05


class Chain:

    def __init__(self, eng, sem, done=0):
        self.eng, self.sem, self.done, self.offset = eng, sem, done, 0

    def link(self, ins):
        ins.then_inc(self.sem, 1)
        self.done += 1
        self.eng.wait_ge(self.sem, self.offset + self.done)

    def enter(self, i, steps):
        self.offset, self.first, self.steps = i * steps, self.done, steps

    def leave(self, rounds):
        assert self.done - self.first == self.steps, (self.done - self.first, self.steps)
        self.offset, self.done = 0, self.first + rounds * self.steps


def flat(ap):
    return ap.rearrange("p a b -> p (a b)")


def over_last(ap, n):
    return ap.unsqueeze(2).to_broadcast([ap.shape[0], ap.shape[1], n])


def over_mid(ap, n):
    return ap.unsqueeze(1).to_broadcast([ap.shape[0], n, ap.shape[1]])


FIRST_SEMAPHORE, LAST_SEMAPHORE = 110, 250
turn = []


@contextmanager
def signal(nc, name):
    num = turn.pop(0)
    handle = nc.alloc_semaphore(name=name, num=num)
    yield handle
    nc.gpsimd.sem_clear(handle)
    nc.release_semaphore(handle)
    turn.append(num)


def free(eng, *sems, by=1):
    for sem in sems:
        eng.sem_inc(sem, by)


class Shapes:

    def __init__(self, nodes, edges):
        self.N, self.E = nodes, edges
        self.NT = -(-nodes // P)
        self.NP = self.NT * P
        self.EP = max(p for p in range(1, P + 1) if edges % p == 0 and (edges // p) % 4 == 0)
        self.ET = edges // self.EP
        most = (edges + self.NT * (P - 1)) // P
        self.T = -(-most // 32) * 32
        assert self.NT == 25 and self.EP == 125 and self.T == 416


class Edges:

    def __init__(self, sb, nc, s, name, detailed):
        self.row = sb(f"{name}_row", [P, s.T], I32)
        self.local = sb(f"{name}_local", [P, s.T], F32)
        self.tile = sb(f"{name}_tile", [1, s.T], I32)
        if detailed:
            self.node = sb(f"{name}_node", [P, s.T], I32)
            self.last = sb(f"{name}_last", [P, s.T], F32)
            self.cut = sb(f"{name}_cut", [P, s.T], F32)
            self.gather = nc.dram_tensor(f"{name}_gather", [P, s.T * P], BF16, kind="Internal").ap()


def constants(nc, k):
    with nc.Block() as block:
        @block.gpsimd
        def _(pool):
            pool.iota(k.iota[:, :], [[1, P]], base=0, channel_multiplier=0,
                      allow_small_or_imprecise_dtypes=True).then_inc(k.s_iota, 1)
            pool.iota(k.iota16[:, :], [[1, k.s.T]], base=0, channel_multiplier=0,
                      allow_small_or_imprecise_dtypes=True).then_inc(k.s_iota, 1)
            pool.iota(k.iota_p[:, :], [[0, 1]], base=0, channel_multiplier=1,
                      allow_small_or_imprecise_dtypes=True).then_inc(k.s_iota, 1)
            pool.iota(k.ident[:, :], [[1, P]], base=0, channel_multiplier=-1,
                      allow_small_or_imprecise_dtypes=True).then_inc(k.s_iota, 1)

        @block.vector
        def _(dve):
            chain = Chain(dve, k.s_const)
            dve.wait_ge(k.s_iota, 4)
            chain.link(dve.tensor_scalar(k.upto[:, :], k.ident[:, :], 0.0, -1.0, ALU.is_le, ALU.mult))
            chain.link(dve.tensor_scalar(k.ident[:, :], k.ident[:, :], 0.0, None, ALU.is_equal))
            chain.link(dve.memset(k.ones16[:, :], 1.0))
            chain.link(dve.memset(k.zeros16[:, :], 0.0))
            chain.link(dve.memset(k.ones[:, :], 1.0))


def bucket_edges(nc, k, order, key_d, node_d, type_d, name, refine):
    s = k.s
    T, NT, EP, ET = s.T, s.NT, s.EP, s.ET
    CH = 500
    NCH = NT * ET // CH
    half = NCH // 4
    assert CH * NCH == NT * ET and NCH % 4 == 0
    with ExitStack() as ctx:
        def sb(n, shape, dt):
            return ctx.enter_context(nc.sbuf_tensor(f"{name}_{n}", shape, dt))

        def sem(n):
            return ctx.enter_context(signal(nc, f"{name}_{n}"))

        key = sb("key", [EP, ET], I32)
        node = sb("node_in", [EP, ET], I32)
        typ = sb("type_in", [EP, ET], I32)
        work = sb("work", [EP, ET], I32)
        low = sb("low", [EP, ET], I32)
        bucket = sb("bucket", [EP, ET], F16)
        U = sb("U", [EP, ET], F32)
        W = sb("W", [EP, ET], F32)
        pcol = sb("pcol", [EP, ET], F32)
        tcol = sb("tcol", [EP, ET], F32)
        posf = sb("posf", [EP, ET], F32)
        outer = ExitStack()
        with outer:
            def sbo(n, shape, dt):
                return outer.enter_context(nc.sbuf_tensor(f"{name}_{n}", shape, dt))
            onehot = sbo("onehot", [EP, NT, ET], F16)
            total = sbo("total", [EP, NT, ET], F32)
            before = sbo("before", [EP, NT, ET], F32)
            count = sbo("count", [EP, NT], F32)
            counti = sbo("counti", [EP, NT], I32)
            tiles = sbo("tiles", [EP, NT], F32)
            start = sbo("start", [EP, NT], F32)
            startc = sbo("startc", [EP, NT], F32)
            tbl = sbo("tbl", [1, T, NT], F16)
            start16 = sbo("start16", [1, NT], F16)
            tsum = sbo("tsum", [1, T], F32)
            s_in = sem("s_in")
            s_hot = sem("s_hot")
            s_mm = sem("s_mm")
            s_ev = sem("s_ev")
            s_dve = sem("s_dve")
            hot_f = onehot[:, :, :].rearrange("p b t -> p (b t)")
            tot_f = total[:, :, :].rearrange("p b t -> p (b t)")
            bef_f = before[:, :, :].rearrange("p b t -> p (b t)")
            with nc.Block() as block:
                @block.sync
                def _(sp):
                    sp.dma_start(key[:, :], key_d.rearrange("(p t) -> p t", p=EP)).then_inc(s_in, 16)
                    sp.dma_start(node[:, :], node_d.rearrange("(p t) -> p t", p=EP)).then_inc(s_in, 16)
                    if type_d is not None:
                        sp.dma_start(typ[:, :], type_d.rearrange("(p t) -> p t", p=EP)).then_inc(s_in, 16)

                @block.vector
                def _(dve):
                    c = Chain(dve, s_dve)
                    dve.wait_ge(s_in, 48 if type_d is not None else 32)
                    c.link(dve.tensor_scalar(work[:, :], key[:, :], 7, None, ALU.arith_shift_right))
                    c.link(dve.tensor_copy(bucket[:, :], work[:, :]))
                    dve.tensor_tensor(onehot[:, :, :], over_mid(bucket[:, :], NT),
                                      over_last(k.iota16[0:EP, 0:NT], ET), ALU.is_equal).then_inc(s_hot, 1)
                    if type_d is not None:
                        c.link(dve.tensor_scalar(work[:, :], node[:, :], 3, None, ALU.logical_shift_left))
                        c.link(dve.tensor_tensor(node[:, :], work[:, :], typ[:, :], ALU.bitwise_or))
                    c.link(dve.tensor_scalar(work[:, :], node[:, :], 4, None, ALU.arith_shift_right))
                    c.link(dve.tensor_scalar(U[:, :], work[:, :], 1.0, None, ALU.add))
                    c.link(dve.tensor_scalar(work[:, :], node[:, :], 15, 7, ALU.bitwise_and, ALU.logical_shift_left))
                    c.link(dve.tensor_scalar(low[:, :], key[:, :], 127, None, ALU.bitwise_and))
                    c.link(dve.tensor_tensor(W[:, :], work[:, :], low[:, :], ALU.add))
                    dve.wait_ge(s_ev, NCH * 2 + 1)
                    c.link(dve.tensor_reduce(count[:, :], total[:, :, :], AX.X, ALU.add))
                    c.link(dve.tensor_scalar(count[:, :], count[:, :], 127.0, None, ALU.add))
                    c.link(dve.tensor_copy(counti[:, :], count[:, :]))
                    c.link(dve.tensor_scalar(counti[:, :], counti[:, :], 7, None, ALU.arith_shift_right))
                    c.link(dve.tensor_copy(tiles[:, :], counti[:, :]))
                    c.link(dve.tensor_tensor_scan(start[:, :], tiles[:, :], tiles[:, :], 0.0, ALU.add, ALU.max))
                    c.link(dve.tensor_tensor(start[:, :], start[:, :], tiles[:, :], ALU.subtract))
                    c.link(dve.tensor_scalar(startc[:, :], start[:, :], float(P), None, ALU.mult))
                    c.link(dve.tensor_copy(start16[:, :], start[0:1, :]))
                    c.link(dve.tensor_tensor(tbl[:, :, :], over_mid(start16[:, :], T),
                                             over_last(k.iota16[0:1, :], NT), ALU.is_le))
                    c.link(dve.tensor_reduce(tsum[:, :], tbl[:, :, :], AX.X, ALU.add))
                    c.link(dve.tensor_scalar(order.tile[:, :], tsum[:, :], -1.0, None, ALU.add))
                    for b in range(NT):
                        last = dve.tensor_tensor_scan(total[:, b, :], total[:, b, :], total[:, b, :],
                                                      startc[:, b:b + 1], ALU.add, ALU.max)
                    c.link(last)
                    c.link(dve.tensor_tensor(bef_f, bef_f, tot_f, ALU.add))
                    c.link(dve.tensor_tensor(bef_f, bef_f, hot_f, ALU.mult))
                    c.link(dve.tensor_reduce(posf[:, :], before[:, :, :].rearrange("p b t -> p t b"), AX.X, ALU.add))
                    c.link(dve.tensor_copy(work[:, :], posf[:, :]))
                    c.link(dve.tensor_scalar(low[:, :], work[:, :], 127, None, ALU.bitwise_and))
                    c.link(dve.tensor_copy(pcol[:, :], low[:, :]))
                    c.link(dve.tensor_scalar(low[:, :], work[:, :], 7, None, ALU.arith_shift_right))
                    c.link(dve.tensor_copy(tcol[:, :], low[:, :]))

                @block.tensor
                def _(pe):
                    pe.wait_ge(s_hot, 1)
                    for half_at in range(2):
                        tri = k.ones16 if half_at == 0 else k.upto
                        with pe.Fori(0, half) as i:
                            for u in range(4):
                                bank = 4 * half_at + u
                                if u == 0:
                                    pe.wait_ge(s_ev, i * 4 + (half_at * NCH + 1))
                                pe.matmul(k.psum[0:EP, bank, 0:CH], tri[0:EP, 0:EP],
                                          hot_f[:, ds(i * (4 * CH) + u * CH, CH)],
                                          start=True, stop=True).then_inc(s_mm, 1)

                @block.scalar
                def _(act):
                    free(act, s_ev)
                    for half_at in range(2):
                        dst = tot_f if half_at == 0 else bef_f
                        with act.Fori(0, half) as i:
                            for u in range(4):
                                act.wait_ge(s_mm, i * 4 + (half_at * NCH + u + 1))
                                act.activation(dst[:, ds(i * (4 * CH) + u * CH, CH)],
                                               k.psum[0:EP, 4 * half_at + u, 0:CH], ACT.Copy).then_inc(s_ev, 1)

        oh_t = sb("oh_t", [EP, 4, T], F16)
        oh_p = sb("oh_p", [EP, 4, 2, P], F16)
        s_oh = sem("s_oh")
        s_used = sem("s_used")
        s_put = sem("s_put")
        s_d2 = sem("s_d2")
        ws = sb("ws", [P, T], I32)
        us = sb("us", [P, T], I32)
        val = sb("val", [P, T], F32)
        wl = sb("wl", [P, T], I32)
        with nc.Block() as block:
            @block.vector
            def _(dve):
                with dve.Fori(0, ET // 4) as i:
                    dve.wait_ge(s_used, i * 4 + 1)
                    for u in range(4):
                        t = ds(i * 4 + u, 1)
                        dve.tensor_scalar(oh_t[:, u, :], k.iota16[0:EP, :], tcol[:, t], None, ALU.is_equal)
                        dve.tensor_scalar(oh_p[:, u, 0, :], k.iota16[0:EP, 0:P], pcol[:, t], U[:, t],
                                          ALU.is_equal, ALU.mult)
                        dve.tensor_scalar(oh_p[:, u, 1, :], k.iota16[0:EP, 0:P], pcol[:, t], W[:, t],
                                          ALU.is_equal, ALU.mult).then_inc(s_oh, 1)
                c = Chain(dve, s_d2)
                dve.wait_ge(s_put, 1)
                if refine:
                    c.link(dve.tensor_copy(k.pair[:, :, 0], k.psum[:, 0, 0:T]))
                    c.link(dve.tensor_copy(k.pair[:, :, 1], k.psum[:, 1, 0:T]))
                else:
                    decode(c, dve, k, order, k.psum[:, 0, 0:T], k.psum[:, 1, 0:T], us, ws, wl, val, None)

            @block.tensor
            def _(pe):
                free(pe, s_used)
                for v in range(2):
                    pe.matmul(k.psum[:, v, 0:T], k.zeros16[0:EP, :], k.iota16[0:EP, :], start=True, stop=False)
                with pe.Fori(0, ET // 4) as i:
                    for u in range(4):
                        pe.wait_ge(s_oh, i * 4 + (u + 1))
                        pe.matmul(k.psum[:, 0, 0:T], oh_p[:, u, 0, :], oh_t[:, u, :], start=False, stop=False)
                        pe.matmul(k.psum[:, 1, 0:T], oh_p[:, u, 1, :], oh_t[:, u, :],
                                  start=False, stop=False).then_inc(s_used, 1)
                for v in range(2):
                    last = pe.matmul(k.psum[:, v, 0:T], k.zeros16[0:EP, :], k.iota16[0:EP, :], start=False, stop=True)
                last.then_inc(s_put, 1)


def decode(c, dve, k, order, u_in, w_in, us, ws, wl, val, node):
    c.link(dve.tensor_scalar(val[:, :], u_in, 0.0, None, ALU.is_gt))
    c.link(dve.tensor_copy(ws[:, :], w_in))
    c.link(dve.tensor_scalar(us[:, :], u_in, -1.0, 0.0, ALU.add, ALU.max))
    c.link(dve.tensor_scalar(wl[:, :], us[:, :], 4, None, ALU.logical_shift_left))
    c.link(dve.tensor_scalar(us[:, :], ws[:, :], 7, None, ALU.arith_shift_right))
    c.link(dve.tensor_tensor(order.row[:, :], wl[:, :], us[:, :], ALU.bitwise_or))
    c.link(dve.tensor_scalar(wl[:, :], ws[:, :], 127, None, ALU.bitwise_and))
    c.link(dve.tensor_copy(order.local[:, :], wl[:, :]))
    c.link(dve.scalar_tensor_tensor(order.local[:, :], order.local[:, :], 1.0, val[:, :], ALU.add, ALU.mult))
    c.link(dve.tensor_scalar(order.local[:, :], order.local[:, :], -1.0, None, ALU.add))
    if node is not None:
        c.link(dve.tensor_scalar(node[:, :], order.row[:, :], 3, None, ALU.arith_shift_right))


def sort_tiles(nc, k, order):
    s = k.s
    T = s.T
    B = -(-T // P)
    width = [min(P, T - b * P) for b in range(B)]
    G = 32
    R = T // G
    with ExitStack() as ctx:
        def sb(n, shape, dt):
            return ctx.enter_context(nc.sbuf_tensor(f"st_{n}", shape, dt))

        def sem(n):
            return ctx.enter_context(signal(nc, f"st_{n}"))

        key = sb("key", [P, T], F32)
        val = sb("val", [P, T], F32)
        a = sb("a", [P, T], I32)
        b_ = sb("b", [P, T], I32)
        w = sb("w", [P, T], I32)
        rows = sb("rows", [P, B, P], F32)
        bc = sb("bc", [P, 2, G, P], F32)
        less = sb("less", [P, G, P], F32)
        pos = sb("pos", [P, G], F32)
        hot = sb("hot", [P, G, P], F16)
        out = sb("out", [P, T, 2], F32)
        key_rows = nc.dram_tensor("st_key_rows", [T, P], F32, kind="Internal").ap()
        s_key = sem("s_key")
        s_tr = sem("s_tr")
        s_rows = sem("s_rows")
        s_st = sem("s_st")
        s_bc = [sem(f"s_bc{i}") for i in range(2)]
        s_cmp = sem("s_cmp")
        s_hot = sem("s_hot")
        s_mv = sem("s_mv")
        s_cp = sem("s_cp")
        s_d = sem("s_d")

        def key_row_store(sp, d, rows_ap):
            for b in range(B):
                sp.dma_start(d[b * P:b * P + width[b], :], rows_ap[0:width[b], b, 0:P]).then_inc(s_st, 16)

        with nc.Block() as block:
            @block.vector
            def _(dve):
                c = Chain(dve, s_d)
                U, W = k.pair[:, :, 0], k.pair[:, :, 1]
                c.link(dve.tensor_scalar(val[:, :], U, 0.0, 256.0, ALU.is_equal, ALU.mult))
                c.link(dve.tensor_copy(a[:, :], W))
                c.link(dve.tensor_scalar(a[:, :], a[:, :], 127, None, ALU.bitwise_and))
                c.link(dve.tensor_tensor(key[:, :], val[:, :], a[:, :], ALU.add))
                c.link(dve.tensor_scalar(key[:, :], key[:, :], float(P), k.iota_p[:, :], ALU.mult, ALU.add))
                dve.tensor_copy(val[:, :], key[:, :]).then_inc(s_key, 1)
                dve.wait_ge(s_tr, B)
                for b in range(B):
                    last = dve.tensor_copy(rows[0:width[b], b, :], k.psum[0:width[b], b, 0:P])
                last.then_inc(s_rows, 1)
                c.enter(0, 4)
                with dve.Fori(0, R) as i:
                    c.offset = i * 4
                    if True:
                        dve.wait_ge(s_bc[0], (i + 1) * 16)
                        g = ds(i * G, G)
                        c.link(dve.tensor_tensor(less[:, :, :], bc[:, 0, :, :], over_last(key[:, g], P), ALU.is_lt))
                        c.link(dve.tensor_reduce(pos[:, :], less[:, :, :], AX.X, ALU.add))
                        c.link(dve.tensor_tensor(hot[:, :, :], over_mid(k.iota[:, :], G),
                                                 over_last(pos[:, :], P), ALU.is_equal))
                        dve.sem_inc(s_hot, 1)
                        dve.wait_ge(s_mv, i + 2)
                        c.link(dve.tensor_scalar(out[:, g, :].rearrange("p a b -> p (a b)"), k.psum[:, 4, 0:2 * G], 0.0, None, ALU.add))
                c.leave(R)
                decode(c, dve, k, order, out[:, :, 0], out[:, :, 1], a, w, b_, val, order.node)

            @block.tensor
            def _(pe):
                free(pe, s_mv)
                pe.wait_ge(s_key, 1)
                for b in range(B):
                    pe.transpose(k.psum[0:width[b], b, 0:P], val[:, b * P:b * P + width[b]],
                                 k.ident[:, :]).then_inc(s_tr, 1)
                with pe.Fori(0, R) as i:
                    pe.wait_ge(s_hot, i + 1)
                    for u in range(G):
                        last = pe.matmul(k.psum[:, 4, 2 * u:2 * u + 2], hot[:, u, :],
                                         flat(k.pair[:, ds(i * G + u, 1), :]), start=True, stop=True)
                    last.then_inc(s_mv, 1)

            @block.sync
            def _(sp):
                sp.wait_ge(s_rows, 1)
                key_row_store(sp, key_rows, rows)
                sp.wait_ge(s_st, 16 * B)
                with sp.Fori(0, R) as i:
                    sp.wait_ge(s_mv, i + 1)
                    sp.dma_start(bc[:, 0, :, :].rearrange("p a b -> p (a b)"),
                                 key_rows[ds(i * G, G), :].rearrange("a b -> (a b)").unsqueeze(0)
                                 .to_broadcast([P, G * P])).then_inc(s_bc[0], 16)

        s_tr2 = sem("s_tr2")
        s_fl = sem("s_fl")
        s_back = sem("s_back")
        s_bc2 = sem("s_bc2")
        s_oh = sem("s_oh")
        s_w = sem("s_w")
        s_r2 = sem("s_r2")
        s_st2 = sem("s_st2")
        s_d2 = sem("s_d2")
        first = sb("first", [P, B, P], F32)
        lastf = sb("lastf", [P, B, P], F32)
        ohb = sb("ohb", [P, 2, G, P], BF16)
        local_rows = nc.dram_tensor("st_local_rows", [T, P], F32, kind="Internal").ap()
        with nc.Block() as block:
            @block.vector
            def _(dve):
                free(dve, s_oh)
                c = Chain(dve, s_d2)
                dve.wait_ge(s_tr2, B)
                for b in range(B):
                    last = dve.tensor_copy(rows[0:width[b], b, :], k.psum[0:width[b], b, 0:P])
                last.then_inc(s_r2, 1)
                dve.wait_ge(s_r2, 1)
                c.link(dve.memset(first[:, :, :], -BIG))
                c.link(dve.memset(lastf[:, :, :], 1.0))
                for b in range(B):
                    v = width[b]
                    c.link(dve.tensor_tensor(lastf[0:v, b, 0:P - 1], rows[0:v, b, 0:P - 1], rows[0:v, b, 1:P],
                                             ALU.not_equal))
                    c.link(dve.tensor_scalar(first[0:v, b, 1:P], lastf[0:v, b, 0:P - 1], -BIG, None, ALU.mult))
                dve.sem_inc(s_fl, 1)
                dve.wait_ge(s_back, 2 * B)
                for b in range(B):
                    v = width[b]
                    dve.tensor_copy(order.cut[:, b * P:b * P + v], k.psum[:, 4, b * P:b * P + v])
                    last = dve.tensor_copy(order.last[:, b * P:b * P + v], k.psum[:, 5, b * P:b * P + v])
                c.link(last)
                with dve.Fori(0, R) as i:
                    dve.wait_ge(s_bc2, (i + 1) * 16)
                    dve.wait_ge(s_w, i * 16 + 16)
                    dve.tensor_scalar(ohb[:, 0, :, :], bc[:, 0, :, :], k.iota_p[:, :], None,
                                      ALU.is_equal).then_inc(s_oh, 1)

            @block.tensor
            def _(pe):
                for b in range(B):
                    pe.transpose(k.psum[0:width[b], b, 0:P], order.local[:, b * P:b * P + width[b]],
                                 k.ident[:, :]).then_inc(s_tr2, 1)
                pe.wait_ge(s_fl, 1)
                for b in range(B):
                    v = width[b]
                    pe.transpose(k.psum[:, 4, b * P:b * P + v], first[0:v, b, :], k.ident[0:v, 0:v]).then_inc(s_back, 1)
                    pe.transpose(k.psum[:, 5, b * P:b * P + v], lastf[0:v, b, :], k.ident[0:v, 0:v]).then_inc(s_back, 1)

            @block.sync
            def _(sp):
                free(sp, s_w, by=16)
                sp.wait_ge(s_r2, 1)
                for b in range(B):
                    sp.dma_start(local_rows[b * P:b * P + width[b], :], rows[0:width[b], b, :]).then_inc(s_st2, 16)
                sp.wait_ge(s_st2, 16 * B)
                with sp.Fori(0, R) as i:
                    sp.wait_ge(s_oh, i + 1)
                    sp.dma_start(bc[:, 0, :, :].rearrange("p a b -> p (a b)"),
                                 local_rows[ds(i * G, G), :].rearrange("a b -> (a b)").unsqueeze(0)
                                 .to_broadcast([P, G * P])).then_inc(s_bc2, 16)
                    sp.wait_ge(s_oh, i + 2)
                    sp.dma_start(order.gather[:, ds(i * (G * P), G * P)],
                                 ohb[:, 0, :, :].rearrange("p a b -> p (a b)")).then_inc(s_w, 16)
                sp.wait_ge(s_w, R * 16 + 16)


class Kit:

    def __init__(self, nc, ctx, s):
        self.s = s

        def sb(n, shape, dt):
            return ctx.enter_context(nc.sbuf_tensor(n, shape, dt))

        self.sb = sb
        self.iota = sb("iota", [P, P], F32)
        self.iota16 = sb("iota16", [P, s.T], F16)
        self.iota_p = sb("iota_p", [P, 1], F32)
        self.ident = sb("ident", [P, P], F32)
        self.upto = sb("upto", [P, P], F16)
        self.ones16 = sb("ones16", [P, P], F16)
        self.zeros16 = sb("zeros16", [P, P], F16)
        self.ones = sb("ones", [P, P], F32)
        self.psum = ctx.enter_context(nc.psum_tensor("psum", [P, 8, 512], F32))
        self.s_got = [ctx.enter_context(nc.semaphore(f"s_got{q}")) for q in range(4)]
        self.got = 0
        self.s_iota = ctx.enter_context(nc.semaphore("s_iota"))
        self.s_const = ctx.enter_context(nc.semaphore("s_const"))


def banked(nc, k, name, chunks, produce, take):
    with ExitStack() as ctx:
        s_full = ctx.enter_context(signal(nc, f"{name}_full"))
        s_taken = [ctx.enter_context(signal(nc, f"{name}_taken{i}")) for i in range(2)]
        with nc.Block() as block:
            @block.tensor
            def _(pe):
                for c in range(chunks):
                    if c >= 8:
                        pe.wait_ge(s_taken[c % 2], (c - 8) // 2 + 1)
                    produce(pe, c, c % 8).then_inc(s_full, 1)

            @block.scalar
            def _(act):
                for c in range(0, chunks, 2):
                    act.wait_ge(s_full, c + 1)
                    take(lambda dst, src: act.activation(dst, src, ACT.Copy), c, c % 8).then_inc(s_taken[0], 1)

            @block.vector
            def _(dve):
                for c in range(1, chunks, 2):
                    dve.wait_ge(s_full, c + 1)
                    take(lambda dst, src: dve.tensor_copy(dst, src), c, c % 8).then_inc(s_taken[1], 1)


def chunked(n, size):
    return [(a, min(size, n - a)) for a in range(0, n, size)]


def transpose_all(nc, k, name, src, dst):
    parts = chunked(k.s.NT, 4)

    def produce(pe, c, bank):
        a, n = parts[c]
        for j in range(n):
            last = pe.transpose(k.psum[:, bank, j * P:(j + 1) * P], src[:, a + j, :], k.ident[:, :])
        return last

    def take(copy, c, bank):
        a, n = parts[c]
        return copy(dst[:, a * P:(a + n) * P], k.psum[:, bank, 0:n * P])

    banked(nc, k, name, len(parts), produce, take)


def untranspose_all(nc, k, name, src, dst):
    parts = chunked(k.s.NT, 4)

    def produce(pe, c, bank):
        a, n = parts[c]
        for j in range(n):
            last = pe.transpose(k.psum[:, bank, j * P:(j + 1) * P], src[:, (a + j) * P:(a + j + 1) * P],
                                k.ident[:, :])
        return last

    def take(copy, c, bank):
        a, n = parts[c]
        return copy(flat(dst[:, a:a + n, :]), k.psum[:, bank, 0:n * P])

    banked(nc, k, name, len(parts), produce, take)


def linear(nc, k, name, xs, ws, width, dst):
    per = 512 // width
    parts = chunked(k.s.NT, per)

    def produce(pe, c, bank):
        a, n = parts[c]
        for j in range(n):
            for q, (x, w) in enumerate(zip(xs, ws)):
                last = pe.matmul(k.psum[:, bank, j * width:(j + 1) * width], x[:, (a + j) * P:(a + j + 1) * P],
                                 w, start=q == 0, stop=q == len(xs) - 1)
        return last

    def take(copy, c, bank):
        a, n = parts[c]
        return copy(dst(a, n), k.psum[:, bank, 0:n * width].rearrange("p (a b) -> p a b", b=width))

    banked(nc, k, name, len(parts), produce, take)


def typed_linear(nc, k, name, x_t, w_d, out, silu=False):
    s = k.s
    types = w_d.shape[0]
    parts = chunked(s.NP, 512)
    with ExitStack() as ctx:
        w = ctx.enter_context(nc.sbuf_tensor(f"{name}_w", [P, types, D], F32))
        xm = ctx.enter_context(nc.sbuf_tensor(f"{name}_xm", [P, 2, s.NP], F32))
        s_w = ctx.enter_context(signal(nc, f"{name}_s_w"))
        s_xm = ctx.enter_context(signal(nc, f"{name}_s_xm"))
        s_mm = ctx.enter_context(signal(nc, f"{name}_s_mm"))
        s_sig = ctx.enter_context(signal(nc, f"{name}_s_sig"))
        acc = k.psum[:, :, :].rearrange("p a b -> p (a b)")[:, 0:s.NP]
        with nc.Block() as block:
            @block.sync
            def _(sp):
                sp.dma_start(w[:, :, :], w_d.rearrange("t i o -> i t o")).then_inc(s_w, 16)

            @block.vector
            def _(dve):
                for t in range(types):
                    if t >= 2:
                        dve.wait_ge(s_mm, t - 1)
                    dve.scalar_tensor_tensor(xm[:, t % 2, :], k.type_row[:, :], float(t), x_t[:, :],
                                             ALU.is_equal, ALU.mult).then_inc(s_xm, 1)
                if silu:
                    dve.wait_ge(s_sig, 1)
                    dve.tensor_tensor(out[:, :], xm[:, 0, :], acc, ALU.mult)

            @block.tensor
            def _(pe):
                pe.wait_ge(s_w, 16)
                for t in range(types):
                    pe.wait_ge(s_xm, t + 1)
                    for c, (a, n) in enumerate(parts):
                        last = pe.matmul(k.psum[:, c, 0:n], w[:, t, :], xm[:, t % 2, a:a + n],
                                         start=t == 0, stop=t == types - 1)
                    last.then_inc(s_mm, 1)

            @block.scalar
            def _(act):
                act.wait_ge(s_mm, types)
                if silu:
                    act.activation(xm[:, 0, :], acc, ACT.Sigmoid).then_inc(s_sig, 1)
                else:
                    act.activation(out[:, :], acc, ACT.Copy)


def layer_norm(nc, k, name, x, gain=None, shift=None):
    s = k.s
    NT = s.NT
    with ExitStack() as ctx:
        sq = ctx.enter_context(nc.sbuf_tensor(f"{name}_sq", [P, NT, D], F32))
        m = ctx.enter_context(nc.sbuf_tensor(f"{name}_m", [P, NT], F32))
        v = ctx.enter_context(nc.sbuf_tensor(f"{name}_v", [P, NT], F32))
        r = ctx.enter_context(nc.sbuf_tensor(f"{name}_r", [P, NT], F32))
        s_d = ctx.enter_context(signal(nc, f"{name}_s_d"))
        s_x = ctx.enter_context(signal(nc, f"{name}_s_x"))
        s_a = ctx.enter_context(signal(nc, f"{name}_s_a"))
        with nc.Block() as block:
            @block.vector
            def _(dve):
                c = Chain(dve, s_d)
                c.link(dve.tensor_reduce(m[:, :], x[:, :, :], AX.X, ALU.add))
                c.link(dve.tensor_scalar(m[:, :], m[:, :], 1.0 / D, None, ALU.mult))
                dve.tensor_tensor(x[:, :, :], x[:, :, :], over_last(m[:, :], D), ALU.subtract).then_inc(s_x, 1)
                dve.wait_ge(s_a, 1)
                c.link(dve.tensor_reduce(v[:, :], sq[:, :, :], AX.X, ALU.add))
                dve.tensor_scalar(v[:, :], v[:, :], 1.0 / D, LN_EPS, ALU.mult, ALU.add).then_inc(s_x, 1)
                dve.wait_ge(s_a, 2)
                c.link(dve.reciprocal(r[:, :], r[:, :]))
                c.link(dve.tensor_tensor(x[:, :, :], x[:, :, :], over_last(r[:, :], D), ALU.mult))
                if gain is not None:
                    c.link(dve.tensor_tensor(x[:, :, :], x[:, :, :], over_mid(gain, NT), ALU.mult))
                    c.link(dve.tensor_tensor(x[:, :, :], x[:, :, :], over_mid(shift, NT), ALU.add))

            @block.scalar
            def _(act):
                act.wait_ge(s_x, 1)
                act.activation(sq[:, :, :], x[:, :, :], ACT.Square).then_inc(s_a, 1)
                act.wait_ge(s_x, 2)
                act.activation(r[:, :], v[:, :], ACT.Sqrt).then_inc(s_a, 1)


GRP = 4
RND = 4


def tile_registers(eng, k, order, t0, n, name):
    regs = [eng.alloc_register(f"{name}{u}") for u in range(n)]
    return regs


def load_tiles(eng, k, order, regs, t0):
    eng.load(regs, order.tile[0:1, ds(t0, len(regs))])
    return [eng.snap(r, min_val=0, max_val=k.s.NT - 1) for r in regs]


def gather_rows(nc, k, name, order, rows, table, width, score, stash, heads, queries, scores):
    s = k.s
    rounds = s.T // (GRP * RND)
    qw = D if score == "dot" else heads
    lo, hi = stash
    with ExitStack() as ctx:
        def sb(n, shape, dt):
            return ctx.enter_context(nc.sbuf_tensor(f"{name}_{n}", shape, dt))

        def sems(n):
            return [ctx.enter_context(signal(nc, f"{name}_{n}{q}")) for q in range(RND)]

        got = sb("got", [P, RND, GRP, width], F32)
        idx = sb("idx", [P, RND, GRP], I32)
        hot = sb("hot", [P, RND, GRP * P], BF16)
        prod = sb("prod", [P, 2, GRP * qw], F32)
        s_idx, s_hot, s_q, s_used, s_stash = (sems(n) for n in ("s_idx", "s_hot", "s_q", "s_used", "s_stash"))
        s_got, had = k.s_got, k.got
        k.got += rounds * 16 * GRP
        s_d = ctx.enter_context(signal(nc, f"{name}_s_d"))
        with nc.Block() as block:
            @block.scalar
            def _(act):
                with act.Fori(0, rounds) as i:
                    for q in range(RND):
                        act.wait_ge(s_used[q], i + 1)
                        act.activation(idx[:, q, :], rows[:, ds((i * RND + q) * GRP, GRP)],
                                       ACT.Copy).then_inc(s_idx[q], 1)

            @block.gpsimd
            def _(pool):
                with pool.Fori(0, rounds) as i:
                    for q in range(RND):
                        pool.wait_ge(s_idx[q], i + 1)
                        pool.wait_ge(s_used[q], i + 1)
                        pool.wait_ge(s_stash[q], i * 16 + 16)
                        pool.nop(nofuse=True)
                        for u in range(GRP):
                            pool.indirect_dma_start(
                                got[:, q, u, :], None, table[:, :],
                                bass.IndirectOffsetOnAxis(ap=idx[:, q, u:u + 1], axis=0)).then_inc(s_got[q], 16)

            @block.sync
            def _(sp):
                free(sp, *s_stash, by=16)
                with sp.Fori(0, rounds) as i:
                    for q in range(RND):
                        sp.wait_ge(s_q[q], i + 1)
                        sp.dma_start(hot[:, q, :], order.gather[:, ds((i * RND + q) * (GRP * P), GRP * P)])\
                            .then_inc(s_hot[q], 16)
                    for q in range(RND):
                        sp.wait_ge(s_got[q], i * (16 * GRP) + (had + 16 * GRP))
                        sp.dma_start(k.stash[:, ds((i * RND + q) * GRP, GRP), 0:hi - lo], got[:, q, :, lo:hi])\
                            .then_inc(s_stash[q], 16)
                for q in range(RND):
                    sp.wait_ge(s_stash[q], rounds * 16 + 16)

            @block.tensor
            def _(pe):
                free(pe, *s_q)
                regs = tile_registers(pe, k, order, 0, GRP, f"{name}_pe")
                with pe.Fori(0, rounds) as i:
                    for q in range(RND):
                        node_tile = load_tiles(pe, k, order, regs, (i * RND + q) * GRP)
                        pe.wait_ge(s_hot[q], (i + 1) * 16)
                        pe.wait_ge(s_used[q], i + 1)
                        for u in range(GRP):
                            for part in range(3):
                                last = pe.matmul(k.psum[:, q, u * qw:(u + 1) * qw], hot[:, q, u * P:(u + 1) * P],
                                                 queries[:, part, ds(node_tile[u] * qw, qw)],
                                                 start=part == 0, stop=part == 2)
                        last.then_inc(s_q[q], 1)

            @block.vector
            def _(dve):
                free(dve, *s_used)
                c = Chain(dve, s_d)
                with dve.Fori(0, rounds) as i:
                    c.enter(i, RND if score == "dot" else 2 * RND)
                    for q in range(RND):
                        dve.wait_ge(s_got[q], i * (16 * GRP) + (had + 16 * GRP))
                        dve.wait_ge(s_q[q], i + 2)
                        at = scores[:, ds((i * RND + q) * (GRP * heads), GRP * heads)]
                        ps = k.psum[:, q, 0:GRP * qw]
                        pr = prod[:, q % 2, :]
                        if score == "dot":
                            dve.tensor_tensor(pr.rearrange("p (a b) -> p a b", a=GRP), got[:, q, :, 0:D],
                                              ps.rearrange("p (a b) -> p a b", a=GRP), ALU.mult).then_inc(s_used[q], 1)
                            dve.wait_ge(s_used[q], i + 2)
                            c.link(dve.tensor_reduce(at, pr.rearrange("p (a b) -> p a b", b=D // heads), AX.X, ALU.add))
                        else:
                            dve.tensor_tensor(pr.rearrange("p (a b) -> p a b", a=GRP), got[:, q, :, width - heads:width],
                                              ps.rearrange("p (a b) -> p a b", a=GRP), ALU.add).then_inc(s_used[q], 1)
                            dve.wait_ge(s_used[q], i + 2)
                            c.link(dve.tensor_scalar(at, pr, NEG_SLOPE, None, ALU.mult))
                            c.link(dve.tensor_tensor(at, at, pr, ALU.max))
                c.leave(rounds)


def segment_max(nc, k, name, order, heads, scores, peaks):
    s = k.s
    NT = s.NT
    TG = 16
    rounds = s.T // TG
    rows = TG * heads
    LANES = 4
    with ExitStack() as ctx:
        def sb(n, shape, dt):
            return ctx.enter_context(nc.sbuf_tensor(f"{name}_{n}", shape, dt))

        def sem(n):
            return ctx.enter_context(signal(nc, f"{name}_{n}"))

        hot = sb("hot", [P, TG, P], F32)
        cut = sb("cut", [P, rows], F32)
        stat = sb("stat", [P, rows], F32)
        cut_t = sb("cut_t", [rows, P], F32)
        run = sb("run", [rows, P], F32)
        tail = sb("tail", [P, TG, heads + 1], F32)
        gone = sb("gone", [P, TG], F32)
        best = sb("best", [P, TG, heads], F32)
        lane = sb("lane", [P, LANES, NT * heads], F32)
        s_d, s_tr, s_cut, s_run, s_back, s_tail, s_mv, s_pre, s_best = (sem(n) for n in (
            "s_d", "s_tr", "s_cut", "s_run", "s_back", "s_tail", "s_mv", "s_pre", "s_best"))
        W1 = heads + 1
        with nc.Block() as block:
            @block.vector
            def _(dve):
                free(dve, s_best)
                c = Chain(dve, s_d)
                for v in range(LANES):
                    c.link(dve.tensor_copy(lane[:, v, :], flat(peaks[:, :, :])))
                regs = tile_registers(dve, k, order, 0, TG, f"{name}_dve")
                with dve.Fori(0, rounds) as i:
                    c.enter(i, 7)
                    node_tile = load_tiles(dve, k, order, regs, i * TG)
                    g = ds(i * TG, TG)
                    c.link(dve.tensor_scalar(cut[:, :].rearrange("p (a b) -> p a b", b=heads),
                                             over_last(order.cut[:, g], heads), 1.0, None, ALU.mult))
                    c.link(dve.tensor_scalar(stat[:, :], scores[:, ds(i * rows, rows)], 1.0, None, ALU.mult))
                    dve.sem_inc(s_pre, 1)
                    c.link(dve.tensor_tensor(hot[:, :, :], over_mid(k.iota[:, :], TG), over_last(order.local[:, g], P),
                                             ALU.is_equal))
                    dve.wait_ge(s_tr, i + 1)
                    dve.wait_ge(s_cut, i + 1)
                    dve.tensor_tensor_scan(run[:, :], cut_t[:, :], k.psum[0:rows, 1, 0:P], -BIG,
                                           ALU.add, ALU.max).then_inc(s_run, 1)
                    dve.wait_ge(s_back, i + 1)
                    c.link(dve.tensor_tensor(tail[:, :, 0:heads], k.psum[:, 2, 0:rows].rearrange("p (a b) -> p a b", b=heads),
                                             over_last(order.last[:, g], heads), ALU.mult))
                    c.link(dve.tensor_scalar(tail[:, :, heads:W1], order.last[:, g].unsqueeze(2), 1.0, None, ALU.mult))
                    dve.sem_inc(s_tail, 1)
                    dve.wait_ge(s_mv, i + 1)
                    moved = k.psum[:, 3, 0:TG * W1].rearrange("p (a b) -> p a b", b=W1)
                    c.link(dve.tensor_scalar(gone[:, :].unsqueeze(2), moved[:, :, heads:W1], -1.0, BIG, ALU.add, ALU.mult))
                    c.link(dve.tensor_tensor(best[:, :, :], moved[:, :, 0:heads], over_last(gone[:, :], heads), ALU.add))
                    for u in range(TG):
                        at = lane[:, u % LANES, ds(node_tile[u] * heads, heads)]
                        if u >= LANES:
                            dve.wait_ge(s_best, i * TG + (u - LANES + 2))
                        else:
                            dve.wait_ge(s_best, i * TG + 1)
                        dve.tensor_tensor(at, at, best[:, u, :], ALU.max).then_inc(s_best, 1)
                    dve.wait_ge(s_best, i * TG + (TG + 1))
                c.leave(rounds)
                c.link(dve.tensor_tensor(lane[:, 0:2, :], lane[:, 0:2, :], lane[:, 2:4, :], ALU.max))
                c.link(dve.tensor_tensor(flat(peaks[:, :, :]), lane[:, 0, :], lane[:, 1, :], ALU.max))

            @block.tensor
            def _(pe):
                with pe.Fori(0, rounds) as i:
                    pe.wait_ge(s_pre, i + 1)
                    pe.nop(nofuse=True)
                    pe.transpose(k.psum[0:rows, 0, 0:P], cut[:, :], k.ident[:, :])
                    pe.transpose(k.psum[0:rows, 1, 0:P], stat[:, :], k.ident[:, :]).then_inc(s_tr, 1)
                    pe.wait_ge(s_run, i + 1)
                    pe.nop(nofuse=True)
                    pe.transpose(k.psum[:, 2, 0:rows], run[:, :], k.ident[0:rows, 0:rows]).then_inc(s_back, 1)
                    pe.wait_ge(s_tail, i + 1)
                    for u in range(TG):
                        last = pe.matmul(k.psum[:, 3, u * W1:(u + 1) * W1], hot[:, u, :], tail[:, u, :],
                                         start=True, stop=True)
                    last.then_inc(s_mv, 1)

            @block.scalar
            def _(act):
                with act.Fori(0, rounds) as i:
                    act.wait_ge(s_tr, i + 1)
                    act.activation(cut_t[:, :], k.psum[0:rows, 0, 0:P], ACT.Copy).then_inc(s_cut, 1)


def weigh_rows(nc, k, name, order, heads, features, scores, peaks3, acc):
    s = k.s
    rounds = s.T // (GRP * RND)
    F, FW = features, features + heads
    with ExitStack() as ctx:
        def sb(n, shape, dt):
            return ctx.enter_context(nc.sbuf_tensor(f"{name}_{n}", shape, dt))

        def sems(n, m=RND):
            return [ctx.enter_context(signal(nc, f"{name}_{n}{q}")) for q in range(m)]

        hot_t = sb("hot_t", [P, RND, GRP * P], BF16)
        msg = sb("msg", [P, RND, GRP, F], F32)
        hot = sb("hot", [P, RND, GRP, P], F32)
        diff = sb("diff", [P, RND, GRP * heads], F32)
        wtd = sb("wtd", [P, RND, GRP, FW], F32)
        s_in, s_msg, s_pk, s_diff, s_exp, s_wtd, s_sc, s_hot = (sems(n) for n in (
            "s_in", "s_msg", "s_pk", "s_diff", "s_exp", "s_wtd", "s_sc", "s_hot"))
        s_acc = sems("s_acc", GRP)
        with nc.Block() as block:
            @block.sync
            def _(sp):
                with sp.Fori(0, rounds) as i:
                    for q in range(RND):
                        g0 = (i * RND + q) * GRP
                        sp.wait_ge(s_pk[q], i + 1)
                        sp.dma_start(hot_t[:, q, :], order.gather[:, ds(g0 * P, GRP * P)]).then_inc(s_in[q], 16)
                        sp.wait_ge(s_wtd[q], i + 1)
                        sp.dma_start(msg[:, q, :, :], k.stash[:, ds(g0, GRP), 0:F]).then_inc(s_msg[q], 16)

            @block.tensor
            def _(pe):
                free(pe, *s_pk, s_sc[GRP - 1])
                regs = tile_registers(pe, k, order, 0, GRP, f"{name}_pe")

                def peak(i, q):
                    node_tile = load_tiles(pe, k, order, regs, (i * RND + q) * GRP)
                    pe.wait_ge(s_in[q], (i + 1) * 16)
                    pe.wait_ge(s_diff[q], i + 1)
                    for u in range(GRP):
                        for part in range(3):
                            last = pe.matmul(k.psum[:, q, u * heads:(u + 1) * heads], hot_t[:, q, u * P:(u + 1) * P],
                                             peaks3[:, part, ds(node_tile[u] * heads, heads)],
                                             start=part == 0, stop=part == 2)
                    last.then_inc(s_pk[q], 1)

                def scatter(i, q):
                    pe.wait_ge(s_wtd[q], i + 2)
                    pe.wait_ge(s_hot[q], i + 1)
                    for u in range(GRP):
                        pe.wait_ge(s_acc[u], i * RND + (q + 1))
                        last = pe.matmul(k.psum[:, 4 + u, 0:FW], hot[:, q, u, :], wtd[:, q, u, :], start=True, stop=True)
                        last.then_inc(s_sc[u], 1)

                with pe.Fori(0, rounds) as i:
                    peak(i, 0)
                    for q in range(1, RND):
                        peak(i, q)
                        scatter(i, q - 1)
                    scatter(i, RND - 1)

            @block.scalar
            def _(act):
                free(act, *s_exp)
                with act.Fori(0, rounds) as i:
                    for q in range(RND):
                        act.wait_ge(s_diff[q], i + 2)
                        act.wait_ge(s_sc[GRP - 1], i * RND + 1)
                        act.activation(wtd[:, q, :, F:FW], diff[:, q, :].rearrange("p (a b) -> p a b", a=GRP),
                                       ACT.Exp).then_inc(s_exp[q], 1)

            @block.vector
            def _(dve):
                free(dve, *s_diff, *s_wtd, *s_acc)
                regs = tile_registers(dve, k, order, 0, GRP, f"{name}_dve")

                def subtract(i, q):
                    g0 = (i * RND + q) * GRP
                    dve.wait_ge(s_sc[GRP - 1], i * RND + 1)
                    dve.tensor_tensor(hot[:, q, :, :], over_mid(k.iota[:, :], GRP),
                                      over_last(order.local[:, ds(g0, GRP)], P), ALU.is_equal).then_inc(s_hot[q], 1)
                    dve.wait_ge(s_pk[q], i + 2)
                    dve.wait_ge(s_exp[q], i + 1)
                    dve.tensor_tensor(diff[:, q, :], scores[:, ds(g0 * heads, GRP * heads)],
                                      k.psum[:, q, 0:GRP * heads], ALU.subtract).then_inc(s_diff[q], 1)

                def weigh(i, q):
                    dve.wait_ge(s_exp[q], i + 2)
                    dve.wait_ge(s_msg[q], (i + 1) * 16)
                    dve.tensor_tensor(
                        wtd[:, q, :, 0:F].rearrange("p g (a b) -> p g a b", a=heads),
                        msg[:, q, :, :].rearrange("p g (a b) -> p g a b", a=heads),
                        wtd[:, q, :, F:FW].unsqueeze(3).to_broadcast([P, GRP, heads, F // heads]),
                        ALU.mult).then_inc(s_wtd[q], 1)

                def add(i, q):
                    node_tile = load_tiles(dve, k, order, regs, (i * RND + q) * GRP)
                    for u in range(GRP):
                        at = acc[:, u % 2, ds(node_tile[u] * FW, FW)]
                        dve.wait_ge(s_sc[u], i * RND + (q + (2 if u == GRP - 1 else 1)))
                        dve.wait_ge(s_acc[(u - 2) % GRP], i * RND + (q + 1 if u < 2 else q + 2))
                        dve.tensor_tensor(at, at, k.psum[:, 4 + u, 0:FW], ALU.add).then_inc(s_acc[u], 1)

                with dve.Fori(0, rounds) as i:
                    subtract(i, 0)
                    subtract(i, 1)
                    weigh(i, 0)
                    for q in range(2, RND):
                        subtract(i, q)
                        weigh(i, q - 1)
                        add(i, q - 2)
                    weigh(i, RND - 1)
                    add(i, RND - 2)
                    add(i, RND - 1)


def gather_sum(nc, k, name, order, rows, table, width, acc):
    s = k.s
    rounds = s.T // (GRP * RND)
    with ExitStack() as ctx:
        def sb(n, shape, dt):
            return ctx.enter_context(nc.sbuf_tensor(f"{name}_{n}", shape, dt))

        def sems(n, m=RND):
            return [ctx.enter_context(signal(nc, f"{name}_{n}{q}")) for q in range(m)]

        got = sb("got", [P, RND, GRP, width], F32)
        idx = sb("idx", [P, RND, GRP], I32)
        hot = sb("hot", [P, RND, GRP, P], F32)
        s_idx, s_hot, s_used = (sems(n) for n in ("s_idx", "s_hot", "s_used"))
        s_got, had = k.s_got, k.got
        k.got += rounds * 16 * GRP
        s_acc = sems("s_acc", GRP)
        with nc.Block() as block:
            @block.scalar
            def _(act):
                with act.Fori(0, rounds) as i:
                    for q in range(RND):
                        act.wait_ge(s_used[q], i + 1)
                        act.activation(idx[:, q, :], rows[:, ds((i * RND + q) * GRP, GRP)],
                                       ACT.Copy).then_inc(s_idx[q], 1)

            @block.gpsimd
            def _(pool):
                with pool.Fori(0, rounds) as i:
                    for q in range(RND):
                        pool.wait_ge(s_idx[q], i + 1)
                        pool.wait_ge(s_used[q], i + 1)
                        pool.nop(nofuse=True)
                        for u in range(GRP):
                            pool.indirect_dma_start(
                                got[:, q, u, :], None, table[:, :],
                                bass.IndirectOffsetOnAxis(ap=idx[:, q, u:u + 1], axis=0)).then_inc(s_got[q], 16)

            @block.tensor
            def _(pe):
                free(pe, *s_used)
                with pe.Fori(0, rounds) as i:
                    for q in range(RND):
                        pe.wait_ge(s_got[q], i * (16 * GRP) + (had + 16 * GRP))
                        pe.wait_ge(s_hot[q], i + 1)
                        for u in range(GRP):
                            pe.wait_ge(s_acc[u], i * RND + (q + 1))
                            last = pe.matmul(k.psum[:, u, 0:width], hot[:, q, u, :], got[:, q, u, :],
                                             start=True, stop=True)
                        last.then_inc(s_used[q], 1)

            @block.vector
            def _(dve):
                free(dve, *s_acc)
                regs = tile_registers(dve, k, order, 0, GRP, f"{name}_dve")
                with dve.Fori(0, rounds) as i:
                    for q in range(RND):
                        g0 = (i * RND + q) * GRP
                        dve.wait_ge(s_used[q], i + 1)
                        dve.tensor_tensor(hot[:, q, :, :], over_mid(k.iota[:, :], GRP),
                                          over_last(order.local[:, ds(g0, GRP)], P), ALU.is_equal).then_inc(s_hot[q], 1)
                    for q in range(RND):
                        g0 = (i * RND + q) * GRP
                        node_tile = load_tiles(dve, k, order, regs, g0)
                        for u in range(GRP):
                            at = acc[:, u % 2, ds(node_tile[u] * width, width)]
                            dve.wait_ge(s_used[q], i + 2)
                            dve.wait_ge(s_acc[(u - 2) % GRP], i * RND + (q + 1 if u < 2 else q + 2))
                            dve.tensor_tensor(at, at, k.psum[:, u, 0:width], ALU.add).then_inc(s_acc[u], 1)


NEG_SLOPE = 0.2


def load_rows(nc, k, name, pairs):
    with ExitStack() as ctx:
        s_in = ctx.enter_context(signal(nc, f"{name}_s_in"))
        with nc.Block() as block:
            @block.sync
            def _(sp):
                for dst, src in pairs:
                    sp.dma_start(dst, src).then_inc(s_in, 16)
                sp.wait_ge(s_in, 16 * len(pairs))


def row_bcast(vec):
    return vec.unsqueeze(0).to_broadcast([P, vec.shape[0]])


def steps(nc, name, body):
    with ExitStack() as ctx:
        s_d = ctx.enter_context(signal(nc, f"{name}_s_d"))
        with nc.Block() as block:
            @block.vector
            def _(dve):
                body(Chain(dve, s_d).link, dve)


def relation_weights(nc, k, name, w_d, pri_d, out, pri):
    heads, rels, hs = w_d.shape[0], w_d.shape[1], w_d.shape[2]
    with ExitStack() as ctx:
        s_z = ctx.enter_context(signal(nc, f"{name}_s_z"))
        s_in = ctx.enter_context(signal(nc, f"{name}_s_in"))
        s_d = ctx.enter_context(signal(nc, f"{name}_s_d"))
        n_in = 16 * heads * (2 if pri is not None else 1)
        with nc.Block() as block:
            @block.vector
            def _(dve):
                dve.memset(out[:, :, :], 0.0).then_inc(s_z, 1)
                if pri is not None:
                    c = Chain(dve, s_d)
                    dve.wait_ge(s_in, n_in)
                    c.link(dve.tensor_scalar(pri[:, :], pri[:, :], 1.0 / float(np.sqrt(hs)), None, ALU.mult))
                    c.link(dve.tensor_tensor(out[:, :, :], out[:, :, :], over_last(pri[:, :], D), ALU.mult))

            @block.sync
            def _(sp):
                sp.wait_ge(s_z, 1)
                for h in range(heads):
                    at = slice(h * hs, (h + 1) * hs)
                    sp.dma_start(out[at, :, at], w_d[h].rearrange("r i o -> i r o")).then_inc(s_in, 16)
                    if pri is not None:
                        sp.dma_start(pri[at, :], pri_d[h].unsqueeze(0).to_broadcast([hs, rels])).then_inc(s_in, 16)
                sp.wait_ge(s_in, n_in)


def relation_table(nc, k, name, k_t, v_t, wk, wv, table):
    s = k.s
    rels = wk.shape[1]
    half = rels // 2
    rows = table.rearrange("(n r) c -> n r c", r=rels)
    with ExitStack() as ctx:
        out = ctx.enter_context(nc.sbuf_tensor(f"{name}_out", [P, 2, rels, 2 * D], F32))
        s_mm = ctx.enter_context(signal(nc, f"{name}_s_mm"))
        s_a = ctx.enter_context(signal(nc, f"{name}_s_a"))
        s_v = ctx.enter_context(signal(nc, f"{name}_s_v"))
        s_st = [ctx.enter_context(signal(nc, f"{name}_s_st{i}")) for i in range(2)]
        with nc.Block() as block:
            @block.tensor
            def _(pe):
                for j in range(s.NT):
                    if j >= 2:
                        pe.wait_ge(s_a, j - 1)
                        pe.wait_ge(s_v, j - 1)
                    for b in range(4):
                        x, w = ((k_t, wk), (v_t, wv))[b // 2]
                        last = pe.matmul(k.psum[:, 4 * (j % 2) + b, :], x[:, j * P:(j + 1) * P],
                                         flat(w[:, (b % 2) * half:(b % 2 + 1) * half, :]), start=True, stop=True)
                    last.then_inc(s_mm, 1)

            def empty(eng, j, side, copy):
                eng.wait_ge(s_mm, j + 1)
                if j >= 2:
                    eng.wait_ge(s_st[j % 2], 16 * (j // 2))
                b0 = 4 * (j % 2) + 2 * side
                return copy(out[:, j % 2, :, side * D:(side + 1) * D],
                            k.psum[:, b0:b0 + 2, :].rearrange("p a (r c) -> p (a r) c", c=D))

            @block.scalar
            def _(act):
                for j in range(s.NT):
                    empty(act, j, 0, lambda d, x: act.activation(d, x, ACT.Copy)).then_inc(s_a, 1)

            @block.vector
            def _(dve):
                for j in range(s.NT):
                    empty(dve, j, 1, lambda d, x: dve.tensor_copy(d, x)).then_inc(s_v, 1)

            @block.sync
            def _(sp):
                for j in range(s.NT):
                    sp.wait_ge(s_a, j + 1)
                    sp.wait_ge(s_v, j + 1)
                    sp.dma_start(rows[j * P:(j + 1) * P, :, :], out[:, j % 2, :, :]).then_inc(s_st[j % 2], 16)
                sp.wait_ge(s_st[0], 16 * ((s.NT + 1) // 2))
                sp.wait_ge(s_st[1], 16 * (s.NT // 2))


def store_table(nc, k, name, src, table):
    load_rows(nc, k, name, [(table.rearrange("(t p) c -> p t c", p=P), src)])


def graph_transformer(nc, k, l, X, order, W, table):
    s = k.s
    NT, NP = s.NT, s.NP
    heads, rels = W["pri"].shape[1], W["pri"].shape[2]
    FW = D + heads
    n = f"g{l}"
    with ExitStack() as outer:
        def sb(nm, shape, dt, where=outer):
            return where.enter_context(nc.sbuf_tensor(f"{n}_{nm}", shape, dt))

        scores = sb("scores", [P, s.T * heads], F32)
        peaks = sb("peaks", [P, NT, heads], F32)
        with ExitStack() as ctx:
            q3 = sb("q3", [P, 3, NP], BF16, ctx)
            with ExitStack() as c2:
                x_t = sb("x_t", [P, NP], F32, c2)
                k_t = sb("k_t", [P, NP], F32, c2)
                v_t = sb("v_t", [P, NP], F32, c2)
                transpose_all(nc, k, f"{n}_xt", X, x_t)
                typed_linear(nc, k, f"{n}_k", x_t, W["Wk"][l], k_t)
                typed_linear(nc, k, f"{n}_v", x_t, W["Wv"][l], v_t)
                with ExitStack() as c3:
                    wk = sb("wk", [P, rels, D], F32, c3)
                    wv = sb("wv", [P, rels, D], F32, c3)
                    pri = sb("pri", [P, rels], F32, c3)
                    relation_weights(nc, k, f"{n}_wk", W["Watt"][l], W["pri"][l], wk, pri)
                    relation_weights(nc, k, f"{n}_wv", W["Wmsg"][l], None, wv, None)
                    relation_table(nc, k, f"{n}_tab", k_t, v_t, wk, wv, table)
                typed_linear(nc, k, f"{n}_q", x_t, W["Wq"][l], k_t)
                q = v_t[:, :].rearrange("p (a b) -> p a b", b=D)
                untranspose_all(nc, k, f"{n}_qn", k_t, q)
                steps(nc, f"{n}_q3", lambda link, dve: split3_steps(link, dve, v_t[:, :], [q3[:, j, :] for j in range(3)], k_t[:, :]))
            gather_rows(nc, k, f"{n}_e1", order, order.row, table, 2 * D, "dot", (D, 2 * D), heads, q3, scores)
        steps(nc, f"{n}_pk", lambda link, dve: link(dve.memset(peaks[:, :, :], -BIG)))
        segment_max(nc, k, f"{n}_e2", order, heads, scores, peaks)
        acc = sb("acc", [P, 2, NT * FW], F32)
        with ExitStack() as ctx:
            peaks3 = sb("peaks3", [P, 3, NT * heads], BF16, ctx)
            rest = sb("rest", [P, NT * heads], F32, ctx)

            def prepare(link, dve):
                split3_steps(link, dve, flat(peaks[:, :, :]), [peaks3[:, j, :] for j in range(3)], rest[:, :])
                link(dve.memset(acc[:, :, :], 0.0))
            steps(nc, f"{n}_pre", prepare)
            weigh_rows(nc, k, f"{n}_e3", order, heads, D, scores, peaks3, acc)
        with ExitStack() as ctx:
            agg = sb("agg", [P, NT, D], F32, ctx)
            a_t = sb("a_t", [P, NP], F32, ctx)
            o_t = sb("o_t", [P, NP], F32, ctx)
            den = sb("den", [P, NT * heads], F32, ctx)
            al = sb("al", [P, NT], F32, ctx)
            sk = sb("sk", [P, rels], F32, ctx)
            gain = sb("gain", [P, 2, D], F32, ctx)
            load_rows(nc, k, f"{n}_ld", [(sk[:, :], row_bcast(W["skip"][l])), (gain[:, 0, :], row_bcast(W["ln_g"][l])),
                                         (gain[:, 1, :], row_bcast(W["ln_b"][l]))])

            def normalise(link, dve):
                a3 = acc[:, 0, :].rearrange("p (t c) -> p t c", c=FW)
                link(dve.tensor_tensor(acc[:, 0, :], acc[:, 0, :], acc[:, 1, :], ALU.add))
                d3 = den[:, :].rearrange("p (t h) -> p t h", h=heads)
                link(dve.tensor_scalar(d3, a3[:, :, D:FW], 1e-16, None, ALU.add))
                link(dve.reciprocal(den[:, :], den[:, :]))
                link(dve.tensor_tensor(agg[:, :, :].rearrange("p t (h c) -> p t h c", h=heads),
                                       a3[:, :, 0:D].rearrange("p t (h c) -> p t h c", h=heads),
                                       d3.unsqueeze(3).to_broadcast([P, NT, heads, D // heads]), ALU.mult))
            steps(nc, f"{n}_norm", normalise)
            transpose_all(nc, k, f"{n}_at", agg, a_t)
            typed_linear(nc, k, f"{n}_o", a_t, W["Wa"][l], o_t, silu=True)
            untranspose_all(nc, k, f"{n}_on", o_t, agg)
            s_sk = ctx.enter_context(signal(nc, f"{n}_s_sk"))
            s_mix = ctx.enter_context(signal(nc, f"{n}_s_mix"))
            hit = sb("hit", [P, NT], F32, ctx)
            with nc.Block() as block:
                @block.scalar
                def _(act):
                    act.activation(sk[:, :], sk[:, :], ACT.Sigmoid).then_inc(s_sk, 1)

                @block.vector
                def _(dve):
                    link = Chain(dve, s_mix).link
                    dve.wait_ge(s_sk, 1)
                    link(dve.memset(al[:, :], 0.0))
                    for t in range(rels):
                        link(dve.tensor_scalar(hit[:, :], k.type_col[:, :], float(t), sk[:, t:t + 1],
                                               ALU.is_equal, ALU.mult))
                        link(dve.tensor_tensor(al[:, :], al[:, :], hit[:, :], ALU.add))
                    link(dve.tensor_tensor(agg[:, :, :], agg[:, :, :], X[:, :, :], ALU.subtract))
                    link(dve.tensor_tensor(agg[:, :, :], agg[:, :, :], over_last(al[:, :], D), ALU.mult))
                    link(dve.tensor_tensor(X[:, :, :], X[:, :, :], agg[:, :, :], ALU.add))
            layer_norm(nc, k, f"{n}_ln", X, gain[:, 0, :], gain[:, 1, :])


def split3_steps(link, dve, src, parts, rest):
    link(dve.tensor_copy(parts[0], src))
    link(dve.tensor_tensor(rest, src, parts[0], ALU.subtract))
    link(dve.tensor_copy(parts[1], rest))
    link(dve.tensor_tensor(rest, rest, parts[1], ALU.subtract))
    link(dve.tensor_copy(parts[2], rest))


def sage(nc, k, X, order, W, table):
    s = k.s
    NT = s.NT
    width = D + 4
    with ExitStack() as outer:
        def sb(nm, shape, dt, where=outer):
            return where.enter_context(nc.sbuf_tensor(f"sage_{nm}", shape, dt))

        acc = sb("acc", [P, 2, NT * width], F32)
        with ExitStack() as ctx:
            row = sb("row", [P, NT, width], F32, ctx)

            def fill(link, dve):
                link(dve.memset(row[:, :, D:width], 1.0))
                link(dve.tensor_copy(row[:, :, 0:D], X[:, :, :]))
                link(dve.memset(acc[:, :, :], 0.0))
            steps(nc, "sage_fill", fill)
            store_table(nc, k, "sage_store", row[:, :, :], table)
        gather_sum(nc, k, "sage_e", order, order.row, table, width, acc)
        mean = sb("mean", [P, NT, D], F32)
        x_t = sb("x_t", [P, s.NP], F32)
        m_t = sb("m_t", [P, s.NP], F32)
        some = sb("some", [P, NT], F32)
        cnt = sb("cnt", [P, NT], F32)
        w = sb("w", [P, 2, D], F32)
        wt = sb("wt", [P, 2, D], F32)
        bias = sb("bias", [P, 2, D], F32)
        y = sb("y", [P, NT, D], F32)
        load_rows(nc, k, "sage_ld", [(w[:, 0, :], W["W_self"]), (w[:, 1, :], W["W_neigh"]),
                                     (bias[:, 0, :], row_bcast(W["b_self"])), (bias[:, 1, :], row_bcast(W["b_neigh"]))])

        def average(link, dve):
            a3 = acc[:, 0, :].rearrange("p (t c) -> p t c", c=width)
            link(dve.tensor_tensor(acc[:, 0, :], acc[:, 0, :], acc[:, 1, :], ALU.add))
            link(dve.tensor_scalar(some[:, :].unsqueeze(2), a3[:, :, D:D + 1], 0.0, None, ALU.is_gt))
            link(dve.tensor_scalar(cnt[:, :].unsqueeze(2), a3[:, :, D:D + 1], 1.0, None, ALU.max))
            link(dve.reciprocal(cnt[:, :], cnt[:, :]))
            link(dve.tensor_tensor(mean[:, :, :], a3[:, :, 0:D], over_last(cnt[:, :], D), ALU.mult))
            link(dve.tensor_tensor(y[:, :, :], over_last(some[:, :], D), over_mid(bias[:, 1, :], NT), ALU.mult))
            link(dve.tensor_tensor(y[:, :, :], y[:, :, :], over_mid(bias[:, 0, :], NT), ALU.add))
        steps(nc, "sage_avg", average)
        transpose_weights(nc, k, "sage_wt", w, wt, 2)
        transpose_all(nc, k, "sage_xt", X, x_t)
        transpose_all(nc, k, "sage_mt", mean, m_t)
        linear(nc, k, "sage_lin", [x_t, m_t], [wt[:, 0, :], wt[:, 1, :]], D, lambda a, m: mean[:, a:a + m, :])

        def finish(link, dve):
            link(dve.tensor_tensor(y[:, :, :], y[:, :, :], mean[:, :, :], ALU.add))
            link(dve.tensor_scalar(y[:, :, :], y[:, :, :], 0.0, None, ALU.max))
            link(dve.tensor_tensor(X[:, :, :], X[:, :, :], y[:, :, :], ALU.add))
        steps(nc, "sage_fin", finish)
    layer_norm(nc, k, "sage_ln", X)


def transpose_weights(nc, k, name, w, wt, n):
    def produce(pe, c, bank):
        return pe.transpose(k.psum[:, bank, 0:D], w[:, c, :], k.ident[:, :])

    banked(nc, k, name, n, produce, lambda copy, c, bank: copy(wt[:, c, :], k.psum[:, bank, 0:D]))


def gated_graph(nc, k, X, order, W, table):
    s = k.s
    NT, NP = s.NT, s.NP
    rounds = W["weight"].shape[0]
    with ExitStack() as outer:
        def sb(nm, shape, dt, where=outer):
            return where.enter_context(nc.sbuf_tensor(f"ggn_{nm}", shape, dt))

        w = sb("w", [P, 7, D], F32)
        wt = sb("wt", [P, 7, D], F32)
        wm = sb("wm", [P, rounds, D], F32)
        bias = sb("bias", [P, 7, D], F32)
        H = sb("H", [P, NT, D], F32)
        h_t = sb("h_t", [P, NP], F32)
        a_t = sb("a_t", [P, NP], F32)
        M = sb("M", [P, NT, D], F32)
        acc = sb("acc", [P, 2, NT * D], F32)
        load_rows(nc, k, "ggn_ld", [
            (w[:, 0:3, :], W["w_ih"].rearrange("(a p) c -> p a c", p=P)),
            (w[:, 3:6, :], W["w_hh"].rearrange("(a p) c -> p a c", p=P)),
            (w[:, 6, :], W["lin_w"]), (wm[:, :, :], W["weight"].rearrange("l i o -> i l o")),
            (flat(bias[:, 0:3, :]), row_bcast(W["b_ih"])), (flat(bias[:, 3:6, :]), row_bcast(W["b_hh"])),
            (bias[:, 6, :], row_bcast(W["lin_b"]))])
        transpose_weights(nc, k, "ggn_wt", w, wt, 7)
        steps(nc, "ggn_b", lambda link, dve: link(
            dve.tensor_tensor(bias[:, 0:2, :], bias[:, 0:2, :], bias[:, 3:5, :], ALU.add)))
        transpose_all(nc, k, "ggn_xt", X, h_t)
        linear(nc, k, "ggn_lin", [h_t], [wt[:, 6, :]], D, lambda a, m: H[:, a:a + m, :])
        steps(nc, "ggn_lb", lambda link, dve: link(
            dve.tensor_tensor(H[:, :, :], H[:, :, :], over_mid(bias[:, 6, :], NT), ALU.add)))
        for r in range(rounds):
            n = f"ggn{r}"
            transpose_all(nc, k, f"{n}_ht", H, h_t)
            linear(nc, k, f"{n}_m", [h_t], [wm[:, r, :]], D, lambda a, m: M[:, a:a + m, :])
            store_table(nc, k, f"{n}_st", M[:, :, :], table)
            steps(nc, f"{n}_z", lambda link, dve: link(dve.memset(acc[:, :, :], 0.0)))
            gather_sum(nc, k, f"{n}_e", order, order.node, table, D, acc)
            steps(nc, f"{n}_s", lambda link, dve: link(
                dve.tensor_tensor(flat(M[:, :, :]), acc[:, 0, :], acc[:, 1, :], ALU.add)))
            transpose_all(nc, k, f"{n}_at", M, a_t)
            gru(nc, k, n, H, h_t, a_t, wt, bias)
        steps(nc, "ggn_fin", lambda link, dve: link(
            dve.tensor_tensor(X[:, :, :], X[:, :, :], H[:, :, :], ALU.add)))
    layer_norm(nc, k, "ggn_ln", X)


def gru(nc, k, n, H, h_t, a_t, wt, bias):
    s = k.s
    parts = chunked(s.NT, 4)
    with ExitStack() as ctx:
        def sb(nm, shape, dt):
            return ctx.enter_context(nc.sbuf_tensor(f"{n}_{nm}", shape, dt))

        g = sb("gates", [P, 2, 4, 4, D], F32)
        t = sb("t", [P, 2, 4, D], F32)
        s_mm, s_g, s_rz, s_n, s_tanh, s_d = (ctx.enter_context(signal(nc, f"{n}_{x}"))
                                             for x in ("s_mm", "s_g", "s_rz", "s_n", "s_tanh", "s_d"))
        with nc.Block() as block:
            @block.tensor
            def _(pe):
                for c, (a, m) in enumerate(parts):
                    if c >= 2:
                        pe.wait_ge(s_g, c - 1)
                    for j in range(m):
                        bank = 4 * (c % 2) + j
                        xa, xh = a_t[:, (a + j) * P:(a + j + 1) * P], h_t[:, (a + j) * P:(a + j + 1) * P]
                        pe.matmul(k.psum[:, bank, 0:2 * D], xa, flat(wt[:, 0:2, :]), start=True, stop=False)
                        pe.matmul(k.psum[:, bank, 0:2 * D], xh, flat(wt[:, 3:5, :]), start=False, stop=True)
                        pe.matmul(k.psum[:, bank, 2 * D:3 * D], xa, wt[:, 2, :], start=True, stop=True)
                        last = pe.matmul(k.psum[:, bank, 3 * D:4 * D], xh, wt[:, 5, :], start=True, stop=True)
                    last.then_inc(s_mm, 1)

            @block.scalar
            def _(act):
                for c, (a, m) in enumerate(parts):
                    act.wait_ge(s_g, c + 1)
                    rz = g[:, c % 2, 0:m, 0:2, :]
                    act.activation(rz, rz, ACT.Sigmoid).then_inc(s_rz, 1)
                    act.wait_ge(s_n, c + 1)
                    act.activation(t[:, c % 2, 0:m, :], t[:, c % 2, 0:m, :], ACT.Tanh).then_inc(s_tanh, 1)

            @block.vector
            def _(dve):
                ch = Chain(dve, s_d)
                brow = bias[:, 0:3, :]
                for c, (a, m) in enumerate(parts):
                    b0 = 4 * (c % 2)
                    dve.wait_ge(s_mm, c + 1)
                    for j in range(m):
                        dve.tensor_tensor(g[:, c % 2, j, 0:3, :], k.psum[:, b0 + j, 0:3 * D].rearrange("p (a b) -> p a b", b=D),
                                          brow, ALU.add)
                        last = dve.tensor_tensor(g[:, c % 2, j, 3, :], k.psum[:, b0 + j, 3 * D:4 * D], bias[:, 5, :], ALU.add)
                    last.then_inc(s_g, 1)
                    dve.wait_ge(s_rz, c + 1)
                    tt = t[:, c % 2, 0:m, :]
                    ch.link(dve.tensor_tensor(tt, g[:, c % 2, 0:m, 0, :], g[:, c % 2, 0:m, 3, :], ALU.mult))
                    dve.tensor_tensor(tt, tt, g[:, c % 2, 0:m, 2, :], ALU.add).then_inc(s_n, 1)
                    dve.wait_ge(s_tanh, c + 1)
                    h = H[:, a:a + m, :]
                    ch.link(dve.tensor_tensor(h, h, tt, ALU.subtract))
                    ch.link(dve.tensor_tensor(h, h, g[:, c % 2, 0:m, 1, :], ALU.mult))
                    ch.link(dve.tensor_tensor(h, h, tt, ALU.add))


def gat(nc, k, n, in_t, ws, heads, width, att_src, att_dst, order, table, out):
    s = k.s
    NT = s.NT
    row = width + heads
    hw = width // heads
    with ExitStack() as outer:
        def sb(nm, shape, dt, where=outer):
            return where.enter_context(nc.sbuf_tensor(f"{n}_{nm}", shape, dt))

        scores = sb("scores", [P, s.T * heads], F32)
        peaks = sb("peaks", [P, NT, heads], F32)
        own = sb("own", [P, NT, heads], F32)
        to = sb("to", [P, NT, heads], F32)
        acc = sb("acc", [P, 2, NT * row], F32)
        peaks3 = sb("peaks3", [P, 3, NT * heads], BF16)
        keep_h = outer.enter_context(ExitStack())
        h = sb("h", [P, NT, row], F32, keep_h)
        with ExitStack() as ctx:
            att = sb("att", [P, 2, width], F32, ctx)
            prod = sb("prod", [P, NT, width], F32, ctx)
            load_rows(nc, k, f"{n}_ld", [(att[:, 0, :], row_bcast(att_src)), (att[:, 1, :], row_bcast(att_dst))])
            linear(nc, k, f"{n}_h", in_t, ws, width, lambda a, m: h[:, a:a + m, 0:width])

            def node_scores(link, dve):
                for side, dst in ((0, h[:, :, width:row]), (1, to[:, :, :])):
                    link(dve.tensor_tensor(prod[:, :, :], h[:, :, 0:width], over_mid(att[:, side, :], NT), ALU.mult))
                    link(dve.tensor_reduce(dst, prod[:, :, :].rearrange("p t (h c) -> p t h c", c=hw), AX.X, ALU.add))
                link(dve.tensor_tensor(own[:, :, :], h[:, :, width:row], to[:, :, :], ALU.add))
                link(dve.tensor_scalar(peaks[:, :, :], own[:, :, :], NEG_SLOPE, None, ALU.mult))
                link(dve.tensor_tensor(own[:, :, :], own[:, :, :], peaks[:, :, :], ALU.max))
                link(dve.tensor_copy(peaks[:, :, :], own[:, :, :]))
            steps(nc, f"{n}_sc", node_scores)
        store_table(nc, k, f"{n}_st", h[:, :, :], table)
        with ExitStack() as ctx:
            to3 = sb("to3", [P, 3, NT * heads], BF16, ctx)
            rest = sb("rest", [P, NT * heads], F32, ctx)
            steps(nc, f"{n}_to3", lambda link, dve: split3_steps(
                link, dve, flat(to[:, :, :]), [to3[:, j, :] for j in range(3)], rest[:, :]))
            gather_rows(nc, k, f"{n}_e1", order, order.node, table, row, "add", (0, width), heads, to3, scores)
        segment_max(nc, k, f"{n}_e2", order, heads, scores, peaks)
        s_own = outer.enter_context(signal(nc, f"{n}_s_own"))
        s_exp = outer.enter_context(signal(nc, f"{n}_s_exp"))
        s_o = outer.enter_context(signal(nc, f"{n}_s_o"))
        a3 = acc[:, 0, :].rearrange("p (t c) -> p t c", c=row)
        with nc.Block() as block:
            @block.vector
            def _(dve):
                link = Chain(dve, s_o).link
                dve.tensor_tensor(own[:, :, :], own[:, :, :], peaks[:, :, :], ALU.subtract).then_inc(s_own, 1)
                split3_steps(link, dve, flat(peaks[:, :, :]), [peaks3[:, j, :] for j in range(3)], flat(to[:, :, :]))
                link(dve.memset(acc[:, 1, :], 0.0))
                dve.wait_ge(s_exp, 1)
                link(dve.tensor_copy(a3[:, :, width:row], own[:, :, :]))
                link(dve.tensor_tensor(a3[:, :, 0:width].rearrange("p t (h c) -> p t h c", h=heads),
                                       h[:, :, 0:width].rearrange("p t (h c) -> p t h c", h=heads),
                                       own[:, :, :].unsqueeze(3).to_broadcast([P, NT, heads, hw]), ALU.mult))

            @block.scalar
            def _(act):
                act.wait_ge(s_own, 1)
                act.activation(own[:, :, :], own[:, :, :], ACT.Exp).then_inc(s_exp, 1)
        keep_h.close()
        weigh_rows(nc, k, f"{n}_e3", order, heads, width, scores, peaks3, acc)

        def normalise(link, dve):
            link(dve.tensor_tensor(acc[:, 0, :], acc[:, 0, :], acc[:, 1, :], ALU.add))
            link(dve.tensor_copy(own[:, :, :], a3[:, :, width:row]))
            link(dve.reciprocal(own[:, :, :], own[:, :, :]))
            link(dve.tensor_tensor(out[:, :, :].rearrange("p t (h c) -> p t h c", h=heads),
                                   a3[:, :, 0:width].rearrange("p t (h c) -> p t h c", h=heads),
                                   own[:, :, :].unsqueeze(3).to_broadcast([P, NT, heads, hw]), ALU.mult))
        steps(nc, f"{n}_nrm", normalise)


def attention_network(nc, k, X, order, W, table1, table2):
    s = k.s
    NT, NP = s.NT, s.NP
    f1 = W["W1"].shape[1]
    with ExitStack() as outer:
        def sb(nm, shape, dt, where=outer):
            return where.enter_context(nc.sbuf_tensor(f"gat_{nm}", shape, dt))

        h_t = sb("h_t", [P, 2, NP], F32)
        wrow = sb("wrow", [P, 2, f1], F32)
        with ExitStack() as ctx:
            o1 = sb("o1", [P, NT, f1], F32, ctx)
            load_rows(nc, k, "gat_ld", [(wrow[:, 0, :], W["W1"])])
            transpose_all(nc, k, "gat_xt", X, h_t[:, 0, :])
            gat(nc, k, "ga", [h_t[:, 0, :]], [wrow[:, 0, :]], W["att_src1"].shape[0], f1,
                W["att_src1"].rearrange("h c -> (h c)"), W["att_dst1"].rearrange("h c -> (h c)"), order, table1, o1)
            b1 = sb("b1", [P, f1], F32, ctx)
            neg = sb("neg", [P, NT, f1], F32, ctx)
            load_rows(nc, k, "gat_lb", [(b1[:, :], row_bcast(W["b1"])),
                                        (wrow[:, :, 0:D], W["W2"].rearrange("(a p) c -> p a c", p=P))])
            s_n, s_e, s_d = (ctx.enter_context(signal(nc, f"gat_{x}")) for x in ("s_n", "s_e", "s_d"))
            with nc.Block() as block:
                @block.vector
                def _(dve):
                    link = Chain(dve, s_d).link
                    link(dve.tensor_tensor(o1[:, :, :], o1[:, :, :], over_mid(b1[:, :], NT), ALU.add))
                    dve.tensor_scalar(neg[:, :, :], o1[:, :, :], 0.0, None, ALU.min).then_inc(s_n, 1)
                    link(dve.tensor_scalar(o1[:, :, :], o1[:, :, :], 0.0, None, ALU.max))
                    dve.wait_ge(s_e, 1)
                    link(dve.tensor_scalar(neg[:, :, :], neg[:, :, :], -1.0, None, ALU.add))
                    link(dve.tensor_tensor(o1[:, :, :], o1[:, :, :], neg[:, :, :], ALU.add))

                @block.scalar
                def _(act):
                    act.wait_ge(s_n, 1)
                    act.activation(neg[:, :, :], neg[:, :, :], ACT.Exp).then_inc(s_e, 1)
            for half in range(2):
                transpose_all(nc, k, f"gat_ot{half}", o1[:, :, half * D:(half + 1) * D], h_t[:, half, :])
        o2 = sb("o2", [P, NT, D], F32)
        gat(nc, k, "gb", [h_t[:, 0, :], h_t[:, 1, :]], [wrow[:, 0, 0:D], wrow[:, 1, 0:D]], 1, D,
            W["att_src2"].rearrange("h c -> (h c)"), W["att_dst2"].rearrange("h c -> (h c)"), order, table2, o2)
        b2 = sb("b2", [P, D], F32)
        load_rows(nc, k, "gat_lb2", [(b2[:, :], row_bcast(W["b2"]))])

        def finish(link, dve):
            link(dve.tensor_tensor(X[:, :, :], X[:, :, :], o2[:, :, :], ALU.add))
            link(dve.tensor_tensor(X[:, :, :], X[:, :, :], over_mid(b2[:, :], NT), ALU.add))
        steps(nc, "gat_fin", finish)
    layer_norm(nc, k, "gat_ln", X)


def load_nodes(nc, k, x, node_type, X):
    s = k.s
    full = s.N // P
    left = s.N - full * P
    with ExitStack() as ctx:
        raw_row = ctx.enter_context(nc.sbuf_tensor("raw_row", [P, s.N], I32))
        raw_col = ctx.enter_context(nc.sbuf_tensor("raw_col", [P, s.NT], I32))
        s_z = ctx.enter_context(signal(nc, "ln_s_z"))
        s_in = ctx.enter_context(signal(nc, "ln_s_in"))
        s_d = ctx.enter_context(signal(nc, "ln_s_d"))
        with nc.Block() as block:
            @block.vector
            def _(dve):
                link = Chain(dve, s_d).link
                dve.memset(X[:, full, :], 0.0)
                dve.memset(raw_col[:, :], -1)
                dve.memset(k.type_row[:, s.N:s.NP], -1.0).then_inc(s_z, 1)
                dve.wait_ge(s_in, 16 * 5)
                link(dve.tensor_copy(k.type_row[:, 0:s.N], raw_row[:, :]))
                link(dve.tensor_copy(k.type_col[:, :], raw_col[:, :]))

            @block.sync
            def _(sp):
                sp.wait_ge(s_z, 1)
                sp.dma_start(X[:, 0:full, :], x[0:full * P, :].rearrange("(t p) c -> p t c", p=P)).then_inc(s_in, 16)
                sp.dma_start(X[0:left, full, :], x[full * P:s.N, :]).then_inc(s_in, 16)
                sp.dma_start(raw_row[:, :], row_bcast(node_type)).then_inc(s_in, 16)
                with nc.allow_non_contiguous_dma("node types by column, once"):
                    sp.dma_start(raw_col[:, 0:full], node_type[0:full * P].rearrange("(t p) -> p t", p=P)).then_inc(s_in, 16)
                    sp.dma_start(raw_col[0:left, full:full + 1], node_type[full * P:s.N].unsqueeze(1)).then_inc(s_in, 16)


def store_nodes(nc, k, X, out):
    s = k.s
    full = s.N // P
    left = s.N - full * P
    with signal(nc, "s_out") as s_out, nc.Block() as block:
        @block.sync
        def _(sp):
            sp.dma_start(out[0:full * P, :].rearrange("(t p) c -> p t c", p=P), X[:, 0:full, :]).then_inc(s_out, 16)
            sp.dma_start(out[full * P:s.N, :], X[0:left, full, :]).then_inc(s_out, 16)
            sp.wait_ge(s_out, 32)


def group(arrays, prefix):
    return {n[len(prefix):]: a for n, a in arrays.items() if n.startswith(prefix)}


def gnn_program(nc, a, out, upto=9):
    s = Shapes(a["x"].shape[0], a["src"].shape[0])
    turn[:] = range(FIRST_SEMAPHORE, LAST_SEMAPHORE + 1)

    def dram(n, shape):
        return nc.dram_tensor(n, shape, F32, kind="Internal").ap()

    w1 = group(a, "L0_gnn_")
    rels = w1["pri"].shape[2]
    gat_w = group(a, "L3_gnn_")
    heads, f1 = gat_w["att_src1"].shape[0], gat_w["W1"].shape[1]
    with ExitStack() as ctx:
        k = Kit(nc, ctx, s)
        k.type_col = k.sb("type_col", [P, s.NT], F32)
        k.stash = dram("stash", [P, s.T, f1])
        X = k.sb("X", [P, s.NT, D], F32)
        by_dst = Edges(k.sb, nc, s, "by_dst", True)
        by_src = Edges(k.sb, nc, s, "by_src", False)
        constants(nc, k)
        with nc.sbuf_tensor("pair", [P, s.T, 2], F16) as pair:
            k.pair = pair
            bucket_edges(nc, k, by_dst, a["dst"], a["src"], a["edge_type_8"], "bd", True)
            sort_tiles(nc, k, by_dst)
        bucket_edges(nc, k, by_src, a["src"], a["dst"], None, "bs", False)
        with nc.sbuf_tensor("type_row", [P, s.NP], F32) as type_row, nc.sbuf_tensor("X0", [P, s.NT, D], F32) as X0:
            k.type_row = type_row
            load_nodes(nc, k, a["x"], a["node_type_8"], X)
            steps(nc, "keep", lambda link, dve: link(dve.tensor_copy(X0[:, :, :], X[:, :, :])))
            table = dram("relation_table", [s.NP * rels, 2 * D])
            for l in range(w1["Wk"].shape[0]):
                graph_transformer(nc, k, l, X, by_dst, w1, table)
            with nc.sbuf_tensor("e_t", [P, s.NP], F32) as e_t, nc.sbuf_tensor("wff", [P, 2, D], F32) as wff:
                load_rows(nc, k, "ff_ld", [(wff[:, 0, :], w1["Wff"]), (wff[:, 1, :], row_bcast(w1["bff"]))])
                transpose_all(nc, k, "ff_t", X, e_t)
                linear(nc, k, "ff", [e_t], [wff[:, 0, :]], D, lambda t, m: X[:, t:t + m, :])

                def residual(link, dve):
                    link(dve.tensor_tensor(X[:, :, :], X[:, :, :], over_mid(wff[:, 1, :], s.NT), ALU.add))
                    link(dve.tensor_tensor(X[:, :, :], X[:, :, :], X0[:, :, :], ALU.add))
                steps(nc, "ff_r", residual)
        layer_norm(nc, k, "ff_ln", X)
        if upto >= 1:
            sage(nc, k, X, by_src, group(a, "L1_gnn_"), dram("sage_table", [s.NP, D + 4]))
        if upto >= 2:
            gated_graph(nc, k, X, by_dst, group(a, "L2_gnn_"), dram("message_table", [s.NP, D]))
        if upto >= 3:
            attention_network(nc, k, X, by_dst, gat_w, dram("gat_table1", [s.NP, f1 + heads]),
                              dram("gat_table2", [s.NP, D + 1]))
        store_nodes(nc, k, X, out)


def kernel(**inputs):
    import concourse.bacc as bacc
    from concourse.bass_utils import run_bass_kernel_spmd

    nc = bacc.Bacc("TRN2", target_bir_lowering=False, num_devices=1)
    arrays, aps = {}, {}
    for name, value in inputs.items():
        arrays[f"in_{name}"] = np.ascontiguousarray(value)
        aps[name] = nc.dram_tensor(f"in_{name}", arrays[f"in_{name}"].shape,
                                   mybir.dt.from_np(arrays[f"in_{name}"].dtype), kind="ExternalInput").ap()
    nodes, features = inputs["x"].shape
    out = nc.dram_tensor("out", [nodes, features], F32, kind="ExternalOutput").ap()
    gnn_program(nc, aps, out)
    result = run_bass_kernel_spmd(nc, [arrays], core_ids=[0])
    return result.results[0]["out"]
```

```python
from contextlib import ExitStack, contextmanager

import numpy as np

import concourse.bass as bass
from concourse import mybir

F32 = mybir.dt.float32
F16 = mybir.dt.float16
BF16 = mybir.dt.bfloat16
I32 = mybir.dt.int32
ALU = mybir.AluOpType
ACT = mybir.ActivationFunctionType
AX = mybir.AxisListType
ds = bass.ds

P = 128
D = 128
BIG = 3.0e38
LN_EPS = 1e-05


class Chain:

    def __init__(self, eng, sem, done=0):
        self.eng, self.sem, self.done, self.offset = eng, sem, done, 0

    def link(self, ins):
        ins.then_inc(self.sem, 1)
        self.done += 1
        self.eng.wait_ge(self.sem, self.offset + self.done)

    def enter(self, i, steps):
        self.offset, self.first, self.steps = i * steps, self.done, steps

    def leave(self, rounds):
        assert self.done - self.first == self.steps, (self.done - self.first, self.steps)
        self.offset, self.done = 0, self.first + rounds * self.steps


def flat(ap):
    return ap.rearrange("p a b -> p (a b)")


def over_last(ap, n):
    return ap.unsqueeze(2).to_broadcast([ap.shape[0], ap.shape[1], n])


def over_mid(ap, n):
    return ap.unsqueeze(1).to_broadcast([ap.shape[0], n, ap.shape[1]])


FIRST_SEMAPHORE, LAST_SEMAPHORE = 110, 250
turn = []


@contextmanager
def signal(nc, name):
    num = turn.pop(0)
    handle = nc.alloc_semaphore(name=name, num=num)
    yield handle
    nc.gpsimd.sem_clear(handle)
    nc.release_semaphore(handle)
    turn.append(num)


def free(eng, *sems, by=1):
    for sem in sems:
        eng.sem_inc(sem, by)


class Shapes:

    def __init__(self, nodes, edges):
        self.N, self.E = nodes, edges
        self.NT = -(-nodes // P)
        self.NP = self.NT * P
        self.EP = max(p for p in range(1, P + 1) if edges % p == 0 and (edges // p) % 4 == 0)
        self.ET = edges // self.EP
        most = (edges + self.NT * (P - 1)) // P
        self.T = -(-most // 32) * 32
        assert self.NT == 25 and self.EP == 125 and self.T == 416


class Edges:

    def __init__(self, sb, nc, s, name, detailed):
        self.row = sb(f"{name}_row", [P, s.T], I32)
        self.local = sb(f"{name}_local", [P, s.T], F32)
        self.tile = sb(f"{name}_tile", [1, s.T], I32)
        if detailed:
            self.node = sb(f"{name}_node", [P, s.T], I32)
            self.last = sb(f"{name}_last", [P, s.T], F32)
            self.cut = sb(f"{name}_cut", [P, s.T], F32)
            self.gather = nc.dram_tensor(f"{name}_gather", [P, s.T * P], BF16, kind="Internal").ap()


def constants(nc, k):
    with nc.Block() as block:
        @block.gpsimd
        def _(pool):
            pool.iota(k.iota[:, :], [[1, P]], base=0, channel_multiplier=0,
                      allow_small_or_imprecise_dtypes=True).then_inc(k.s_iota, 1)
            pool.iota(k.iota16[:, :], [[1, k.s.T]], base=0, channel_multiplier=0,
                      allow_small_or_imprecise_dtypes=True).then_inc(k.s_iota, 1)
            pool.iota(k.iota_p[:, :], [[0, 1]], base=0, channel_multiplier=1,
                      allow_small_or_imprecise_dtypes=True).then_inc(k.s_iota, 1)
            pool.iota(k.ident[:, :], [[1, P]], base=0, channel_multiplier=-1,
                      allow_small_or_imprecise_dtypes=True).then_inc(k.s_iota, 1)

        @block.vector
        def _(dve):
            chain = Chain(dve, k.s_const)
            dve.wait_ge(k.s_iota, 4)
            chain.link(dve.tensor_scalar(k.upto[:, :], k.ident[:, :], 0.0, -1.0, ALU.is_le, ALU.mult))
            chain.link(dve.tensor_scalar(k.ident[:, :], k.ident[:, :], 0.0, None, ALU.is_equal))
            chain.link(dve.memset(k.ones16[:, :], 1.0))
            chain.link(dve.memset(k.zeros16[:, :], 0.0))
            chain.link(dve.memset(k.ones[:, :], 1.0))


def bucket_edges(nc, k, order, key_d, node_d, type_d, name, refine):
    s = k.s
    T, NT, EP, ET = s.T, s.NT, s.EP, s.ET
    CH = 500
    NCH = NT * ET // CH
    half = NCH // 4
    TC = T // 104
    assert CH * NCH == NT * ET and NCH % 4 == 0
    with ExitStack() as ctx:
        def sb(n, shape, dt):
            return ctx.enter_context(nc.sbuf_tensor(f"{name}_{n}", shape, dt))

        def sem(n):
            return ctx.enter_context(signal(nc, f"{name}_{n}"))

        key = sb("key", [EP, ET], I32)
        node = sb("node_in", [EP, ET], I32)
        typ = sb("type_in", [EP, ET], I32)
        work = sb("work", [EP, ET], I32)
        low = sb("low", [EP, ET], I32)
        bucket = sb("bucket", [EP, ET], F16)
        U = sb("U", [EP, ET], F32)
        W = sb("W", [EP, ET], F32)
        pcol = sb("pcol", [EP, ET], F32)
        tcol = sb("tcol", [EP, ET], F32)
        posf = sb("posf", [EP, ET], F32)
        outer = ExitStack()
        with outer:
            def sbo(n, shape, dt):
                return outer.enter_context(nc.sbuf_tensor(f"{name}_{n}", shape, dt))
            onehot = sbo("onehot", [EP, NT, ET], F16)
            total = sbo("total", [EP, NT, ET], F32)
            before = sbo("before", [EP, NT, ET], F32)
            count = sbo("count", [EP, NT], F32)
            counti = sbo("counti", [EP, NT], I32)
            tiles = sbo("tiles", [EP, NT], F32)
            start = sbo("start", [EP, NT], F32)
            startc = sbo("startc", [EP, NT], F32)
            tix = sbo("tix", [EP, TC], F32)
            tbl = sbo("tbl", [EP, TC, NT], F32)
            tsum = sbo("tsum", [EP, TC], F32)
            tnum = sbo("tnum", [EP, TC], I32)
            s_in = sem("s_in")
            s_hot = sem("s_hot")
            s_mm = sem("s_mm")
            s_ev = sem("s_ev")
            s_tiles = sem("s_tiles")
            s_out = sem("s_out")
            s_dve = sem("s_dve")
            hot_f = onehot[:, :, :].rearrange("p b t -> p (b t)")
            tot_f = total[:, :, :].rearrange("p b t -> p (b t)")
            bef_f = before[:, :, :].rearrange("p b t -> p (b t)")
            with nc.Block() as block:
                @block.sync
                def _(sp):
                    sp.dma_start(key[:, :], key_d.rearrange("(p t) -> p t", p=EP)).then_inc(s_in, 16)
                    sp.dma_start(node[:, :], node_d.rearrange("(p t) -> p t", p=EP)).then_inc(s_in, 16)
                    if type_d is not None:
                        sp.dma_start(typ[:, :], type_d.rearrange("(p t) -> p t", p=EP)).then_inc(s_in, 16)
                    sp.wait_ge(s_tiles, 1)
                    sp.dma_start(order.tile[0:1, :], tnum[0:T // TC, :]).then_inc(s_out, 16)
                    sp.wait_ge(s_out, 16)

                @block.vector
                def _(dve):
                    c = Chain(dve, s_dve)
                    dve.wait_ge(s_in, 48 if type_d is not None else 32)
                    c.link(dve.tensor_scalar(work[:, :], key[:, :], 7, None, ALU.arith_shift_right))
                    c.link(dve.tensor_copy(bucket[:, :], work[:, :]))
                    dve.tensor_tensor(onehot[:, :, :], over_mid(bucket[:, :], NT),
                                      over_last(k.iota16[0:EP, 0:NT], ET), ALU.is_equal).then_inc(s_hot, 1)
                    if type_d is not None:
                        c.link(dve.tensor_scalar(work[:, :], node[:, :], 3, None, ALU.logical_shift_left))
                        c.link(dve.tensor_tensor(node[:, :], work[:, :], typ[:, :], ALU.bitwise_or))
                    c.link(dve.tensor_scalar(work[:, :], node[:, :], 4, None, ALU.arith_shift_right))
                    c.link(dve.tensor_scalar(U[:, :], work[:, :], 1.0, None, ALU.add))
                    c.link(dve.tensor_scalar(work[:, :], node[:, :], 15, 7, ALU.bitwise_and, ALU.logical_shift_left))
                    c.link(dve.tensor_scalar(low[:, :], key[:, :], 127, None, ALU.bitwise_and))
                    c.link(dve.tensor_tensor(W[:, :], work[:, :], low[:, :], ALU.add))
                    c.link(dve.tensor_scalar(tix[:, :], k.iota_p[0:EP, :].to_broadcast([EP, TC]), float(TC), None, ALU.mult))
                    c.link(dve.tensor_tensor(tix[:, :], tix[:, :], k.iota[0:EP, 0:TC], ALU.add))
                    dve.wait_ge(s_ev, NCH + 4)
                    c.link(dve.tensor_reduce(count[:, :], total[:, :, :], AX.X, ALU.add))
                    c.link(dve.tensor_scalar(count[:, :], count[:, :], 127.0, None, ALU.add))
                    c.link(dve.tensor_copy(counti[:, :], count[:, :]))
                    c.link(dve.tensor_scalar(counti[:, :], counti[:, :], 7, None, ALU.arith_shift_right))
                    c.link(dve.tensor_copy(tiles[:, :], counti[:, :]))
                    c.link(dve.tensor_tensor_scan(start[:, :], tiles[:, :], tiles[:, :], 0.0, ALU.add, ALU.max))
                    c.link(dve.tensor_tensor(start[:, :], start[:, :], tiles[:, :], ALU.subtract))
                    c.link(dve.tensor_scalar(startc[:, :], start[:, :], float(P), None, ALU.mult))
                    c.link(dve.tensor_tensor(tbl[:, :, :], over_mid(start[:, :], TC), over_last(tix[:, :], NT), ALU.is_le))
                    c.link(dve.tensor_reduce(tsum[:, :], tbl[:, :, :], AX.X, ALU.add))
                    dve.tensor_scalar(tnum[:, :], tsum[:, :], -1.0, None, ALU.add).then_inc(s_tiles, 1)
                    for b in range(NT):
                        last = dve.tensor_tensor_scan(total[:, b, :], total[:, b, :], total[:, b, :],
                                                      startc[:, b:b + 1], ALU.add, ALU.max)
                    c.link(last)
                    dve.wait_ge(s_ev, NCH * 2 + 4)
                    c.link(dve.tensor_tensor(bef_f, bef_f, tot_f, ALU.add))
                    c.link(dve.tensor_tensor(bef_f, bef_f, hot_f, ALU.mult))
                    c.link(dve.tensor_reduce(posf[:, :], before[:, :, :].rearrange("p b t -> p t b"), AX.X, ALU.add))
                    c.link(dve.tensor_copy(work[:, :], posf[:, :]))
                    c.link(dve.tensor_scalar(low[:, :], work[:, :], 127, None, ALU.bitwise_and))
                    c.link(dve.tensor_copy(pcol[:, :], low[:, :]))
                    c.link(dve.tensor_scalar(low[:, :], work[:, :], 7, None, ALU.arith_shift_right))
                    c.link(dve.tensor_copy(tcol[:, :], low[:, :]))

                @block.tensor
                def _(pe):
                    pe.wait_ge(s_hot, 1)
                    for half_at in range(2):
                        tri = k.ones16 if half_at == 0 else k.upto
                        with pe.Fori(0, half) as i:
                            for u in range(4):
                                bank = 4 * half_at + u
                                pe.wait_ge(s_ev, i * 4 + (half_at * NCH + u + 1))
                                pe.matmul(k.psum[0:EP, bank, 0:CH], tri[0:EP, 0:EP],
                                          hot_f[:, ds(i * (4 * CH) + u * CH, CH)],
                                          start=True, stop=True).then_inc(s_mm, 1)

                @block.scalar
                def _(act):
                    free(act, s_ev, by=4)
                    for half_at in range(2):
                        dst = tot_f if half_at == 0 else bef_f
                        with act.Fori(0, half) as i:
                            for u in range(4):
                                act.wait_ge(s_mm, i * 4 + (half_at * NCH + u + 1))
                                act.activation(dst[:, ds(i * (4 * CH) + u * CH, CH)],
                                               k.psum[0:EP, 4 * half_at + u, 0:CH], ACT.Copy).then_inc(s_ev, 1)

        PER, SETS = 4, 4
        oh_t = sb("oh_t", [EP, SETS, PER, T], F16)
        oh_p = sb("oh_p", [EP, SETS, PER, P], F16)
        put = sb("put", [EP, SETS, 2, PER, P], F16)
        s_oh = [sem(f"s_oh{h}") for h in range(SETS)]
        s_u = [sem(f"s_u{h}") for h in range(SETS)]
        s_w = [sem(f"s_w{h}") for h in range(SETS)]
        s_used = [sem(f"s_used{h}") for h in range(SETS)]
        s_put = sem("s_put")
        s_d2 = sem("s_d2")
        ws = sb("ws", [P, T], I32)
        us = sb("us", [P, T], I32)
        val = sb("val", [P, T], F32)
        wl = sb("wl", [P, T], I32)
        with nc.Block() as block:
            @block.vector
            def _(dve):
                with dve.Fori(0, ET // (SETS * PER)) as i:
                    for h in range(SETS):
                        dve.wait_ge(s_used[h], i + 1)
                        for u in range(PER):
                            t = ds(i * (SETS * PER) + (h * PER + u), 1)
                            dve.tensor_scalar(oh_p[:, h, u, :], k.iota16[0:EP, 0:P], pcol[:, t], None,
                                              ALU.is_equal).then_inc(s_oh[h], 1)
                            dve.tensor_scalar(oh_t[:, h, u, :], k.iota16[0:EP, :], tcol[:, t], None,
                                              ALU.is_equal).then_inc(s_oh[h], 1)
                c = Chain(dve, s_d2)
                dve.wait_ge(s_put, 1)
                if refine:
                    c.link(dve.tensor_copy(k.pair[:, :, 0], k.psum[:, 0, 0:T]))
                    c.link(dve.tensor_copy(k.pair[:, :, 1], k.psum[:, 1, 0:T]))
                else:
                    decode(c, dve, k, order, k.psum[:, 0, 0:T], k.psum[:, 1, 0:T], us, ws, wl, val, None)

            @block.tensor
            def _(pe):
                free(pe, *s_used)
                for v in range(2):
                    pe.matmul(k.psum[:, v, 0:T], k.zeros16[0:EP, :], k.iota16[0:EP, :], start=True, stop=False)
                with pe.Fori(0, ET // (SETS * PER)) as i:
                    for h in range(SETS):
                        for u in range(PER):
                            pe.wait_ge(s_oh[h], i * (2 * PER) + (2 * u + 2))
                            pe.wait_ge(s_u[h], i * PER + (u + 1))
                            pe.wait_ge(s_w[h], i + 1)
                            for v in range(2):
                                last = pe.matmul(k.psum[:, v, 0:T], put[:, h, v, u, :], oh_t[:, h, u, :],
                                                 start=False, stop=False)
                        last.then_inc(s_used[h], 1)
                for v in range(2):
                    last = pe.matmul(k.psum[:, v, 0:T], k.zeros16[0:EP, :], k.iota16[0:EP, :], start=False, stop=True)
                last.then_inc(s_put, 1)

            @block.scalar
            def _(act):
                with act.Fori(0, ET // (SETS * PER)) as i:
                    for h in range(SETS):
                        act.wait_ge(s_used[h], i + 1)
                        for u in range(PER):
                            act.wait_ge(s_oh[h], i * (2 * PER) + (2 * u + 1))
                            act.nop(nofuse=True)
                            act.activation(put[:, h, 0, u, :], oh_p[:, h, u, :], ACT.Copy,
                                           scale=U[:, ds(i * (SETS * PER) + (h * PER + u), 1)]).then_inc(s_u[h], 1)

            @block.gpsimd
            def _(pool):
                with pool.Fori(0, ET // (SETS * PER)) as i:
                    for h in range(SETS):
                        pool.wait_ge(s_used[h], i + 1)
                        pool.wait_ge(s_oh[h], i * (2 * PER) + (2 * PER - 1))
                        pool.nop(nofuse=True)
                        pool.tensor_tensor(put[:, h, 1, :, :], oh_p[:, h, :, :],
                                           over_last(W[:, ds(i * (SETS * PER) + h * PER, PER)], P),
                                           ALU.mult).then_inc(s_w[h], 1)


def decode(c, dve, k, order, u_in, w_in, us, ws, wl, val, node):
    c.link(dve.tensor_scalar(val[:, :], u_in, 0.0, None, ALU.is_gt))
    c.link(dve.tensor_copy(ws[:, :], w_in))
    c.link(dve.tensor_scalar(us[:, :], u_in, -1.0, 0.0, ALU.add, ALU.max))
    c.link(dve.tensor_scalar(wl[:, :], us[:, :], 4, None, ALU.logical_shift_left))
    c.link(dve.tensor_scalar(us[:, :], ws[:, :], 7, None, ALU.arith_shift_right))
    c.link(dve.tensor_tensor(order.row[:, :], wl[:, :], us[:, :], ALU.bitwise_or))
    c.link(dve.tensor_scalar(wl[:, :], ws[:, :], 127, None, ALU.bitwise_and))
    c.link(dve.tensor_copy(order.local[:, :], wl[:, :]))
    c.link(dve.scalar_tensor_tensor(order.local[:, :], order.local[:, :], 1.0, val[:, :], ALU.add, ALU.mult))
    c.link(dve.tensor_scalar(order.local[:, :], order.local[:, :], -1.0, None, ALU.add))
    if node is not None:
        c.link(dve.tensor_scalar(node[:, :], order.row[:, :], 3, None, ALU.arith_shift_right))


def sort_tiles(nc, k, order):
    s = k.s
    T = s.T
    B = -(-T // P)
    width = [min(P, T - b * P) for b in range(B)]
    G = 8
    R = T // (2 * G)
    with ExitStack() as ctx:
        def sb(n, shape, dt):
            return ctx.enter_context(nc.sbuf_tensor(f"st_{n}", shape, dt))

        def sem(n):
            return ctx.enter_context(signal(nc, f"st_{n}"))

        def pair_of(n):
            return [sem(f"{n}{h}") for h in range(2)]

        key = sb("key", [P, T], F32)
        val = sb("val", [P, T], F32)
        a = sb("a", [P, T], I32)
        b_ = sb("b", [P, T], I32)
        w = sb("w", [P, T], I32)
        node = sb("node", [P, T], F16)
        ident16 = sb("ident16", [P, P], F16)
        diag = sb("diag", [P, P], F16)
        less = sb("less", [P, 2, G, P], F16)
        hot = sb("hot", [P, 2, G, P], F16)
        out = sb("out", [P, T, 2], F32)
        s_d, s_key = sem("s_d"), sem("s_key")
        s_bc, s_less, s_rank, s_hot, s_mv, s_out = (pair_of(n) for n in (
            "s_bc", "s_less", "s_rank", "s_hot", "s_mv", "s_out"))

        def near(i, h, by):
            return i + (h + by) // 2, (h + by) % 2

        def in_rounds(eng, position):
            for h in range(2):
                position(0, h, h == 0, False)
            with eng.Fori(1, R - 1) as i:
                for h in range(2):
                    position(i, h, False, False)
            for h in range(2):
                position(R - 1, h, False, h == 1)

        with nc.Block() as block:
            @block.vector
            def _(dve):
                c = Chain(dve, s_d)
                U, W = k.pair[:, :, 0], k.pair[:, :, 1]
                c.link(dve.tensor_copy(ident16[:, :], k.ident[:, :]))
                c.link(dve.tensor_scalar(diag[:, :], k.ident[:, :], float(P), None, ALU.mult))
                c.link(dve.tensor_scalar(val[:, :], U, 0.0, 256.0, ALU.is_equal, ALU.mult))
                c.link(dve.tensor_copy(a[:, :], W))
                c.link(dve.tensor_scalar(a[:, :], a[:, :], 127, None, ALU.bitwise_and))
                c.link(dve.tensor_tensor(key[:, :], val[:, :], a[:, :], ALU.add))
                c.link(dve.tensor_copy(node[:, :], key[:, :]))
                c.link(dve.tensor_scalar(key[:, :], key[:, :], float(P), k.iota_p[:, :], ALU.mult, ALU.add))
                dve.sem_inc(s_key, 1)
                free(dve, *s_less, *s_hot)

                def compare(i, h):
                    dve.wait_ge(s_bc[h], i + 1)
                    dve.wait_ge(s_rank[h], i + 1)
                    dve.tensor_tensor(less[:, h, :, :],
                                      k.psum[:, 2 * h:2 * h + 2, :].rearrange("p a (b c) -> p (a b) c", c=P),
                                      over_last(key[:, ds(i * (2 * G) + h * G, G)], P), ALU.is_gt).then_inc(s_less[h], 1)

                def spread(i, h):
                    dve.wait_ge(s_rank[h], i + 2)
                    dve.wait_ge(s_mv[h], i + 1)
                    dve.tensor_tensor(hot[:, h, :, :], over_mid(k.iota[:, :], G),
                                      over_last(k.psum[:, 4 + h, 0:G], P), ALU.is_equal).then_inc(s_hot[h], 1)

                def position(i, h, first, last):
                    compare(i, h)
                    if not first:
                        spread(*near(i, h, -1))

                in_rounds(dve, position)
                spread(R - 1, 1)
                for h in range(2):
                    dve.wait_ge(s_out[h], R + 1)
                decode(c, dve, k, order, out[:, :, 0], out[:, :, 1], a, w, b_, val, order.node)

            @block.tensor
            def _(pe):
                free(pe, *s_rank, *s_mv)
                pe.wait_ge(s_key, 1)

                def broadcast(i, h):
                    pe.wait_ge(s_less[h], i + 1)
                    for b in range(2):
                        pe.matmul(k.psum[:, 2 * h + b, :], k.ones16[0:1, :],
                                  over_mid(k.iota16[0:1, 0:P], 4), start=True, stop=False)
                        for u in range(4):
                            last = pe.matmul(k.psum[:, 2 * h + b, u * P:(u + 1) * P],
                                             node[:, ds(i * (2 * G) + (h * G + b * 4 + u), 1)].to_broadcast([P, P]),
                                             diag[:, :], start=False, stop=u == 3)
                    last.then_inc(s_bc[h], 1)

                def rank(i, h):
                    pe.wait_ge(s_less[h], i + 2)
                    pe.wait_ge(s_hot[h], i + 1)
                    for u in range(G):
                        last = pe.matmul(k.psum[:, 4 + h, u:u + 1], less[:, h, u, :], k.ones16[:, 0:1],
                                         start=True, stop=True)
                    last.then_inc(s_rank[h], 1)

                def move(i, h):
                    pe.wait_ge(s_hot[h], i + 2)
                    pe.wait_ge(s_out[h], i + 1)
                    for u in range(G):
                        last = pe.matmul(k.psum[:, 6 + h, 2 * u:2 * u + 2], hot[:, h, u, :],
                                         flat(k.pair[:, ds(i * (2 * G) + (h * G + u), 1), :]), start=True, stop=True)
                    last.then_inc(s_mv[h], 1)

                def position(i, h, first, last):
                    if not last:
                        broadcast(*near(i, h, 1))
                    rank(i, h)
                    if not first:
                        move(*near(i, h, -1))

                broadcast(0, 0)
                in_rounds(pe, position)
                move(R - 1, 1)

            @block.scalar
            def _(act):
                free(act, *s_out)
                with act.Fori(0, R) as i:
                    for h in range(2):
                        act.wait_ge(s_mv[h], i + 2)
                        act.nop(nofuse=True)
                        act.activation(flat(out[:, ds(i * (2 * G) + h * G, G), :]), k.psum[:, 6 + h, 0:2 * G],
                                       ACT.Copy).then_inc(s_out[h], 1)

        G2 = 16
        R2 = T // (2 * G2)
        s_tr, s_rows, s_flags, s_back, s_d2 = (sem(n) for n in ("s_tr", "s_rows", "s_flags", "s_back", "s_d2"))
        s_wide, s_oh, s_w = (pair_of(n) for n in ("s_wide", "s_oh", "s_w"))
        rows = sb("rows", [P, B, P], F32)
        first = sb("first", [P, B, P], F32)
        lastf = sb("lastf", [P, B, P], F32)
        ohb = sb("ohb", [P, 2, G2, P], BF16)
        with nc.Block() as block:
            @block.vector
            def _(dve):
                c = Chain(dve, s_d2)
                c.link(dve.tensor_copy(node[:, :], order.local[:, :]))
                dve.wait_ge(s_tr, B)
                for b in range(B):
                    last = dve.tensor_copy(rows[0:width[b], b, :], k.psum[0:width[b], b, 0:P])
                last.then_inc(s_rows, 1)
                dve.wait_ge(s_rows, 1)
                c.link(dve.memset(first[:, :, :], -BIG))
                c.link(dve.memset(lastf[:, :, :], 1.0))
                for b in range(B):
                    v = width[b]
                    c.link(dve.tensor_tensor(lastf[0:v, b, 0:P - 1], rows[0:v, b, 0:P - 1], rows[0:v, b, 1:P],
                                             ALU.not_equal))
                    c.link(dve.tensor_scalar(first[0:v, b, 1:P], lastf[0:v, b, 0:P - 1], -BIG, None, ALU.mult))
                dve.sem_inc(s_flags, 1)
                dve.wait_ge(s_back, 2 * B)
                for b in range(B):
                    v = width[b]
                    dve.tensor_copy(order.cut[:, b * P:b * P + v], k.psum[:, 4, b * P:b * P + v])
                    last = dve.tensor_copy(order.last[:, b * P:b * P + v], k.psum[:, 5, b * P:b * P + v])
                c.link(last)
                free(dve, *s_oh)
                with dve.Fori(0, R2) as i:
                    for h in range(2):
                        dve.wait_ge(s_wide[h], i + 1)
                        dve.wait_ge(s_w[h], i * 16 + 16)
                        dve.tensor_scalar(flat(ohb[:, h, :, :]), flat(k.psum[:, 4 * h:4 * h + 4, :]), k.iota_p[:, :],
                                          None, ALU.is_equal).then_inc(s_oh[h], 1)

            @block.tensor
            def _(pe):
                for b in range(B):
                    pe.transpose(k.psum[0:width[b], b, 0:P], order.local[:, b * P:b * P + width[b]],
                                 k.ident[:, :]).then_inc(s_tr, 1)
                pe.wait_ge(s_flags, 1)
                for b in range(B):
                    v = width[b]
                    pe.transpose(k.psum[:, 4, b * P:b * P + v], first[0:v, b, :], k.ident[0:v, 0:v]).then_inc(s_back, 1)
                    pe.transpose(k.psum[:, 5, b * P:b * P + v], lastf[0:v, b, :], k.ident[0:v, 0:v]).then_inc(s_back, 1)
                with pe.Fori(0, R2) as i:
                    for h in range(2):
                        pe.wait_ge(s_oh[h], i + 1)
                        for u in range(G2):
                            last = pe.matmul(k.psum[:, 4 * h + u // 4, (u % 4) * P:(u % 4 + 1) * P],
                                             node[:, ds(i * (2 * G2) + (h * G2 + u), 1)].to_broadcast([P, P]),
                                             ident16[:, :], start=True, stop=True)
                        last.then_inc(s_wide[h], 1)

            @block.sync
            def _(sp):
                free(sp, *s_w, by=16)
                with sp.Fori(0, R2) as i:
                    for h in range(2):
                        sp.wait_ge(s_oh[h], i + 2)
                        sp.dma_start(order.gather[:, ds(i * (2 * G2 * P) + h * (G2 * P), G2 * P)],
                                     flat(ohb[:, h, :, :])).then_inc(s_w[h], 16)
                for h in range(2):
                    sp.wait_ge(s_w[h], R2 * 16 + 16)


class Kit:

    def __init__(self, nc, ctx, s):
        self.s = s

        def sb(n, shape, dt):
            return ctx.enter_context(nc.sbuf_tensor(n, shape, dt))

        self.sb = sb
        self.iota = sb("iota", [P, P], F32)
        self.iota16 = sb("iota16", [P, s.T], F16)
        self.iota_p = sb("iota_p", [P, 1], F32)
        self.ident = sb("ident", [P, P], F32)
        self.upto = sb("upto", [P, P], F16)
        self.ones16 = sb("ones16", [P, P], F16)
        self.zeros16 = sb("zeros16", [P, P], F16)
        self.ones = sb("ones", [P, P], F32)
        self.psum = ctx.enter_context(nc.psum_tensor("psum", [P, 8, 512], F32))
        self.s_got = [ctx.enter_context(nc.semaphore(f"s_got{q}")) for q in range(4)]
        self.got = 0
        self.s_iota = ctx.enter_context(nc.semaphore("s_iota"))
        self.s_const = ctx.enter_context(nc.semaphore("s_const"))


def banked(nc, k, name, chunks, produce, take):
    with ExitStack() as ctx:
        s_full = ctx.enter_context(signal(nc, f"{name}_full"))
        s_taken = [ctx.enter_context(signal(nc, f"{name}_taken{i}")) for i in range(2)]
        with nc.Block() as block:
            @block.tensor
            def _(pe):
                for c in range(chunks):
                    if c >= 8:
                        pe.wait_ge(s_taken[c % 2], (c - 8) // 2 + 1)
                    produce(pe, c, c % 8).then_inc(s_full, 1)

            @block.scalar
            def _(act):
                for c in range(0, chunks, 2):
                    act.wait_ge(s_full, c + 1)
                    take(lambda dst, src: act.activation(dst, src, ACT.Copy), c, c % 8).then_inc(s_taken[0], 1)

            @block.vector
            def _(dve):
                for c in range(1, chunks, 2):
                    dve.wait_ge(s_full, c + 1)
                    take(lambda dst, src: dve.tensor_copy(dst, src), c, c % 8).then_inc(s_taken[1], 1)


def chunked(n, size):
    return [(a, min(size, n - a)) for a in range(0, n, size)]


def transpose_all(nc, k, name, src, dst):
    parts = chunked(k.s.NT, 4)

    def produce(pe, c, bank):
        a, n = parts[c]
        for j in range(n):
            last = pe.transpose(k.psum[:, bank, j * P:(j + 1) * P], src[:, a + j, :], k.ident[:, :])
        return last

    def take(copy, c, bank):
        a, n = parts[c]
        return copy(dst[:, a * P:(a + n) * P], k.psum[:, bank, 0:n * P])

    banked(nc, k, name, len(parts), produce, take)


def untranspose_all(nc, k, name, src, dst):
    parts = chunked(k.s.NT, 4)

    def produce(pe, c, bank):
        a, n = parts[c]
        for j in range(n):
            last = pe.transpose(k.psum[:, bank, j * P:(j + 1) * P], src[:, (a + j) * P:(a + j + 1) * P],
                                k.ident[:, :])
        return last

    def take(copy, c, bank):
        a, n = parts[c]
        return copy(flat(dst[:, a:a + n, :]), k.psum[:, bank, 0:n * P])

    banked(nc, k, name, len(parts), produce, take)


def linear(nc, k, name, xs, ws, width, dst):
    per = 512 // width
    parts = chunked(k.s.NT, per)

    def produce(pe, c, bank):
        a, n = parts[c]
        for j in range(n):
            for q, (x, w) in enumerate(zip(xs, ws)):
                last = pe.matmul(k.psum[:, bank, j * width:(j + 1) * width], x[:, (a + j) * P:(a + j + 1) * P],
                                 w, start=q == 0, stop=q == len(xs) - 1)
        return last

    def take(copy, c, bank):
        a, n = parts[c]
        return copy(dst(a, n), k.psum[:, bank, 0:n * width].rearrange("p (a b) -> p a b", b=width))

    banked(nc, k, name, len(parts), produce, take)


def typed_linear(nc, k, name, x_t, w_d, out, silu=False):
    s = k.s
    types = w_d.shape[0]
    parts = chunked(s.NP, 512)
    with ExitStack() as ctx:
        w = ctx.enter_context(nc.sbuf_tensor(f"{name}_w", [P, types, D], F32))
        xm = ctx.enter_context(nc.sbuf_tensor(f"{name}_xm", [P, 2, s.NP], F32))
        s_w = ctx.enter_context(signal(nc, f"{name}_s_w"))
        s_xm = ctx.enter_context(signal(nc, f"{name}_s_xm"))
        s_mm = ctx.enter_context(signal(nc, f"{name}_s_mm"))
        s_sig = ctx.enter_context(signal(nc, f"{name}_s_sig"))
        acc = k.psum[:, :, :].rearrange("p a b -> p (a b)")[:, 0:s.NP]
        with nc.Block() as block:
            @block.sync
            def _(sp):
                sp.dma_start(w[:, :, :], w_d.rearrange("t i o -> i t o")).then_inc(s_w, 16)

            @block.vector
            def _(dve):
                for t in range(types):
                    if t >= 2:
                        dve.wait_ge(s_mm, t - 1)
                    dve.scalar_tensor_tensor(xm[:, t % 2, :], k.type_row[:, :], float(t), x_t[:, :],
                                             ALU.is_equal, ALU.mult).then_inc(s_xm, 1)
                if silu:
                    dve.wait_ge(s_sig, 1)
                    dve.tensor_tensor(out[:, :], xm[:, 0, :], acc, ALU.mult)

            @block.tensor
            def _(pe):
                pe.wait_ge(s_w, 16)
                for t in range(types):
                    pe.wait_ge(s_xm, t + 1)
                    for c, (a, n) in enumerate(parts):
                        last = pe.matmul(k.psum[:, c, 0:n], w[:, t, :], xm[:, t % 2, a:a + n],
                                         start=t == 0, stop=t == types - 1)
                    last.then_inc(s_mm, 1)

            @block.scalar
            def _(act):
                act.wait_ge(s_mm, types)
                if silu:
                    act.activation(xm[:, 0, :], acc, ACT.Sigmoid).then_inc(s_sig, 1)
                else:
                    act.activation(out[:, :], acc, ACT.Copy)


def layer_norm(nc, k, name, x, gain=None, shift=None):
    s = k.s
    NT = s.NT
    with ExitStack() as ctx:
        sq = ctx.enter_context(nc.sbuf_tensor(f"{name}_sq", [P, NT, D], F32))
        m = ctx.enter_context(nc.sbuf_tensor(f"{name}_m", [P, NT], F32))
        v = ctx.enter_context(nc.sbuf_tensor(f"{name}_v", [P, NT], F32))
        r = ctx.enter_context(nc.sbuf_tensor(f"{name}_r", [P, NT], F32))
        s_d = ctx.enter_context(signal(nc, f"{name}_s_d"))
        s_x = ctx.enter_context(signal(nc, f"{name}_s_x"))
        s_a = ctx.enter_context(signal(nc, f"{name}_s_a"))
        with nc.Block() as block:
            @block.vector
            def _(dve):
                c = Chain(dve, s_d)
                c.link(dve.tensor_reduce(m[:, :], x[:, :, :], AX.X, ALU.add))
                c.link(dve.tensor_scalar(m[:, :], m[:, :], 1.0 / D, None, ALU.mult))
                dve.tensor_tensor(x[:, :, :], x[:, :, :], over_last(m[:, :], D), ALU.subtract).then_inc(s_x, 1)
                dve.wait_ge(s_a, 1)
                c.link(dve.tensor_reduce(v[:, :], sq[:, :, :], AX.X, ALU.add))
                dve.tensor_scalar(v[:, :], v[:, :], 1.0 / D, LN_EPS, ALU.mult, ALU.add).then_inc(s_x, 1)
                dve.wait_ge(s_a, 2)
                c.link(dve.reciprocal(r[:, :], r[:, :]))
                c.link(dve.tensor_tensor(x[:, :, :], x[:, :, :], over_last(r[:, :], D), ALU.mult))
                if gain is not None:
                    c.link(dve.tensor_tensor(x[:, :, :], x[:, :, :], over_mid(gain, NT), ALU.mult))
                    c.link(dve.tensor_tensor(x[:, :, :], x[:, :, :], over_mid(shift, NT), ALU.add))

            @block.scalar
            def _(act):
                act.wait_ge(s_x, 1)
                act.activation(sq[:, :, :], x[:, :, :], ACT.Square).then_inc(s_a, 1)
                act.wait_ge(s_x, 2)
                act.activation(r[:, :], v[:, :], ACT.Sqrt).then_inc(s_a, 1)


GRP = 4
RND = 4


def tile_registers(eng, n, name):
    return [eng.alloc_register(f"{name}{u}") for u in range(n)]


def load_tiles(eng, order, regs, t0, tiles):
    eng.load(regs, order.tile[0:1, ds(t0, len(regs))])
    return [eng.snap(r, min_val=0, max_val=tiles - 1) for r in regs]


def back(i, q, lag):
    return (i, q - lag) if q >= lag else (i - 1, q - lag + RND)


def score_rows(nc, k, name, order, rows, table, width, score, stash, heads, queries, scores, peaks):
    s = k.s
    NT = s.NT
    rounds = s.T // (GRP * RND)
    qw = D if score == "dot" else heads
    lo, hi = stash
    TG = GRP * RND
    W1 = heads + 1
    lanes_of_rows = TG * heads
    AHEAD = 2
    LANES = 4
    with ExitStack() as ctx:
        def sb(n, shape, dt):
            return ctx.enter_context(nc.sbuf_tensor(f"{name}_{n}", shape, dt))

        def sem(n):
            return ctx.enter_context(signal(nc, f"{name}_{n}"))

        def sems(n):
            return [sem(f"{n}{q}") for q in range(RND)]

        got = sb("got", [P, RND, GRP, width], F32)
        idx = sb("idx", [P, RND, GRP], I32)
        hot_t = sb("hot_t", [P, RND, GRP * P], BF16)
        prod = sb("prod", [P, 2, GRP * qw], F32)
        hot = sb("hot", [P, TG, P], F32)
        cut = sb("cut", [P, lanes_of_rows], F32)
        stat = sb("stat", [P, lanes_of_rows], F32)
        cut_t = sb("cut_t", [lanes_of_rows, P], F32)
        run = sb("run", [lanes_of_rows, P], F32)
        tail = sb("tail", [P, TG, W1], F32)
        gone = sb("gone", [P, TG], F32)
        best = sb("best", [P, TG, heads], F32)
        lane = sb("lane", [P, LANES, NT * heads], F32)
        s_idx, s_hot, s_q, s_used, s_stash = (sems(n) for n in ("s_idx", "s_hot", "s_q", "s_used", "s_stash"))
        s_d, s_scored, s_tr, s_pre, s_cut, s_run, s_back, s_tail, s_mv, s_best = (sem(n) for n in (
            "s_d", "s_scored", "s_tr", "s_pre", "s_cut", "s_run", "s_back", "s_tail", "s_mv", "s_best"))
        s_got, had = k.s_got, k.got
        k.got += rounds * 16 * GRP
        with nc.Block() as block:
            @block.scalar
            def _(act):
                def indices(i, q):
                    act.wait_ge(s_used[q], i + 1)
                    act.activation(idx[:, q, :], rows[:, ds((i * RND + q) * GRP, GRP)], ACT.Copy).then_inc(s_idx[q], 1)

                def columns(i):
                    act.wait_ge(s_scored, i + 1)
                    act.wait_ge(s_tr, i + 1)
                    act.nop(nofuse=True)
                    act.activation(cut[:, :].rearrange("p (a b) -> p a b", b=heads),
                                   over_last(order.cut[:, ds(i * TG, TG)], heads), ACT.Copy)
                    act.activation(stat[:, :], scores[:, ds(i * lanes_of_rows, lanes_of_rows)],
                                   ACT.Copy).then_inc(s_pre, 1)

                def cuts(i):
                    act.wait_ge(s_tr, i + 2)
                    act.wait_ge(s_run, i + 1)
                    act.activation(cut_t[:, :], k.psum[0:lanes_of_rows, 4, 0:P], ACT.Copy).then_inc(s_cut, 1)

                for q in range(RND):
                    indices(0, q)
                with act.Fori(1, rounds) as i:
                    for q in range(RND - 1):
                        indices(i, q)
                    columns(i - 1)
                    indices(i, RND - 1)
                    cuts(i - 1)
                columns(rounds - 1)
                cuts(rounds - 1)

            @block.gpsimd
            def _(pool):
                with pool.Fori(0, rounds) as i:
                    for q in range(RND):
                        pool.wait_ge(s_idx[q], i + 1)
                        pool.wait_ge(s_used[q], i + 1)
                        pool.wait_ge(s_stash[q], i * 16 + 16)
                        pool.nop(nofuse=True)
                        for u in range(GRP):
                            pool.indirect_dma_start(
                                got[:, q, u, :], None, table[:, :],
                                bass.IndirectOffsetOnAxis(ap=idx[:, q, u:u + 1], axis=0)).then_inc(s_got[q], 16)

            @block.sync
            def _(sp):
                free(sp, *s_stash, by=16)

                def one_hots(i, q):
                    sp.wait_ge(s_q[q], i + 1)
                    sp.dma_start(hot_t[:, q, :], order.gather[:, ds((i * RND + q) * (GRP * P), GRP * P)])\
                        .then_inc(s_hot[q], 16)

                def put_away(i, q):
                    sp.wait_ge(s_got[q], i * (16 * GRP) + (had + 16 * GRP))
                    sp.dma_start(k.stash[:, ds((i * RND + q) * GRP, GRP), 0:hi - lo], got[:, q, :, lo:hi])\
                        .then_inc(s_stash[q], 16)

                for q in range(RND):
                    one_hots(0, q)
                with sp.Fori(0, rounds - 1) as i:
                    for q in range(RND):
                        put_away(i, q)
                        one_hots(i + 1, q)
                for q in range(RND):
                    put_away(rounds - 1, q)
                for q in range(RND):
                    sp.wait_ge(s_stash[q], rounds * 16 + 16)

            @block.tensor
            def _(pe):
                free(pe, *s_q, s_tr)
                regs = tile_registers(pe, TG, f"{name}_pe")

                def query(i, q, tiles):
                    pe.wait_ge(s_hot[q], i * 16 + 16)
                    pe.wait_ge(s_used[q], i + 1)
                    for u in range(GRP):
                        for part in range(3):
                            last = pe.matmul(k.psum[:, q, u * qw:(u + 1) * qw], hot_t[:, q, u * P:(u + 1) * P],
                                             queries[:, part, ds(tiles[u] * qw, qw)],
                                             start=part == 0, stop=part == 2)
                    last.then_inc(s_q[q], 1)

                def to_rows(i):
                    pe.wait_ge(s_pre, i + 1)
                    pe.wait_ge(s_run, i + 1)
                    pe.nop(nofuse=True)
                    pe.transpose(k.psum[0:lanes_of_rows, 4, 0:P], cut[:, :], k.ident[:, :])
                    pe.transpose(k.psum[0:lanes_of_rows, 5, 0:P], stat[:, :], k.ident[:, :]).then_inc(s_tr, 1)

                def to_columns(i):
                    pe.wait_ge(s_run, i + 2)
                    pe.nop(nofuse=True)
                    pe.transpose(k.psum[:, 6, 0:lanes_of_rows], run[:, :],
                                 k.ident[0:lanes_of_rows, 0:lanes_of_rows]).then_inc(s_back, 1)

                def to_nodes(i):
                    pe.wait_ge(s_tail, i + 1)
                    pe.wait_ge(s_best, i * TG + 1)
                    for u in range(TG):
                        last = pe.matmul(k.psum[:, 7, u * W1:(u + 1) * W1], hot[:, u, :], tail[:, u, :],
                                         start=True, stop=True)
                    last.then_inc(s_mv, 1)

                def ahead(i, q, node_tile):
                    r, p = (i, q + AHEAD) if q + AHEAD < RND else (i + 1, q + AHEAD - RND)
                    query(r, p, node_tile[q * GRP:(q + 1) * GRP])

                maxima = (to_rows, to_columns, to_nodes)
                node_tile = load_tiles(pe, order, regs[0:AHEAD * GRP], 0, NT)
                for q in range(AHEAD):
                    query(0, q, node_tile[q * GRP:(q + 1) * GRP])
                node_tile = load_tiles(pe, order, regs, AHEAD * GRP, NT)
                for q in range(RND):
                    ahead(0, q, node_tile)
                with pe.Fori(1, rounds - 1) as i:
                    node_tile = load_tiles(pe, order, regs, i * TG + AHEAD * GRP, NT)
                    for q in range(RND):
                        ahead(i, q, node_tile)
                        if q < len(maxima):
                            maxima[q](i - 1)
                left = RND - AHEAD
                node_tile = load_tiles(pe, order, regs[0:left * GRP], (rounds - 1) * TG + AHEAD * GRP, NT)
                for q in range(len(maxima)):
                    if q < left:
                        ahead(rounds - 1, q, node_tile)
                    maxima[q](rounds - 2)
                for step in maxima:
                    step(rounds - 1)

            @block.vector
            def _(dve):
                c = Chain(dve, s_d)
                for v in range(LANES):
                    c.link(dve.tensor_copy(lane[:, v, :], flat(peaks[:, :, :])))
                free(dve, *s_used, s_run, s_best)
                regs = tile_registers(dve, TG, f"{name}_dve")

                def scored(i, q):
                    dve.wait_ge(s_got[q], i * (16 * GRP) + (had + 16 * GRP))
                    dve.wait_ge(s_q[q], i + 2)
                    at = scores[:, ds((i * RND + q) * (GRP * heads), GRP * heads)]
                    ps = k.psum[:, q, 0:GRP * qw]
                    pr = prod[:, q % 2, :]
                    if score == "dot":
                        dve.tensor_tensor(pr.rearrange("p (a b) -> p a b", a=GRP), got[:, q, :, 0:D],
                                          ps.rearrange("p (a b) -> p a b", a=GRP), ALU.mult).then_inc(s_used[q], 1)
                        dve.wait_ge(s_used[q], i + 2)
                        last = dve.tensor_reduce(at, pr.rearrange("p (a b) -> p a b", b=D // heads), AX.X, ALU.add)
                    else:
                        dve.tensor_tensor(pr.rearrange("p (a b) -> p a b", a=GRP), got[:, q, :, width - heads:width],
                                          ps.rearrange("p (a b) -> p a b", a=GRP), ALU.add).then_inc(s_used[q], 1)
                        dve.wait_ge(s_used[q], i + 2)
                        last = dve.scalar_tensor_tensor(at, pr, NEG_SLOPE, pr, ALU.mult, ALU.max)
                    if q == RND - 1:
                        last.then_inc(s_scored, 1)
                        dve.wait_ge(s_scored, i + 1)
                    else:
                        c.link(last)

                def spread(i):
                    c.link(dve.tensor_tensor(hot[:, :, :], over_mid(k.iota[:, :], TG),
                                             over_last(order.local[:, ds(i * TG, TG)], P), ALU.is_equal))

                def scan(i):
                    dve.wait_ge(s_tr, i + 2)
                    dve.wait_ge(s_cut, i + 1)
                    dve.tensor_tensor_scan(run[:, :], cut_t[:, :], k.psum[0:lanes_of_rows, 5, 0:P], -BIG,
                                           ALU.add, ALU.max).then_inc(s_run, 1)

                def tails(i):
                    g = ds(i * TG, TG)
                    dve.wait_ge(s_back, i + 1)
                    dve.tensor_tensor(tail[:, :, 0:heads],
                                      k.psum[:, 6, 0:lanes_of_rows].rearrange("p (a b) -> p a b", b=heads),
                                      over_last(order.last[:, g], heads), ALU.mult)
                    c.link(dve.tensor_scalar(tail[:, :, heads:W1], order.last[:, g].unsqueeze(2), 1.0, None, ALU.mult))
                    dve.sem_inc(s_tail, 1)

                def raise_peaks(i, node_tile):
                    dve.wait_ge(s_mv, i + 1)
                    moved = k.psum[:, 7, 0:TG * W1].rearrange("p (a b) -> p a b", b=W1)
                    c.link(dve.tensor_scalar(gone[:, :].unsqueeze(2), moved[:, :, heads:W1], -1.0, BIG, ALU.add, ALU.mult))
                    c.link(dve.tensor_tensor(best[:, :, :], moved[:, :, 0:heads], over_last(gone[:, :], heads), ALU.add))
                    for u in range(TG):
                        at = lane[:, u % LANES, ds(node_tile[u] * heads, heads)]
                        dve.wait_ge(s_best, i * TG + (u - LANES + 2 if u >= LANES else 1))
                        dve.tensor_tensor(at, at, best[:, u, :], ALU.max).then_inc(s_best, 1)
                    dve.wait_ge(s_best, i * TG + (TG + 1))

                for q in range(RND):
                    scored(0, q)
                scored(1, 0)
                spread(0)
                scored(1, 1)
                scan(0)
                scored(1, 2)
                tails(0)
                scored(1, 3)
                with dve.Fori(2, rounds) as i:
                    c.enter(i - 2, RND + 3)
                    node_tile = load_tiles(dve, order, regs, (i - 2) * TG, NT)
                    scored(i, 0)
                    raise_peaks(i - 2, node_tile)
                    scored(i, 1)
                    scan(i - 1)
                    spread(i - 1)
                    scored(i, 2)
                    tails(i - 1)
                    scored(i, 3)
                c.leave(rounds - 2)
                raise_peaks(rounds - 2, load_tiles(dve, order, regs, (rounds - 2) * TG, NT))
                spread(rounds - 1)
                scan(rounds - 1)
                tails(rounds - 1)
                raise_peaks(rounds - 1, load_tiles(dve, order, regs, (rounds - 1) * TG, NT))
                c.link(dve.tensor_tensor(lane[:, 0:2, :], lane[:, 0:2, :], lane[:, 2:4, :], ALU.max))
                c.link(dve.tensor_tensor(flat(peaks[:, :, :]), lane[:, 0, :], lane[:, 1, :], ALU.max))


def weigh_rows(nc, k, name, order, heads, features, scores, peaks3, acc):
    s = k.s
    NT = s.NT
    TG = GRP * RND
    rounds = s.T // TG
    F, FW = features, features + heads
    with ExitStack() as ctx:
        def sb(n, shape, dt):
            return ctx.enter_context(nc.sbuf_tensor(f"{name}_{n}", shape, dt))

        def sems(n, m=RND):
            return [ctx.enter_context(signal(nc, f"{name}_{n}{q}")) for q in range(m)]

        hot_t = sb("hot_t", [P, RND, GRP * P], BF16)
        msg = sb("msg", [P, RND, GRP, F], F32)
        hot = sb("hot", [P, RND, GRP, P], F32)
        diff = sb("diff", [P, RND, GRP * heads], F32)
        wtd = sb("wtd", [P, RND, GRP, FW], F32)
        s_in, s_msg, s_pk, s_diff, s_exp, s_wtd, s_hot = (sems(n) for n in (
            "s_in", "s_msg", "s_pk", "s_diff", "s_exp", "s_wtd", "s_hot"))
        s_sum = sems("s_sum", GRP)
        s_acc = sems("s_acc", GRP)
        WEIGH, SCATTER, ADD = 1, 2, 3
        with nc.Block() as block:
            @block.sync
            def _(sp):
                with sp.Fori(0, rounds) as i:
                    for q in range(RND):
                        g0 = (i * RND + q) * GRP
                        sp.wait_ge(s_pk[q], i + 1)
                        sp.dma_start(hot_t[:, q, :], order.gather[:, ds(g0 * P, GRP * P)]).then_inc(s_in[q], 16)
                        sp.wait_ge(s_wtd[q], i + 1)
                        sp.dma_start(msg[:, q, :, :], k.stash[:, ds(g0, GRP), 0:F]).then_inc(s_msg[q], 16)

            @block.tensor
            def _(pe):
                free(pe, *s_pk)
                free(pe, *s_sum, by=RND)
                regs = tile_registers(pe, TG, f"{name}_pe")

                def peak(i, q, node_tile):
                    pe.wait_ge(s_in[q], i * 16 + 16)
                    pe.wait_ge(s_diff[q], i + 1)
                    for u in range(GRP):
                        for part in range(3):
                            last = pe.matmul(k.psum[:, q, u * heads:(u + 1) * heads], hot_t[:, q, u * P:(u + 1) * P],
                                             peaks3[:, part, ds(node_tile[q * GRP + u] * heads, heads)],
                                             start=part == 0, stop=part == 2)
                    last.then_inc(s_pk[q], 1)

                def scatter(i, q):
                    pe.wait_ge(s_wtd[q], i + 2)
                    pe.wait_ge(s_hot[q], i + 1)
                    for u in range(GRP):
                        pe.wait_ge(s_acc[u], i * RND + (q + 1))
                        pe.matmul(k.psum[:, 4 + u, 0:FW], hot[:, q, u, :], wtd[:, q, u, :],
                                  start=True, stop=True).then_inc(s_sum[u], 1)

                node_tile = load_tiles(pe, order, regs, 0, NT)
                for q in range(RND):
                    peak(0, q, node_tile)
                    if q >= SCATTER:
                        scatter(0, q - SCATTER)
                with pe.Fori(1, rounds) as i:
                    node_tile = load_tiles(pe, order, regs, i * TG, NT)
                    for q in range(RND):
                        peak(i, q, node_tile)
                        scatter(*back(i, q, SCATTER))
                for q in range(SCATTER):
                    scatter(*back(rounds, q, SCATTER))

            @block.scalar
            def _(act):
                free(act, *s_exp)
                with act.Fori(0, rounds) as i:
                    for q in range(RND):
                        act.wait_ge(s_diff[q], i + 2)
                        act.wait_ge(s_sum[GRP - 1], i * RND + (q + 1))
                        act.activation(wtd[:, q, :, F:FW], diff[:, q, :].rearrange("p (a b) -> p a b", a=GRP),
                                       ACT.Exp).then_inc(s_exp[q], 1)

            @block.vector
            def _(dve):
                free(dve, *s_diff, *s_wtd, *s_acc)
                regs = tile_registers(dve, TG, f"{name}_dve")

                def spread(i, q):
                    dve.wait_ge(s_sum[GRP - 1], i * RND + (q + 1))
                    dve.tensor_tensor(hot[:, q, :, :], over_mid(k.iota[:, :], GRP),
                                      over_last(order.local[:, ds((i * RND + q) * GRP, GRP)], P),
                                      ALU.is_equal).then_inc(s_hot[q], 1)

                def subtract(i, q):
                    dve.wait_ge(s_pk[q], i + 2)
                    dve.wait_ge(s_exp[q], i + 1)
                    dve.tensor_tensor(diff[:, q, :], scores[:, ds((i * RND + q) * (GRP * heads), GRP * heads)],
                                      k.psum[:, q, 0:GRP * heads], ALU.subtract).then_inc(s_diff[q], 1)

                def weigh(i, q):
                    dve.wait_ge(s_exp[q], i + 2)
                    dve.wait_ge(s_msg[q], i * 16 + 16)
                    dve.tensor_tensor(
                        wtd[:, q, :, 0:F].rearrange("p g (a b) -> p g a b", a=heads),
                        msg[:, q, :, :].rearrange("p g (a b) -> p g a b", a=heads),
                        wtd[:, q, :, F:FW].unsqueeze(3).to_broadcast([P, GRP, heads, F // heads]),
                        ALU.mult).then_inc(s_wtd[q], 1)

                def add(i, q, node_tile):
                    for u in range(GRP):
                        at = acc[:, u % 2, ds(node_tile[u] * FW, FW)]
                        dve.wait_ge(s_sum[u], i * RND + (q + RND + 1))
                        dve.wait_ge(s_acc[(u - 2) % GRP], i * RND + (q + 1 if u < 2 else q + 2))
                        dve.tensor_tensor(at, at, k.psum[:, 4 + u, 0:FW], ALU.add).then_inc(s_acc[u], 1)

                for q in range(RND):
                    spread(0, q)
                    if q >= ADD:
                        add(0, q - ADD, load_tiles(dve, order, regs[0:GRP], (q - ADD) * GRP, NT))
                    subtract(0, q)
                    if q >= WEIGH:
                        weigh(0, q - WEIGH)
                with dve.Fori(1, rounds) as i:
                    node_tile = load_tiles(dve, order, regs, i * TG - ADD * GRP, NT)
                    for q in range(RND):
                        spread(i, q)
                        add(*back(i, q, ADD), node_tile[q * GRP:(q + 1) * GRP])
                        subtract(i, q)
                        weigh(*back(i, q, WEIGH))
                node_tile = load_tiles(dve, order, regs[0:ADD * GRP], (rounds * RND - ADD) * GRP, NT)
                for q in range(ADD):
                    add(*back(rounds, q, ADD), node_tile[q * GRP:(q + 1) * GRP])
                    if q < WEIGH:
                        weigh(*back(rounds, q, WEIGH))


def gather_sum(nc, k, name, order, rows, table, width, acc):
    s = k.s
    rounds = s.T // (GRP * RND)
    with ExitStack() as ctx:
        def sb(n, shape, dt):
            return ctx.enter_context(nc.sbuf_tensor(f"{name}_{n}", shape, dt))

        def sems(n, m=RND):
            return [ctx.enter_context(signal(nc, f"{name}_{n}{q}")) for q in range(m)]

        got = sb("got", [P, RND, GRP, width], F32)
        idx = sb("idx", [P, RND, GRP], I32)
        hot = sb("hot", [P, RND, GRP, P], F32)
        s_idx, s_hot, s_used = (sems(n) for n in ("s_idx", "s_hot", "s_used"))
        s_got, had = k.s_got, k.got
        k.got += rounds * 16 * GRP
        s_acc = sems("s_acc", GRP)
        with nc.Block() as block:
            @block.scalar
            def _(act):
                with act.Fori(0, rounds) as i:
                    for q in range(RND):
                        act.wait_ge(s_used[q], i + 1)
                        act.activation(idx[:, q, :], rows[:, ds((i * RND + q) * GRP, GRP)],
                                       ACT.Copy).then_inc(s_idx[q], 1)

            @block.gpsimd
            def _(pool):
                with pool.Fori(0, rounds) as i:
                    for q in range(RND):
                        pool.wait_ge(s_idx[q], i + 1)
                        pool.wait_ge(s_used[q], i + 1)
                        pool.nop(nofuse=True)
                        for u in range(GRP):
                            pool.indirect_dma_start(
                                got[:, q, u, :], None, table[:, :],
                                bass.IndirectOffsetOnAxis(ap=idx[:, q, u:u + 1], axis=0)).then_inc(s_got[q], 16)

            @block.tensor
            def _(pe):
                free(pe, *s_used)
                with pe.Fori(0, rounds) as i:
                    for q in range(RND):
                        pe.wait_ge(s_got[q], i * (16 * GRP) + (had + 16 * GRP))
                        pe.wait_ge(s_hot[q], i + 1)
                        for u in range(GRP):
                            pe.wait_ge(s_acc[u], i * RND + (q + 1))
                            last = pe.matmul(k.psum[:, u, 0:width], hot[:, q, u, :], got[:, q, u, :],
                                             start=True, stop=True)
                        last.then_inc(s_used[q], 1)

            @block.vector
            def _(dve):
                free(dve, *s_acc)
                regs = tile_registers(dve, GRP * RND, f"{name}_dve")
                with dve.Fori(0, rounds) as i:
                    node_tile = load_tiles(dve, order, regs, i * (GRP * RND), s.NT)
                    for q in range(RND):
                        g0 = (i * RND + q) * GRP
                        dve.wait_ge(s_used[q], i + 1)
                        dve.tensor_tensor(hot[:, q, :, :], over_mid(k.iota[:, :], GRP),
                                          over_last(order.local[:, ds(g0, GRP)], P), ALU.is_equal).then_inc(s_hot[q], 1)
                    for q in range(RND):
                        for u in range(GRP):
                            at = acc[:, u % 2, ds(node_tile[q * GRP + u] * width, width)]
                            dve.wait_ge(s_used[q], i + 2)
                            dve.wait_ge(s_acc[(u - 2) % GRP], i * RND + (q + 1 if u < 2 else q + 2))
                            dve.tensor_tensor(at, at, k.psum[:, u, 0:width], ALU.add).then_inc(s_acc[u], 1)


NEG_SLOPE = 0.2


def load_rows(nc, k, name, pairs):
    with ExitStack() as ctx:
        s_in = ctx.enter_context(signal(nc, f"{name}_s_in"))
        with nc.Block() as block:
            @block.sync
            def _(sp):
                for dst, src in pairs:
                    sp.dma_start(dst, src).then_inc(s_in, 16)
                sp.wait_ge(s_in, 16 * len(pairs))


def row_bcast(vec):
    return vec.unsqueeze(0).to_broadcast([P, vec.shape[0]])


def steps(nc, name, body):
    with ExitStack() as ctx:
        s_d = ctx.enter_context(signal(nc, f"{name}_s_d"))
        with nc.Block() as block:
            @block.vector
            def _(dve):
                body(Chain(dve, s_d).link, dve)


def relation_weights(nc, k, name, w_d, pri_d, out, pri):
    heads, rels, hs = w_d.shape[0], w_d.shape[1], w_d.shape[2]
    with ExitStack() as ctx:
        s_z = ctx.enter_context(signal(nc, f"{name}_s_z"))
        s_in = ctx.enter_context(signal(nc, f"{name}_s_in"))
        s_d = ctx.enter_context(signal(nc, f"{name}_s_d"))
        n_in = 16 * heads * (2 if pri is not None else 1)
        with nc.Block() as block:
            @block.vector
            def _(dve):
                dve.memset(out[:, :, :], 0.0).then_inc(s_z, 1)
                if pri is not None:
                    c = Chain(dve, s_d)
                    dve.wait_ge(s_in, n_in)
                    c.link(dve.tensor_scalar(pri[:, :], pri[:, :], 1.0 / float(np.sqrt(hs)), None, ALU.mult))
                    c.link(dve.tensor_tensor(out[:, :, :], out[:, :, :], over_last(pri[:, :], D), ALU.mult))

            @block.sync
            def _(sp):
                sp.wait_ge(s_z, 1)
                for h in range(heads):
                    at = slice(h * hs, (h + 1) * hs)
                    sp.dma_start(out[at, :, at], w_d[h].rearrange("r i o -> i r o")).then_inc(s_in, 16)
                    if pri is not None:
                        sp.dma_start(pri[at, :], pri_d[h].unsqueeze(0).to_broadcast([hs, rels])).then_inc(s_in, 16)
                sp.wait_ge(s_in, n_in)


def relation_table(nc, k, name, k_t, v_t, wk, wv, table):
    s = k.s
    rels = wk.shape[1]
    half = rels // 2
    rows = table.rearrange("(n r) c -> n r c", r=rels)
    with ExitStack() as ctx:
        out = ctx.enter_context(nc.sbuf_tensor(f"{name}_out", [P, 2, rels, 2 * D], F32))
        s_mm = ctx.enter_context(signal(nc, f"{name}_s_mm"))
        s_a = ctx.enter_context(signal(nc, f"{name}_s_a"))
        s_v = ctx.enter_context(signal(nc, f"{name}_s_v"))
        s_st = [ctx.enter_context(signal(nc, f"{name}_s_st{i}")) for i in range(2)]
        with nc.Block() as block:
            @block.tensor
            def _(pe):
                for j in range(s.NT):
                    if j >= 2:
                        pe.wait_ge(s_a, j - 1)
                        pe.wait_ge(s_v, j - 1)
                    for b in range(4):
                        x, w = ((k_t, wk), (v_t, wv))[b // 2]
                        last = pe.matmul(k.psum[:, 4 * (j % 2) + b, :], x[:, j * P:(j + 1) * P],
                                         flat(w[:, (b % 2) * half:(b % 2 + 1) * half, :]), start=True, stop=True)
                    last.then_inc(s_mm, 1)

            def empty(eng, j, side, copy):
                eng.wait_ge(s_mm, j + 1)
                if j >= 2:
                    eng.wait_ge(s_st[j % 2], 16 * (j // 2))
                b0 = 4 * (j % 2) + 2 * side
                return copy(out[:, j % 2, :, side * D:(side + 1) * D],
                            k.psum[:, b0:b0 + 2, :].rearrange("p a (r c) -> p (a r) c", c=D))

            @block.scalar
            def _(act):
                for j in range(s.NT):
                    empty(act, j, 0, lambda d, x: act.activation(d, x, ACT.Copy)).then_inc(s_a, 1)

            @block.vector
            def _(dve):
                for j in range(s.NT):
                    empty(dve, j, 1, lambda d, x: dve.tensor_copy(d, x)).then_inc(s_v, 1)

            @block.sync
            def _(sp):
                for j in range(s.NT):
                    sp.wait_ge(s_a, j + 1)
                    sp.wait_ge(s_v, j + 1)
                    sp.dma_start(rows[j * P:(j + 1) * P, :, :], out[:, j % 2, :, :]).then_inc(s_st[j % 2], 16)
                sp.wait_ge(s_st[0], 16 * ((s.NT + 1) // 2))
                sp.wait_ge(s_st[1], 16 * (s.NT // 2))


def store_table(nc, k, name, src, table):
    load_rows(nc, k, name, [(table.rearrange("(t p) c -> p t c", p=P), src)])


def graph_transformer(nc, k, l, X, order, W, table):
    s = k.s
    NT, NP = s.NT, s.NP
    heads, rels = W["pri"].shape[1], W["pri"].shape[2]
    FW = D + heads
    n = f"g{l}"
    with ExitStack() as outer:
        def sb(nm, shape, dt, where=outer):
            return where.enter_context(nc.sbuf_tensor(f"{n}_{nm}", shape, dt))

        scores = sb("scores", [P, s.T * heads], F32)
        peaks = sb("peaks", [P, NT, heads], F32)
        with ExitStack() as ctx:
            q3 = sb("q3", [P, 3, NP], BF16, ctx)
            with ExitStack() as c2:
                x_t = sb("x_t", [P, NP], F32, c2)
                k_t = sb("k_t", [P, NP], F32, c2)
                v_t = sb("v_t", [P, NP], F32, c2)
                transpose_all(nc, k, f"{n}_xt", X, x_t)
                typed_linear(nc, k, f"{n}_k", x_t, W["Wk"][l], k_t)
                typed_linear(nc, k, f"{n}_v", x_t, W["Wv"][l], v_t)
                with ExitStack() as c3:
                    wk = sb("wk", [P, rels, D], F32, c3)
                    wv = sb("wv", [P, rels, D], F32, c3)
                    pri = sb("pri", [P, rels], F32, c3)
                    relation_weights(nc, k, f"{n}_wk", W["Watt"][l], W["pri"][l], wk, pri)
                    relation_weights(nc, k, f"{n}_wv", W["Wmsg"][l], None, wv, None)
                    relation_table(nc, k, f"{n}_tab", k_t, v_t, wk, wv, table)
                typed_linear(nc, k, f"{n}_q", x_t, W["Wq"][l], k_t)
                q = v_t[:, :].rearrange("p (a b) -> p a b", b=D)
                untranspose_all(nc, k, f"{n}_qn", k_t, q)
                steps(nc, f"{n}_q3", lambda link, dve: split3_steps(link, dve, v_t[:, :], [q3[:, j, :] for j in range(3)], k_t[:, :]))
            steps(nc, f"{n}_pk", lambda link, dve: link(dve.memset(peaks[:, :, :], -BIG)))
            score_rows(nc, k, f"{n}_e1", order, order.row, table, 2 * D, "dot", (D, 2 * D), heads, q3, scores, peaks)
        acc = sb("acc", [P, 2, NT * FW], F32)
        with ExitStack() as ctx:
            peaks3 = sb("peaks3", [P, 3, NT * heads], BF16, ctx)
            rest = sb("rest", [P, NT * heads], F32, ctx)

            def prepare(link, dve):
                split3_steps(link, dve, flat(peaks[:, :, :]), [peaks3[:, j, :] for j in range(3)], rest[:, :])
                link(dve.memset(acc[:, :, :], 0.0))
            steps(nc, f"{n}_pre", prepare)
            weigh_rows(nc, k, f"{n}_e3", order, heads, D, scores, peaks3, acc)
        with ExitStack() as ctx:
            agg = sb("agg", [P, NT, D], F32, ctx)
            a_t = sb("a_t", [P, NP], F32, ctx)
            o_t = sb("o_t", [P, NP], F32, ctx)
            den = sb("den", [P, NT * heads], F32, ctx)
            al = sb("al", [P, NT], F32, ctx)
            sk = sb("sk", [P, rels], F32, ctx)
            gain = sb("gain", [P, 2, D], F32, ctx)
            load_rows(nc, k, f"{n}_ld", [(sk[:, :], row_bcast(W["skip"][l])), (gain[:, 0, :], row_bcast(W["ln_g"][l])),
                                         (gain[:, 1, :], row_bcast(W["ln_b"][l]))])

            def normalise(link, dve):
                a3 = acc[:, 0, :].rearrange("p (t c) -> p t c", c=FW)
                link(dve.tensor_tensor(acc[:, 0, :], acc[:, 0, :], acc[:, 1, :], ALU.add))
                d3 = den[:, :].rearrange("p (t h) -> p t h", h=heads)
                link(dve.tensor_scalar(d3, a3[:, :, D:FW], 1e-16, None, ALU.add))
                link(dve.reciprocal(den[:, :], den[:, :]))
                link(dve.tensor_tensor(agg[:, :, :].rearrange("p t (h c) -> p t h c", h=heads),
                                       a3[:, :, 0:D].rearrange("p t (h c) -> p t h c", h=heads),
                                       d3.unsqueeze(3).to_broadcast([P, NT, heads, D // heads]), ALU.mult))
            steps(nc, f"{n}_norm", normalise)
            transpose_all(nc, k, f"{n}_at", agg, a_t)
            typed_linear(nc, k, f"{n}_o", a_t, W["Wa"][l], o_t, silu=True)
            untranspose_all(nc, k, f"{n}_on", o_t, agg)
            s_sk = ctx.enter_context(signal(nc, f"{n}_s_sk"))
            s_mix = ctx.enter_context(signal(nc, f"{n}_s_mix"))
            hit = sb("hit", [P, NT], F32, ctx)
            with nc.Block() as block:
                @block.scalar
                def _(act):
                    act.activation(sk[:, :], sk[:, :], ACT.Sigmoid).then_inc(s_sk, 1)

                @block.vector
                def _(dve):
                    link = Chain(dve, s_mix).link
                    dve.wait_ge(s_sk, 1)
                    link(dve.memset(al[:, :], 0.0))
                    for t in range(rels):
                        link(dve.tensor_scalar(hit[:, :], k.type_col[:, :], float(t), sk[:, t:t + 1],
                                               ALU.is_equal, ALU.mult))
                        link(dve.tensor_tensor(al[:, :], al[:, :], hit[:, :], ALU.add))
                    link(dve.tensor_tensor(agg[:, :, :], agg[:, :, :], X[:, :, :], ALU.subtract))
                    link(dve.tensor_tensor(agg[:, :, :], agg[:, :, :], over_last(al[:, :], D), ALU.mult))
                    link(dve.tensor_tensor(X[:, :, :], X[:, :, :], agg[:, :, :], ALU.add))
            layer_norm(nc, k, f"{n}_ln", X, gain[:, 0, :], gain[:, 1, :])


def split3_steps(link, dve, src, parts, rest):
    link(dve.tensor_copy(parts[0], src))
    link(dve.tensor_tensor(rest, src, parts[0], ALU.subtract))
    link(dve.tensor_copy(parts[1], rest))
    link(dve.tensor_tensor(rest, rest, parts[1], ALU.subtract))
    link(dve.tensor_copy(parts[2], rest))


def sage(nc, k, X, order, W, table):
    s = k.s
    NT = s.NT
    width = D + 4
    with ExitStack() as outer:
        def sb(nm, shape, dt, where=outer):
            return where.enter_context(nc.sbuf_tensor(f"sage_{nm}", shape, dt))

        acc = sb("acc", [P, 2, NT * width], F32)
        with ExitStack() as ctx:
            row = sb("row", [P, NT, width], F32, ctx)

            def fill(link, dve):
                link(dve.memset(row[:, :, D:width], 1.0))
                link(dve.tensor_copy(row[:, :, 0:D], X[:, :, :]))
                link(dve.memset(acc[:, :, :], 0.0))
            steps(nc, "sage_fill", fill)
            store_table(nc, k, "sage_store", row[:, :, :], table)
        gather_sum(nc, k, "sage_e", order, order.row, table, width, acc)
        mean = sb("mean", [P, NT, D], F32)
        x_t = sb("x_t", [P, s.NP], F32)
        m_t = sb("m_t", [P, s.NP], F32)
        some = sb("some", [P, NT], F32)
        cnt = sb("cnt", [P, NT], F32)
        w = sb("w", [P, 2, D], F32)
        wt = sb("wt", [P, 2, D], F32)
        bias = sb("bias", [P, 2, D], F32)
        y = sb("y", [P, NT, D], F32)
        load_rows(nc, k, "sage_ld", [(w[:, 0, :], W["W_self"]), (w[:, 1, :], W["W_neigh"]),
                                     (bias[:, 0, :], row_bcast(W["b_self"])), (bias[:, 1, :], row_bcast(W["b_neigh"]))])

        def average(link, dve):
            a3 = acc[:, 0, :].rearrange("p (t c) -> p t c", c=width)
            link(dve.tensor_tensor(acc[:, 0, :], acc[:, 0, :], acc[:, 1, :], ALU.add))
            link(dve.tensor_scalar(some[:, :].unsqueeze(2), a3[:, :, D:D + 1], 0.0, None, ALU.is_gt))
            link(dve.tensor_scalar(cnt[:, :].unsqueeze(2), a3[:, :, D:D + 1], 1.0, None, ALU.max))
            link(dve.reciprocal(cnt[:, :], cnt[:, :]))
            link(dve.tensor_tensor(mean[:, :, :], a3[:, :, 0:D], over_last(cnt[:, :], D), ALU.mult))
            link(dve.tensor_tensor(y[:, :, :], over_last(some[:, :], D), over_mid(bias[:, 1, :], NT), ALU.mult))
            link(dve.tensor_tensor(y[:, :, :], y[:, :, :], over_mid(bias[:, 0, :], NT), ALU.add))
        steps(nc, "sage_avg", average)
        transpose_weights(nc, k, "sage_wt", w, wt, 2)
        transpose_all(nc, k, "sage_xt", X, x_t)
        transpose_all(nc, k, "sage_mt", mean, m_t)
        linear(nc, k, "sage_lin", [x_t, m_t], [wt[:, 0, :], wt[:, 1, :]], D, lambda a, m: mean[:, a:a + m, :])

        def finish(link, dve):
            link(dve.tensor_tensor(y[:, :, :], y[:, :, :], mean[:, :, :], ALU.add))
            link(dve.tensor_scalar(y[:, :, :], y[:, :, :], 0.0, None, ALU.max))
            link(dve.tensor_tensor(X[:, :, :], X[:, :, :], y[:, :, :], ALU.add))
        steps(nc, "sage_fin", finish)
    layer_norm(nc, k, "sage_ln", X)


def transpose_weights(nc, k, name, w, wt, n):
    def produce(pe, c, bank):
        return pe.transpose(k.psum[:, bank, 0:D], w[:, c, :], k.ident[:, :])

    banked(nc, k, name, n, produce, lambda copy, c, bank: copy(wt[:, c, :], k.psum[:, bank, 0:D]))


def gated_graph(nc, k, X, order, W, table):
    s = k.s
    NT, NP = s.NT, s.NP
    rounds = W["weight"].shape[0]
    with ExitStack() as outer:
        def sb(nm, shape, dt, where=outer):
            return where.enter_context(nc.sbuf_tensor(f"ggn_{nm}", shape, dt))

        w = sb("w", [P, 7, D], F32)
        wt = sb("wt", [P, 7, D], F32)
        wm = sb("wm", [P, rounds, D], F32)
        bias = sb("bias", [P, 7, D], F32)
        H = sb("H", [P, NT, D], F32)
        h_t = sb("h_t", [P, NP], F32)
        a_t = sb("a_t", [P, NP], F32)
        M = sb("M", [P, NT, D], F32)
        acc = sb("acc", [P, 2, NT * D], F32)
        load_rows(nc, k, "ggn_ld", [
            (w[:, 0:3, :], W["w_ih"].rearrange("(a p) c -> p a c", p=P)),
            (w[:, 3:6, :], W["w_hh"].rearrange("(a p) c -> p a c", p=P)),
            (w[:, 6, :], W["lin_w"]), (wm[:, :, :], W["weight"].rearrange("l i o -> i l o")),
            (flat(bias[:, 0:3, :]), row_bcast(W["b_ih"])), (flat(bias[:, 3:6, :]), row_bcast(W["b_hh"])),
            (bias[:, 6, :], row_bcast(W["lin_b"]))])
        transpose_weights(nc, k, "ggn_wt", w, wt, 7)
        steps(nc, "ggn_b", lambda link, dve: link(
            dve.tensor_tensor(bias[:, 0:2, :], bias[:, 0:2, :], bias[:, 3:5, :], ALU.add)))
        transpose_all(nc, k, "ggn_xt", X, h_t)
        linear(nc, k, "ggn_lin", [h_t], [wt[:, 6, :]], D, lambda a, m: H[:, a:a + m, :])
        steps(nc, "ggn_lb", lambda link, dve: link(
            dve.tensor_tensor(H[:, :, :], H[:, :, :], over_mid(bias[:, 6, :], NT), ALU.add)))
        for r in range(rounds):
            n = f"ggn{r}"
            transpose_all(nc, k, f"{n}_ht", H, h_t)
            linear(nc, k, f"{n}_m", [h_t], [wm[:, r, :]], D, lambda a, m: M[:, a:a + m, :])
            store_table(nc, k, f"{n}_st", M[:, :, :], table)
            steps(nc, f"{n}_z", lambda link, dve: link(dve.memset(acc[:, :, :], 0.0)))
            gather_sum(nc, k, f"{n}_e", order, order.node, table, D, acc)
            steps(nc, f"{n}_s", lambda link, dve: link(
                dve.tensor_tensor(flat(M[:, :, :]), acc[:, 0, :], acc[:, 1, :], ALU.add)))
            transpose_all(nc, k, f"{n}_at", M, a_t)
            gru(nc, k, n, H, h_t, a_t, wt, bias)
        steps(nc, "ggn_fin", lambda link, dve: link(
            dve.tensor_tensor(X[:, :, :], X[:, :, :], H[:, :, :], ALU.add)))
    layer_norm(nc, k, "ggn_ln", X)


def gru(nc, k, n, H, h_t, a_t, wt, bias):
    s = k.s
    parts = chunked(s.NT, 4)
    with ExitStack() as ctx:
        def sb(nm, shape, dt):
            return ctx.enter_context(nc.sbuf_tensor(f"{n}_{nm}", shape, dt))

        g = sb("gates", [P, 2, 4, 4, D], F32)
        t = sb("t", [P, 2, 4, D], F32)
        s_mm, s_g, s_rz, s_n, s_tanh, s_d = (ctx.enter_context(signal(nc, f"{n}_{x}"))
                                             for x in ("s_mm", "s_g", "s_rz", "s_n", "s_tanh", "s_d"))
        with nc.Block() as block:
            @block.tensor
            def _(pe):
                for c, (a, m) in enumerate(parts):
                    if c >= 2:
                        pe.wait_ge(s_g, c - 1)
                    for j in range(m):
                        bank = 4 * (c % 2) + j
                        xa, xh = a_t[:, (a + j) * P:(a + j + 1) * P], h_t[:, (a + j) * P:(a + j + 1) * P]
                        pe.matmul(k.psum[:, bank, 0:2 * D], xa, flat(wt[:, 0:2, :]), start=True, stop=False)
                        pe.matmul(k.psum[:, bank, 0:2 * D], xh, flat(wt[:, 3:5, :]), start=False, stop=True)
                        pe.matmul(k.psum[:, bank, 2 * D:3 * D], xa, wt[:, 2, :], start=True, stop=True)
                        last = pe.matmul(k.psum[:, bank, 3 * D:4 * D], xh, wt[:, 5, :], start=True, stop=True)
                    last.then_inc(s_mm, 1)

            @block.scalar
            def _(act):
                for c, (a, m) in enumerate(parts):
                    act.wait_ge(s_g, c + 1)
                    rz = g[:, c % 2, 0:m, 0:2, :]
                    act.activation(rz, rz, ACT.Sigmoid).then_inc(s_rz, 1)
                    act.wait_ge(s_n, c + 1)
                    act.activation(t[:, c % 2, 0:m, :], t[:, c % 2, 0:m, :], ACT.Tanh).then_inc(s_tanh, 1)

            @block.vector
            def _(dve):
                ch = Chain(dve, s_d)
                brow = bias[:, 0:3, :]
                for c, (a, m) in enumerate(parts):
                    b0 = 4 * (c % 2)
                    dve.wait_ge(s_mm, c + 1)
                    for j in range(m):
                        dve.tensor_tensor(g[:, c % 2, j, 0:3, :], k.psum[:, b0 + j, 0:3 * D].rearrange("p (a b) -> p a b", b=D),
                                          brow, ALU.add)
                        last = dve.tensor_tensor(g[:, c % 2, j, 3, :], k.psum[:, b0 + j, 3 * D:4 * D], bias[:, 5, :], ALU.add)
                    last.then_inc(s_g, 1)
                    dve.wait_ge(s_rz, c + 1)
                    tt = t[:, c % 2, 0:m, :]
                    ch.link(dve.tensor_tensor(tt, g[:, c % 2, 0:m, 0, :], g[:, c % 2, 0:m, 3, :], ALU.mult))
                    dve.tensor_tensor(tt, tt, g[:, c % 2, 0:m, 2, :], ALU.add).then_inc(s_n, 1)
                    dve.wait_ge(s_tanh, c + 1)
                    h = H[:, a:a + m, :]
                    ch.link(dve.tensor_tensor(h, h, tt, ALU.subtract))
                    ch.link(dve.tensor_tensor(h, h, g[:, c % 2, 0:m, 1, :], ALU.mult))
                    ch.link(dve.tensor_tensor(h, h, tt, ALU.add))


def gat(nc, k, n, in_t, ws, heads, width, att_src, att_dst, order, table, out):
    s = k.s
    NT = s.NT
    row = width + heads
    hw = width // heads
    with ExitStack() as outer:
        def sb(nm, shape, dt, where=outer):
            return where.enter_context(nc.sbuf_tensor(f"{n}_{nm}", shape, dt))

        scores = sb("scores", [P, s.T * heads], F32)
        peaks = sb("peaks", [P, NT, heads], F32)
        own = sb("own", [P, NT, heads], F32)
        to = sb("to", [P, NT, heads], F32)
        acc = sb("acc", [P, 2, NT * row], F32)
        peaks3 = sb("peaks3", [P, 3, NT * heads], BF16)
        keep_h = outer.enter_context(ExitStack())
        h = sb("h", [P, NT, row], F32, keep_h)
        with ExitStack() as ctx:
            att = sb("att", [P, 2, width], F32, ctx)
            prod = sb("prod", [P, NT, width], F32, ctx)
            load_rows(nc, k, f"{n}_ld", [(att[:, 0, :], row_bcast(att_src)), (att[:, 1, :], row_bcast(att_dst))])
            linear(nc, k, f"{n}_h", in_t, ws, width, lambda a, m: h[:, a:a + m, 0:width])

            def node_scores(link, dve):
                for side, dst in ((0, h[:, :, width:row]), (1, to[:, :, :])):
                    link(dve.tensor_tensor(prod[:, :, :], h[:, :, 0:width], over_mid(att[:, side, :], NT), ALU.mult))
                    link(dve.tensor_reduce(dst, prod[:, :, :].rearrange("p t (h c) -> p t h c", c=hw), AX.X, ALU.add))
                link(dve.tensor_tensor(own[:, :, :], h[:, :, width:row], to[:, :, :], ALU.add))
                link(dve.tensor_scalar(peaks[:, :, :], own[:, :, :], NEG_SLOPE, None, ALU.mult))
                link(dve.tensor_tensor(own[:, :, :], own[:, :, :], peaks[:, :, :], ALU.max))
                link(dve.tensor_copy(peaks[:, :, :], own[:, :, :]))
            steps(nc, f"{n}_sc", node_scores)
        store_table(nc, k, f"{n}_st", h[:, :, :], table)
        with ExitStack() as ctx:
            to3 = sb("to3", [P, 3, NT * heads], BF16, ctx)
            rest = sb("rest", [P, NT * heads], F32, ctx)
            steps(nc, f"{n}_to3", lambda link, dve: split3_steps(
                link, dve, flat(to[:, :, :]), [to3[:, j, :] for j in range(3)], rest[:, :]))
            score_rows(nc, k, f"{n}_e1", order, order.node, table, row, "add", (0, width), heads, to3, scores, peaks)
        s_own = outer.enter_context(signal(nc, f"{n}_s_own"))
        s_exp = outer.enter_context(signal(nc, f"{n}_s_exp"))
        s_o = outer.enter_context(signal(nc, f"{n}_s_o"))
        a3 = acc[:, 0, :].rearrange("p (t c) -> p t c", c=row)
        with nc.Block() as block:
            @block.vector
            def _(dve):
                link = Chain(dve, s_o).link
                dve.tensor_tensor(own[:, :, :], own[:, :, :], peaks[:, :, :], ALU.subtract).then_inc(s_own, 1)
                split3_steps(link, dve, flat(peaks[:, :, :]), [peaks3[:, j, :] for j in range(3)], flat(to[:, :, :]))
                link(dve.memset(acc[:, 1, :], 0.0))
                dve.wait_ge(s_exp, 1)
                link(dve.tensor_copy(a3[:, :, width:row], own[:, :, :]))
                link(dve.tensor_tensor(a3[:, :, 0:width].rearrange("p t (h c) -> p t h c", h=heads),
                                       h[:, :, 0:width].rearrange("p t (h c) -> p t h c", h=heads),
                                       own[:, :, :].unsqueeze(3).to_broadcast([P, NT, heads, hw]), ALU.mult))

            @block.scalar
            def _(act):
                act.wait_ge(s_own, 1)
                act.activation(own[:, :, :], own[:, :, :], ACT.Exp).then_inc(s_exp, 1)
        keep_h.close()
        weigh_rows(nc, k, f"{n}_e3", order, heads, width, scores, peaks3, acc)

        def normalise(link, dve):
            link(dve.tensor_tensor(acc[:, 0, :], acc[:, 0, :], acc[:, 1, :], ALU.add))
            link(dve.tensor_copy(own[:, :, :], a3[:, :, width:row]))
            link(dve.reciprocal(own[:, :, :], own[:, :, :]))
            link(dve.tensor_tensor(out[:, :, :].rearrange("p t (h c) -> p t h c", h=heads),
                                   a3[:, :, 0:width].rearrange("p t (h c) -> p t h c", h=heads),
                                   own[:, :, :].unsqueeze(3).to_broadcast([P, NT, heads, hw]), ALU.mult))
        steps(nc, f"{n}_nrm", normalise)


def attention_network(nc, k, X, order, W, table1, table2):
    s = k.s
    NT, NP = s.NT, s.NP
    f1 = W["W1"].shape[1]
    with ExitStack() as outer:
        def sb(nm, shape, dt, where=outer):
            return where.enter_context(nc.sbuf_tensor(f"gat_{nm}", shape, dt))

        h_t = sb("h_t", [P, 2, NP], F32)
        wrow = sb("wrow", [P, 2, f1], F32)
        with ExitStack() as ctx:
            o1 = sb("o1", [P, NT, f1], F32, ctx)
            load_rows(nc, k, "gat_ld", [(wrow[:, 0, :], W["W1"])])
            transpose_all(nc, k, "gat_xt", X, h_t[:, 0, :])
            gat(nc, k, "ga", [h_t[:, 0, :]], [wrow[:, 0, :]], W["att_src1"].shape[0], f1,
                W["att_src1"].rearrange("h c -> (h c)"), W["att_dst1"].rearrange("h c -> (h c)"), order, table1, o1)
            b1 = sb("b1", [P, f1], F32, ctx)
            neg = sb("neg", [P, NT, f1], F32, ctx)
            load_rows(nc, k, "gat_lb", [(b1[:, :], row_bcast(W["b1"])),
                                        (wrow[:, :, 0:D], W["W2"].rearrange("(a p) c -> p a c", p=P))])
            s_n, s_e, s_d = (ctx.enter_context(signal(nc, f"gat_{x}")) for x in ("s_n", "s_e", "s_d"))
            with nc.Block() as block:
                @block.vector
                def _(dve):
                    link = Chain(dve, s_d).link
                    link(dve.tensor_tensor(o1[:, :, :], o1[:, :, :], over_mid(b1[:, :], NT), ALU.add))
                    dve.tensor_scalar(neg[:, :, :], o1[:, :, :], 0.0, None, ALU.min).then_inc(s_n, 1)
                    link(dve.tensor_scalar(o1[:, :, :], o1[:, :, :], 0.0, None, ALU.max))
                    dve.wait_ge(s_e, 1)
                    link(dve.tensor_scalar(neg[:, :, :], neg[:, :, :], -1.0, None, ALU.add))
                    link(dve.tensor_tensor(o1[:, :, :], o1[:, :, :], neg[:, :, :], ALU.add))

                @block.scalar
                def _(act):
                    act.wait_ge(s_n, 1)
                    act.activation(neg[:, :, :], neg[:, :, :], ACT.Exp).then_inc(s_e, 1)
            for half in range(2):
                transpose_all(nc, k, f"gat_ot{half}", o1[:, :, half * D:(half + 1) * D], h_t[:, half, :])
        o2 = sb("o2", [P, NT, D], F32)
        gat(nc, k, "gb", [h_t[:, 0, :], h_t[:, 1, :]], [wrow[:, 0, 0:D], wrow[:, 1, 0:D]], 1, D,
            W["att_src2"].rearrange("h c -> (h c)"), W["att_dst2"].rearrange("h c -> (h c)"), order, table2, o2)
        b2 = sb("b2", [P, D], F32)
        load_rows(nc, k, "gat_lb2", [(b2[:, :], row_bcast(W["b2"]))])

        def finish(link, dve):
            link(dve.tensor_tensor(X[:, :, :], X[:, :, :], o2[:, :, :], ALU.add))
            link(dve.tensor_tensor(X[:, :, :], X[:, :, :], over_mid(b2[:, :], NT), ALU.add))
        steps(nc, "gat_fin", finish)
    layer_norm(nc, k, "gat_ln", X)


def load_nodes(nc, k, x, node_type, X):
    s = k.s
    full = s.N // P
    left = s.N - full * P
    with ExitStack() as ctx:
        raw_row = ctx.enter_context(nc.sbuf_tensor("raw_row", [P, s.N], I32))
        raw_col = ctx.enter_context(nc.sbuf_tensor("raw_col", [P, s.NT], I32))
        s_z = ctx.enter_context(signal(nc, "ln_s_z"))
        s_in = ctx.enter_context(signal(nc, "ln_s_in"))
        s_d = ctx.enter_context(signal(nc, "ln_s_d"))
        with nc.Block() as block:
            @block.vector
            def _(dve):
                link = Chain(dve, s_d).link
                dve.memset(X[:, full, :], 0.0)
                dve.memset(raw_col[:, :], -1)
                dve.memset(k.type_row[:, s.N:s.NP], -1.0).then_inc(s_z, 1)
                dve.wait_ge(s_in, 16 * 5)
                link(dve.tensor_copy(k.type_row[:, 0:s.N], raw_row[:, :]))
                link(dve.tensor_copy(k.type_col[:, :], raw_col[:, :]))

            @block.sync
            def _(sp):
                sp.wait_ge(s_z, 1)
                sp.dma_start(X[:, 0:full, :], x[0:full * P, :].rearrange("(t p) c -> p t c", p=P)).then_inc(s_in, 16)
                sp.dma_start(X[0:left, full, :], x[full * P:s.N, :]).then_inc(s_in, 16)
                sp.dma_start(raw_row[:, :], row_bcast(node_type)).then_inc(s_in, 16)
                with nc.allow_non_contiguous_dma("node types by column, once"):
                    sp.dma_start(raw_col[:, 0:full], node_type[0:full * P].rearrange("(t p) -> p t", p=P)).then_inc(s_in, 16)
                    sp.dma_start(raw_col[0:left, full:full + 1], node_type[full * P:s.N].unsqueeze(1)).then_inc(s_in, 16)


def store_nodes(nc, k, X, out):
    s = k.s
    full = s.N // P
    left = s.N - full * P
    with signal(nc, "s_out") as s_out, nc.Block() as block:
        @block.sync
        def _(sp):
            sp.dma_start(out[0:full * P, :].rearrange("(t p) c -> p t c", p=P), X[:, 0:full, :]).then_inc(s_out, 16)
            sp.dma_start(out[full * P:s.N, :], X[0:left, full, :]).then_inc(s_out, 16)
            sp.wait_ge(s_out, 32)


def group(arrays, prefix):
    return {n[len(prefix):]: a for n, a in arrays.items() if n.startswith(prefix)}


def gnn_program(nc, a, out, upto=9):
    s = Shapes(a["x"].shape[0], a["src"].shape[0])
    turn[:] = range(FIRST_SEMAPHORE, LAST_SEMAPHORE + 1)

    def dram(n, shape):
        return nc.dram_tensor(n, shape, F32, kind="Internal").ap()

    w1 = group(a, "L0_gnn_")
    rels = w1["pri"].shape[2]
    gat_w = group(a, "L3_gnn_")
    heads, f1 = gat_w["att_src1"].shape[0], gat_w["W1"].shape[1]
    with ExitStack() as ctx:
        k = Kit(nc, ctx, s)
        k.type_col = k.sb("type_col", [P, s.NT], F32)
        k.stash = dram("stash", [P, s.T, f1])
        X = k.sb("X", [P, s.NT, D], F32)
        by_dst = Edges(k.sb, nc, s, "by_dst", True)
        by_src = Edges(k.sb, nc, s, "by_src", False)
        constants(nc, k)
        with nc.sbuf_tensor("pair", [P, s.T, 2], F16) as pair:
            k.pair = pair
            bucket_edges(nc, k, by_dst, a["dst"], a["src"], a["edge_type_8"], "bd", True)
            sort_tiles(nc, k, by_dst)
        bucket_edges(nc, k, by_src, a["src"], a["dst"], None, "bs", False)
        with nc.sbuf_tensor("type_row", [P, s.NP], F32) as type_row, nc.sbuf_tensor("X0", [P, s.NT, D], F32) as X0:
            k.type_row = type_row
            load_nodes(nc, k, a["x"], a["node_type_8"], X)
            steps(nc, "keep", lambda link, dve: link(dve.tensor_copy(X0[:, :, :], X[:, :, :])))
            table = dram("relation_table", [s.NP * rels, 2 * D])
            for l in range(w1["Wk"].shape[0]):
                graph_transformer(nc, k, l, X, by_dst, w1, table)
            with nc.sbuf_tensor("e_t", [P, s.NP], F32) as e_t, nc.sbuf_tensor("wff", [P, 2, D], F32) as wff:
                load_rows(nc, k, "ff_ld", [(wff[:, 0, :], w1["Wff"]), (wff[:, 1, :], row_bcast(w1["bff"]))])
                transpose_all(nc, k, "ff_t", X, e_t)
                linear(nc, k, "ff", [e_t], [wff[:, 0, :]], D, lambda t, m: X[:, t:t + m, :])

                def residual(link, dve):
                    link(dve.tensor_tensor(X[:, :, :], X[:, :, :], over_mid(wff[:, 1, :], s.NT), ALU.add))
                    link(dve.tensor_tensor(X[:, :, :], X[:, :, :], X0[:, :, :], ALU.add))
                steps(nc, "ff_r", residual)
        layer_norm(nc, k, "ff_ln", X)
        if upto >= 1:
            sage(nc, k, X, by_src, group(a, "L1_gnn_"), dram("sage_table", [s.NP, D + 4]))
        if upto >= 2:
            gated_graph(nc, k, X, by_dst, group(a, "L2_gnn_"), dram("message_table", [s.NP, D]))
        if upto >= 3:
            attention_network(nc, k, X, by_dst, gat_w, dram("gat_table1", [s.NP, f1 + heads]),
                              dram("gat_table2", [s.NP, D + 1]))
        store_nodes(nc, k, X, out)


def kernel(**inputs):
    import concourse.bacc as bacc
    from concourse.bass_utils import run_bass_kernel_spmd

    nc = bacc.Bacc("TRN2", target_bir_lowering=False, num_devices=1)
    arrays, aps = {}, {}
    for name, value in inputs.items():
        arrays[f"in_{name}"] = np.ascontiguousarray(value)
        aps[name] = nc.dram_tensor(f"in_{name}", arrays[f"in_{name}"].shape,
                                   mybir.dt.from_np(arrays[f"in_{name}"].dtype), kind="ExternalInput").ap()
    nodes, features = inputs["x"].shape
    out = nc.dram_tensor("out", [nodes, features], F32, kind="ExternalOutput").ap()
    gnn_program(nc, aps, out)
    result = run_bass_kernel_spmd(nc, [arrays], core_ids=[0])
    return result.results[0]["out"]
```

```python
from contextlib import ExitStack, contextmanager

import numpy as np

import concourse.bass as bass
from concourse import mybir

F32 = mybir.dt.float32
F16 = mybir.dt.float16
BF16 = mybir.dt.bfloat16
I32 = mybir.dt.int32
ALU = mybir.AluOpType
ACT = mybir.ActivationFunctionType
AX = mybir.AxisListType
ds = bass.ds

P = 128
D = 128
BIG = 3.0e38
LN_EPS = 1e-05


class Chain:

    def __init__(self, eng, sem, done=0):
        self.eng, self.sem, self.done, self.offset = eng, sem, done, 0

    def link(self, ins):
        ins.then_inc(self.sem, 1)
        self.done += 1
        self.eng.wait_ge(self.sem, self.offset + self.done)

    def enter(self, i, steps):
        self.offset, self.first, self.steps = i * steps, self.done, steps

    def leave(self, rounds):
        assert self.done - self.first == self.steps, (self.done - self.first, self.steps)
        self.offset, self.done = 0, self.first + rounds * self.steps


def flat(ap):
    return ap.rearrange("p a b -> p (a b)")


def over_last(ap, n):
    return ap.unsqueeze(2).to_broadcast([ap.shape[0], ap.shape[1], n])


def over_mid(ap, n):
    return ap.unsqueeze(1).to_broadcast([ap.shape[0], n, ap.shape[1]])


FIRST_SEMAPHORE, LAST_SEMAPHORE = 110, 250
turn = []


@contextmanager
def signal(nc, name):
    num = turn.pop(0)
    handle = nc.alloc_semaphore(name=name, num=num)
    yield handle
    nc.gpsimd.sem_clear(handle)
    nc.release_semaphore(handle)
    turn.append(num)


def free(eng, *sems, by=1):
    for sem in sems:
        eng.sem_inc(sem, by)


class Shapes:

    def __init__(self, nodes, edges):
        self.N, self.E = nodes, edges
        self.NT = -(-nodes // P)
        self.NP = self.NT * P
        self.EP = max(p for p in range(1, P + 1) if edges % p == 0 and (edges // p) % 4 == 0)
        self.ET = edges // self.EP
        most = (edges + self.NT * (P - 1)) // P
        self.T = -(-most // 32) * 32
        assert self.NT == 25 and self.EP == 125 and self.T == 416


class Edges:

    def __init__(self, sb, nc, s, name, detailed):
        self.row = sb(f"{name}_row", [P, s.T], I32)
        self.local = sb(f"{name}_local", [P, s.T], F32)
        self.tile = sb(f"{name}_tile", [1, s.T + 16], I32)
        if detailed:
            self.node = sb(f"{name}_node", [P, s.T], I32)
            self.last = sb(f"{name}_last", [P, s.T], F32)
            self.cut = sb(f"{name}_cut", [P, s.T], F32)
            self.gather = nc.dram_tensor(f"{name}_gather", [P, s.T * P], BF16, kind="Internal").ap()
            self.scatter = nc.dram_tensor(f"{name}_scatter", [P, s.T * P], BF16, kind="Internal").ap()


def constants(nc, k):
    with nc.Block() as block:
        @block.gpsimd
        def _(pool):
            pool.iota(k.iota[:, :], [[1, P]], base=0, channel_multiplier=0,
                      allow_small_or_imprecise_dtypes=True).then_inc(k.s_iota, 1)
            pool.iota(k.iota16[:, :], [[1, k.s.T]], base=0, channel_multiplier=0,
                      allow_small_or_imprecise_dtypes=True).then_inc(k.s_iota, 1)
            pool.iota(k.iota_p[:, :], [[0, 1]], base=0, channel_multiplier=1,
                      allow_small_or_imprecise_dtypes=True).then_inc(k.s_iota, 1)
            pool.iota(k.ident[:, :], [[1, P]], base=0, channel_multiplier=-1,
                      allow_small_or_imprecise_dtypes=True).then_inc(k.s_iota, 1)

        @block.vector
        def _(dve):
            chain = Chain(dve, k.s_const)
            dve.wait_ge(k.s_iota, 4)
            chain.link(dve.tensor_scalar(k.upto[:, :], k.ident[:, :], 0.0, -1.0, ALU.is_le, ALU.mult))
            chain.link(dve.tensor_scalar(k.ident[:, :], k.ident[:, :], 0.0, None, ALU.is_equal))
            chain.link(dve.memset(k.ones16[:, :], 1.0))
            chain.link(dve.memset(k.zeros16[:, :], 0.0))
            chain.link(dve.memset(k.ones[:, :], 1.0))


def bucket_edges(nc, k, order, key_d, node_d, type_d, name, refine):
    s = k.s
    T, NT, EP, ET = s.T, s.NT, s.EP, s.ET
    CH = 500
    NCH = NT * ET // CH
    half = NCH // 4
    TC = T // 104
    assert CH * NCH == NT * ET and NCH % 4 == 0
    with ExitStack() as ctx:
        def sb(n, shape, dt):
            return ctx.enter_context(nc.sbuf_tensor(f"{name}_{n}", shape, dt))

        def sem(n):
            return ctx.enter_context(signal(nc, f"{name}_{n}"))

        key = sb("key", [EP, ET], I32)
        node = sb("node_in", [EP, ET], I32)
        typ = sb("type_in", [EP, ET], I32)
        work = sb("work", [EP, ET], I32)
        low = sb("low", [EP, ET], I32)
        bucket = sb("bucket", [EP, ET], F16)
        U = sb("U", [EP, ET], F32)
        W = sb("W", [EP, ET], F32)
        pcol = sb("pcol", [EP, ET], F32)
        tcol = sb("tcol", [EP, ET], F32)
        posf = sb("posf", [EP, ET], F32)
        outer = ExitStack()
        with outer:
            def sbo(n, shape, dt):
                return outer.enter_context(nc.sbuf_tensor(f"{name}_{n}", shape, dt))
            onehot = sbo("onehot", [EP, NT, ET], F16)
            total = sbo("total", [EP, NT, ET], F32)
            before = sbo("before", [EP, NT, ET], F32)
            count = sbo("count", [EP, NT], F32)
            counti = sbo("counti", [EP, NT], I32)
            tiles = sbo("tiles", [EP, NT], F32)
            start = sbo("start", [EP, NT], F32)
            startc = sbo("startc", [EP, NT], F32)
            tix = sbo("tix", [EP, TC], F32)
            tbl = sbo("tbl", [EP, TC, NT], F32)
            tsum = sbo("tsum", [EP, TC], F32)
            tnum = sbo("tnum", [EP, TC], I32)
            s_in = sem("s_in")
            s_hot = sem("s_hot")
            s_mm = sem("s_mm")
            s_ev = sem("s_ev")
            s_tiles = sem("s_tiles")
            s_out = sem("s_out")
            s_dve = sem("s_dve")
            hot_f = onehot[:, :, :].rearrange("p b t -> p (b t)")
            tot_f = total[:, :, :].rearrange("p b t -> p (b t)")
            bef_f = before[:, :, :].rearrange("p b t -> p (b t)")
            with nc.Block() as block:
                @block.sync
                def _(sp):
                    sp.dma_start(key[:, :], key_d.rearrange("(p t) -> p t", p=EP)).then_inc(s_in, 16)
                    sp.dma_start(node[:, :], node_d.rearrange("(p t) -> p t", p=EP)).then_inc(s_in, 16)
                    if type_d is not None:
                        sp.dma_start(typ[:, :], type_d.rearrange("(p t) -> p t", p=EP)).then_inc(s_in, 16)
                    sp.wait_ge(s_tiles, 1)
                    sp.dma_start(order.tile[0:1, 0:T], tnum[0:T // TC, :]).then_inc(s_out, 16)
                    sp.wait_ge(s_out, 16)

                @block.vector
                def _(dve):
                    c = Chain(dve, s_dve)
                    dve.wait_ge(s_in, 48 if type_d is not None else 32)
                    c.link(dve.tensor_scalar(work[:, :], key[:, :], 7, None, ALU.arith_shift_right))
                    c.link(dve.tensor_copy(bucket[:, :], work[:, :]))
                    dve.tensor_tensor(onehot[:, :, :], over_mid(bucket[:, :], NT),
                                      over_last(k.iota16[0:EP, 0:NT], ET), ALU.is_equal).then_inc(s_hot, 1)
                    if type_d is not None:
                        c.link(dve.tensor_scalar(work[:, :], node[:, :], 3, None, ALU.logical_shift_left))
                        c.link(dve.tensor_tensor(node[:, :], work[:, :], typ[:, :], ALU.bitwise_or))
                    c.link(dve.tensor_scalar(work[:, :], node[:, :], 4, None, ALU.arith_shift_right))
                    c.link(dve.tensor_scalar(U[:, :], work[:, :], 1.0, None, ALU.add))
                    c.link(dve.tensor_scalar(work[:, :], node[:, :], 15, 7, ALU.bitwise_and, ALU.logical_shift_left))
                    c.link(dve.tensor_scalar(low[:, :], key[:, :], 127, None, ALU.bitwise_and))
                    c.link(dve.tensor_tensor(W[:, :], work[:, :], low[:, :], ALU.add))
                    c.link(dve.memset(order.tile[0:1, T:T + 16], 0))
                    c.link(dve.tensor_scalar(tix[:, :], k.iota_p[0:EP, :].to_broadcast([EP, TC]), float(TC), None, ALU.mult))
                    c.link(dve.tensor_tensor(tix[:, :], tix[:, :], k.iota[0:EP, 0:TC], ALU.add))
                    dve.wait_ge(s_ev, NCH + 4)
                    c.link(dve.tensor_reduce(count[:, :], total[:, :, :], AX.X, ALU.add))
                    c.link(dve.tensor_scalar(count[:, :], count[:, :], 127.0, None, ALU.add))
                    c.link(dve.tensor_copy(counti[:, :], count[:, :]))
                    c.link(dve.tensor_scalar(counti[:, :], counti[:, :], 7, None, ALU.arith_shift_right))
                    c.link(dve.tensor_copy(tiles[:, :], counti[:, :]))
                    c.link(dve.tensor_tensor_scan(start[:, :], tiles[:, :], tiles[:, :], 0.0, ALU.add, ALU.max))
                    c.link(dve.tensor_tensor(start[:, :], start[:, :], tiles[:, :], ALU.subtract))
                    c.link(dve.tensor_scalar(startc[:, :], start[:, :], float(P), None, ALU.mult))
                    c.link(dve.tensor_tensor(tbl[:, :, :], over_mid(start[:, :], TC), over_last(tix[:, :], NT), ALU.is_le))
                    c.link(dve.tensor_reduce(tsum[:, :], tbl[:, :, :], AX.X, ALU.add))
                    dve.tensor_scalar(tnum[:, :], tsum[:, :], -1.0, None, ALU.add).then_inc(s_tiles, 1)
                    for b in range(NT):
                        last = dve.tensor_tensor_scan(total[:, b, :], total[:, b, :], total[:, b, :],
                                                      startc[:, b:b + 1], ALU.add, ALU.max)
                    c.link(last)
                    dve.wait_ge(s_ev, NCH * 2 + 4)
                    c.link(dve.tensor_tensor(bef_f, bef_f, tot_f, ALU.add))
                    c.link(dve.tensor_tensor(bef_f, bef_f, hot_f, ALU.mult))
                    c.link(dve.tensor_reduce(posf[:, :], before[:, :, :].rearrange("p b t -> p t b"), AX.X, ALU.add))
                    c.link(dve.tensor_copy(work[:, :], posf[:, :]))
                    c.link(dve.tensor_scalar(low[:, :], work[:, :], 127, None, ALU.bitwise_and))
                    c.link(dve.tensor_copy(pcol[:, :], low[:, :]))
                    c.link(dve.tensor_scalar(low[:, :], work[:, :], 7, None, ALU.arith_shift_right))
                    c.link(dve.tensor_copy(tcol[:, :], low[:, :]))

                @block.tensor
                def _(pe):
                    pe.wait_ge(s_hot, 1)
                    for half_at in range(2):
                        tri = k.ones16 if half_at == 0 else k.upto
                        with pe.Fori(0, half) as i:
                            for u in range(4):
                                bank = 4 * half_at + u
                                pe.wait_ge(s_ev, i * 4 + (half_at * NCH + u + 1))
                                pe.matmul(k.psum[0:EP, bank, 0:CH], tri[0:EP, 0:EP],
                                          hot_f[:, ds(i * (4 * CH) + u * CH, CH)],
                                          start=True, stop=True).then_inc(s_mm, 1)

                @block.scalar
                def _(act):
                    free(act, s_ev, by=4)
                    for half_at in range(2):
                        dst = tot_f if half_at == 0 else bef_f
                        with act.Fori(0, half) as i:
                            for u in range(4):
                                act.wait_ge(s_mm, i * 4 + (half_at * NCH + u + 1))
                                act.activation(dst[:, ds(i * (4 * CH) + u * CH, CH)],
                                               k.psum[0:EP, 4 * half_at + u, 0:CH], ACT.Copy).then_inc(s_ev, 1)

        PER, SETS = 4, 4
        oh_t = sb("oh_t", [EP, SETS, PER, T], F16)
        oh_p = sb("oh_p", [EP, SETS, PER, P], F16)
        put = sb("put", [EP, SETS, 2, PER, P], F16)
        s_oh = [sem(f"s_oh{h}") for h in range(SETS)]
        s_u = [sem(f"s_u{h}") for h in range(SETS)]
        s_w = [sem(f"s_w{h}") for h in range(SETS)]
        s_used = [sem(f"s_used{h}") for h in range(SETS)]
        s_put = sem("s_put")
        s_d2 = sem("s_d2")
        ws = sb("ws", [P, T], I32)
        us = sb("us", [P, T], I32)
        val = sb("val", [P, T], F32)
        wl = sb("wl", [P, T], I32)
        with nc.Block() as block:
            @block.vector
            def _(dve):
                with dve.Fori(0, ET // (SETS * PER)) as i:
                    for h in range(SETS):
                        dve.wait_ge(s_used[h], i + 1)
                        for u in range(PER):
                            t = ds(i * (SETS * PER) + (h * PER + u), 1)
                            dve.tensor_scalar(oh_p[:, h, u, :], k.iota16[0:EP, 0:P], pcol[:, t], None,
                                              ALU.is_equal).then_inc(s_oh[h], 1)
                            dve.tensor_scalar(oh_t[:, h, u, :], k.iota16[0:EP, :], tcol[:, t], None,
                                              ALU.is_equal).then_inc(s_oh[h], 1)
                c = Chain(dve, s_d2)
                dve.wait_ge(s_put, 1)
                if refine:
                    c.link(dve.tensor_copy(k.pair[:, :, 0], k.psum[:, 0, 0:T]))
                    c.link(dve.tensor_copy(k.pair[:, :, 1], k.psum[:, 1, 0:T]))
                else:
                    decode(c, dve, k, order, k.psum[:, 0, 0:T], k.psum[:, 1, 0:T], us, ws, wl, val, None)

            @block.tensor
            def _(pe):
                free(pe, *s_used)
                for v in range(2):
                    pe.matmul(k.psum[:, v, 0:T], k.zeros16[0:EP, :], k.iota16[0:EP, :], start=True, stop=False)
                with pe.Fori(0, ET // (SETS * PER)) as i:
                    for h in range(SETS):
                        for u in range(PER):
                            pe.wait_ge(s_oh[h], i * (2 * PER) + (2 * u + 2))
                            pe.wait_ge(s_u[h], i * PER + (u + 1))
                            pe.wait_ge(s_w[h], i + 1)
                            for v in range(2):
                                last = pe.matmul(k.psum[:, v, 0:T], put[:, h, v, u, :], oh_t[:, h, u, :],
                                                 start=False, stop=False)
                        last.then_inc(s_used[h], 1)
                for v in range(2):
                    last = pe.matmul(k.psum[:, v, 0:T], k.zeros16[0:EP, :], k.iota16[0:EP, :], start=False, stop=True)
                last.then_inc(s_put, 1)

            @block.scalar
            def _(act):
                with act.Fori(0, ET // (SETS * PER)) as i:
                    for h in range(SETS):
                        act.wait_ge(s_used[h], i + 1)
                        for u in range(PER):
                            act.wait_ge(s_oh[h], i * (2 * PER) + (2 * u + 1))
                            act.nop(nofuse=True)
                            act.activation(put[:, h, 0, u, :], oh_p[:, h, u, :], ACT.Copy,
                                           scale=U[:, ds(i * (SETS * PER) + (h * PER + u), 1)]).then_inc(s_u[h], 1)

            @block.gpsimd
            def _(pool):
                with pool.Fori(0, ET // (SETS * PER)) as i:
                    for h in range(SETS):
                        pool.wait_ge(s_used[h], i + 1)
                        pool.wait_ge(s_oh[h], i * (2 * PER) + (2 * PER - 1))
                        pool.nop(nofuse=True)
                        pool.tensor_tensor(put[:, h, 1, :, :], oh_p[:, h, :, :],
                                           over_last(W[:, ds(i * (SETS * PER) + h * PER, PER)], P),
                                           ALU.mult).then_inc(s_w[h], 1)


def decode(c, dve, k, order, u_in, w_in, us, ws, wl, val, node):
    c.link(dve.tensor_scalar(val[:, :], u_in, 0.0, None, ALU.is_gt))
    c.link(dve.tensor_copy(ws[:, :], w_in))
    c.link(dve.tensor_scalar(us[:, :], u_in, -1.0, 0.0, ALU.add, ALU.max))
    c.link(dve.tensor_scalar(wl[:, :], us[:, :], 4, None, ALU.logical_shift_left))
    c.link(dve.tensor_scalar(us[:, :], ws[:, :], 7, None, ALU.arith_shift_right))
    c.link(dve.tensor_tensor(order.row[:, :], wl[:, :], us[:, :], ALU.bitwise_or))
    c.link(dve.tensor_scalar(wl[:, :], ws[:, :], 127, None, ALU.bitwise_and))
    c.link(dve.tensor_copy(order.local[:, :], wl[:, :]))
    c.link(dve.scalar_tensor_tensor(order.local[:, :], order.local[:, :], 1.0, val[:, :], ALU.add, ALU.mult))
    c.link(dve.tensor_scalar(order.local[:, :], order.local[:, :], -1.0, None, ALU.add))
    if node is not None:
        c.link(dve.tensor_scalar(node[:, :], order.row[:, :], 3, None, ALU.arith_shift_right))


def sort_tiles(nc, k, order):
    s = k.s
    T = s.T
    B = -(-T // P)
    width = [min(P, T - b * P) for b in range(B)]
    G = 8
    R = T // (2 * G)
    with ExitStack() as ctx:
        def sb(n, shape, dt):
            return ctx.enter_context(nc.sbuf_tensor(f"st_{n}", shape, dt))

        def sem(n):
            return ctx.enter_context(signal(nc, f"st_{n}"))

        def pair_of(n):
            return [sem(f"{n}{h}") for h in range(2)]

        key = sb("key", [P, T], F32)
        val = sb("val", [P, T], F32)
        a = sb("a", [P, T], I32)
        b_ = sb("b", [P, T], I32)
        w = sb("w", [P, T], I32)
        node = sb("node", [P, T], F16)
        ident16 = sb("ident16", [P, P], F16)
        diag = sb("diag", [P, P], F16)
        less = sb("less", [P, 2, G, P], F16)
        hot = sb("hot", [P, 2, G, P], F16)
        out = sb("out", [P, T, 2], F32)
        s_d, s_key = sem("s_d"), sem("s_key")
        s_bc, s_less, s_rank, s_hot, s_mv, s_out = (pair_of(n) for n in (
            "s_bc", "s_less", "s_rank", "s_hot", "s_mv", "s_out"))

        def near(i, h, by):
            return i + (h + by) // 2, (h + by) % 2

        def in_rounds(eng, position):
            for h in range(2):
                position(0, h, h == 0, False)
            with eng.Fori(1, R - 1) as i:
                for h in range(2):
                    position(i, h, False, False)
            for h in range(2):
                position(R - 1, h, False, h == 1)

        with nc.Block() as block:
            @block.vector
            def _(dve):
                c = Chain(dve, s_d)
                U, W = k.pair[:, :, 0], k.pair[:, :, 1]
                c.link(dve.tensor_copy(ident16[:, :], k.ident[:, :]))
                c.link(dve.tensor_scalar(diag[:, :], k.ident[:, :], float(P), None, ALU.mult))
                c.link(dve.tensor_scalar(val[:, :], U, 0.0, 256.0, ALU.is_equal, ALU.mult))
                c.link(dve.tensor_copy(a[:, :], W))
                c.link(dve.tensor_scalar(a[:, :], a[:, :], 127, None, ALU.bitwise_and))
                c.link(dve.tensor_tensor(key[:, :], val[:, :], a[:, :], ALU.add))
                c.link(dve.tensor_copy(node[:, :], key[:, :]))
                c.link(dve.tensor_scalar(key[:, :], key[:, :], float(P), k.iota_p[:, :], ALU.mult, ALU.add))
                dve.sem_inc(s_key, 1)
                free(dve, *s_less, *s_hot)

                def compare(i, h):
                    dve.wait_ge(s_bc[h], i + 1)
                    dve.wait_ge(s_rank[h], i + 1)
                    dve.tensor_tensor(less[:, h, :, :],
                                      k.psum[:, 2 * h:2 * h + 2, :].rearrange("p a (b c) -> p (a b) c", c=P),
                                      over_last(key[:, ds(i * (2 * G) + h * G, G)], P), ALU.is_gt).then_inc(s_less[h], 1)

                def spread(i, h):
                    dve.wait_ge(s_rank[h], i + 2)
                    dve.wait_ge(s_mv[h], i + 1)
                    dve.tensor_tensor(hot[:, h, :, :], over_mid(k.iota[:, :], G),
                                      over_last(k.psum[:, 4 + h, 0:G], P), ALU.is_equal).then_inc(s_hot[h], 1)

                def position(i, h, first, last):
                    compare(i, h)
                    if not first:
                        spread(*near(i, h, -1))

                in_rounds(dve, position)
                spread(R - 1, 1)
                for h in range(2):
                    dve.wait_ge(s_out[h], R + 1)
                decode(c, dve, k, order, out[:, :, 0], out[:, :, 1], a, w, b_, val, order.node)

            @block.tensor
            def _(pe):
                free(pe, *s_rank, *s_mv)
                pe.wait_ge(s_key, 1)

                def broadcast(i, h):
                    pe.wait_ge(s_less[h], i + 1)
                    for b in range(2):
                        pe.matmul(k.psum[:, 2 * h + b, :], k.ones16[0:1, :],
                                  over_mid(k.iota16[0:1, 0:P], 4), start=True, stop=False)
                        for u in range(4):
                            last = pe.matmul(k.psum[:, 2 * h + b, u * P:(u + 1) * P],
                                             node[:, ds(i * (2 * G) + (h * G + b * 4 + u), 1)].to_broadcast([P, P]),
                                             diag[:, :], start=False, stop=u == 3)
                    last.then_inc(s_bc[h], 1)

                def rank(i, h):
                    pe.wait_ge(s_less[h], i + 2)
                    pe.wait_ge(s_hot[h], i + 1)
                    for u in range(G):
                        last = pe.matmul(k.psum[:, 4 + h, u:u + 1], less[:, h, u, :], k.ones16[:, 0:1],
                                         start=True, stop=True)
                    last.then_inc(s_rank[h], 1)

                def move(i, h):
                    pe.wait_ge(s_hot[h], i + 2)
                    pe.wait_ge(s_out[h], i + 1)
                    for u in range(G):
                        last = pe.matmul(k.psum[:, 6 + h, 2 * u:2 * u + 2], hot[:, h, u, :],
                                         flat(k.pair[:, ds(i * (2 * G) + (h * G + u), 1), :]), start=True, stop=True)
                    last.then_inc(s_mv[h], 1)

                def position(i, h, first, last):
                    if not last:
                        broadcast(*near(i, h, 1))
                    rank(i, h)
                    if not first:
                        move(*near(i, h, -1))

                broadcast(0, 0)
                in_rounds(pe, position)
                move(R - 1, 1)

            @block.scalar
            def _(act):
                free(act, *s_out)
                with act.Fori(0, R) as i:
                    for h in range(2):
                        act.wait_ge(s_mv[h], i + 2)
                        act.nop(nofuse=True)
                        act.activation(flat(out[:, ds(i * (2 * G) + h * G, G), :]), k.psum[:, 6 + h, 0:2 * G],
                                       ACT.Copy).then_inc(s_out[h], 1)

        G2 = 16
        R2 = T // (2 * G2)
        s_tr, s_rows, s_flags, s_back, s_d2 = (sem(n) for n in ("s_tr", "s_rows", "s_flags", "s_back", "s_d2"))
        s_wide, s_oh, s_w, s_ohs, s_ws = (pair_of(n) for n in ("s_wide", "s_oh", "s_w", "s_ohs", "s_ws"))
        rows = sb("rows", [P, B, P], F32)
        first = sb("first", [P, B, P], F32)
        lastf = sb("lastf", [P, B, P], F32)
        ohb = sb("ohb", [P, 2, G2, P], BF16)
        ohs = sb("ohs", [P, 2, G2, P], BF16)
        with nc.Block() as block:
            @block.vector
            def _(dve):
                c = Chain(dve, s_d2)
                c.link(dve.tensor_copy(node[:, :], order.local[:, :]))
                dve.wait_ge(s_tr, B)
                for b in range(B):
                    last = dve.tensor_copy(rows[0:width[b], b, :], k.psum[0:width[b], b, 0:P])
                last.then_inc(s_rows, 1)
                dve.wait_ge(s_rows, 1)
                c.link(dve.memset(first[:, :, :], -BIG))
                c.link(dve.memset(lastf[:, :, :], 1.0))
                for b in range(B):
                    v = width[b]
                    c.link(dve.tensor_tensor(lastf[0:v, b, 0:P - 1], rows[0:v, b, 0:P - 1], rows[0:v, b, 1:P],
                                             ALU.not_equal))
                    c.link(dve.tensor_scalar(first[0:v, b, 1:P], lastf[0:v, b, 0:P - 1], -BIG, None, ALU.mult))
                dve.sem_inc(s_flags, 1)
                dve.wait_ge(s_back, 2 * B)
                for b in range(B):
                    v = width[b]
                    dve.tensor_copy(order.cut[:, b * P:b * P + v], k.psum[:, 4, b * P:b * P + v])
                    last = dve.tensor_copy(order.last[:, b * P:b * P + v], k.psum[:, 5, b * P:b * P + v])
                c.link(last)
                free(dve, *s_oh)
                with dve.Fori(0, R2) as i:
                    for h in range(2):
                        dve.wait_ge(s_wide[h], i + 1)
                        dve.wait_ge(s_w[h], i * 16 + 16)
                        dve.tensor_scalar(flat(ohb[:, h, :, :]), flat(k.psum[:, 4 * h:4 * h + 4, :]), k.iota_p[:, :],
                                          None, ALU.is_equal).then_inc(s_oh[h], 1)
                        dve.wait_ge(s_ws[h], i * 16 + 16)
                        dve.tensor_tensor(ohs[:, h, :, :], over_mid(k.iota[:, :], G2),
                                          over_last(order.local[:, ds(i * (2 * G2) + h * G2, G2)], P),
                                          ALU.is_equal).then_inc(s_ohs[h], 1)

            @block.tensor
            def _(pe):
                for b in range(B):
                    pe.transpose(k.psum[0:width[b], b, 0:P], order.local[:, b * P:b * P + width[b]],
                                 k.ident[:, :]).then_inc(s_tr, 1)
                pe.wait_ge(s_flags, 1)
                for b in range(B):
                    v = width[b]
                    pe.transpose(k.psum[:, 4, b * P:b * P + v], first[0:v, b, :], k.ident[0:v, 0:v]).then_inc(s_back, 1)
                    pe.transpose(k.psum[:, 5, b * P:b * P + v], lastf[0:v, b, :], k.ident[0:v, 0:v]).then_inc(s_back, 1)
                with pe.Fori(0, R2) as i:
                    for h in range(2):
                        pe.wait_ge(s_oh[h], i + 1)
                        for u in range(G2):
                            last = pe.matmul(k.psum[:, 4 * h + u // 4, (u % 4) * P:(u % 4 + 1) * P],
                                             node[:, ds(i * (2 * G2) + (h * G2 + u), 1)].to_broadcast([P, P]),
                                             ident16[:, :], start=True, stop=True)
                        last.then_inc(s_wide[h], 1)

            @block.sync
            def _(sp):
                free(sp, *s_w, *s_ws, by=16)
                with sp.Fori(0, R2) as i:
                    for h in range(2):
                        sp.wait_ge(s_oh[h], i + 2)
                        sp.dma_start(order.gather[:, ds(i * (2 * G2 * P) + h * (G2 * P), G2 * P)],
                                     flat(ohb[:, h, :, :])).then_inc(s_w[h], 16)
                        sp.wait_ge(s_ohs[h], i + 1)
                        sp.dma_start(order.scatter[:, ds(i * (2 * G2 * P) + h * (G2 * P), G2 * P)],
                                     flat(ohs[:, h, :, :])).then_inc(s_ws[h], 16)
                for h in range(2):
                    sp.wait_ge(s_w[h], R2 * 16 + 16)
                    sp.wait_ge(s_ws[h], R2 * 16 + 16)


class Kit:

    def __init__(self, nc, ctx, s):
        self.s = s

        def sb(n, shape, dt):
            return ctx.enter_context(nc.sbuf_tensor(n, shape, dt))

        self.sb = sb
        self.iota = sb("iota", [P, P], F32)
        self.iota16 = sb("iota16", [P, s.T], F16)
        self.iota_p = sb("iota_p", [P, 1], F32)
        self.ident = sb("ident", [P, P], F32)
        self.upto = sb("upto", [P, P], F16)
        self.ones16 = sb("ones16", [P, P], F16)
        self.zeros16 = sb("zeros16", [P, P], F16)
        self.ones = sb("ones", [P, P], F32)
        self.psum = ctx.enter_context(nc.psum_tensor("psum", [P, 8, 512], F32))
        self.s_got = [ctx.enter_context(nc.semaphore(f"s_got{q}")) for q in range(4)]
        self.got = 0
        self.s_iota = ctx.enter_context(nc.semaphore("s_iota"))
        self.s_const = ctx.enter_context(nc.semaphore("s_const"))


def banked(nc, k, name, chunks, produce, take):
    with ExitStack() as ctx:
        s_full = ctx.enter_context(signal(nc, f"{name}_full"))
        s_taken = [ctx.enter_context(signal(nc, f"{name}_taken{i}")) for i in range(2)]
        with nc.Block() as block:
            @block.tensor
            def _(pe):
                for c in range(chunks):
                    if c >= 8:
                        pe.wait_ge(s_taken[c % 2], (c - 8) // 2 + 1)
                    produce(pe, c, c % 8).then_inc(s_full, 1)

            @block.scalar
            def _(act):
                for c in range(0, chunks, 2):
                    act.wait_ge(s_full, c + 1)
                    take(lambda dst, src: act.activation(dst, src, ACT.Copy), c, c % 8).then_inc(s_taken[0], 1)

            @block.vector
            def _(dve):
                for c in range(1, chunks, 2):
                    dve.wait_ge(s_full, c + 1)
                    take(lambda dst, src: dve.tensor_copy(dst, src), c, c % 8).then_inc(s_taken[1], 1)


def chunked(n, size):
    return [(a, min(size, n - a)) for a in range(0, n, size)]


def transpose_all(nc, k, name, src, dst):
    parts = chunked(k.s.NT, 4)

    def produce(pe, c, bank):
        a, n = parts[c]
        for j in range(n):
            last = pe.transpose(k.psum[:, bank, j * P:(j + 1) * P], src[:, a + j, :], k.ident[:, :])
        return last

    def take(copy, c, bank):
        a, n = parts[c]
        return copy(dst[:, a * P:(a + n) * P], k.psum[:, bank, 0:n * P])

    banked(nc, k, name, len(parts), produce, take)


def untranspose_all(nc, k, name, src, dst):
    parts = chunked(k.s.NT, 4)

    def produce(pe, c, bank):
        a, n = parts[c]
        for j in range(n):
            last = pe.transpose(k.psum[:, bank, j * P:(j + 1) * P], src[:, (a + j) * P:(a + j + 1) * P],
                                k.ident[:, :])
        return last

    def take(copy, c, bank):
        a, n = parts[c]
        return copy(flat(dst[:, a:a + n, :]), k.psum[:, bank, 0:n * P])

    banked(nc, k, name, len(parts), produce, take)


def linear(nc, k, name, xs, ws, width, dst):
    per = 512 // width
    parts = chunked(k.s.NT, per)

    def produce(pe, c, bank):
        a, n = parts[c]
        for j in range(n):
            for q, (x, w) in enumerate(zip(xs, ws)):
                last = pe.matmul(k.psum[:, bank, j * width:(j + 1) * width], x[:, (a + j) * P:(a + j + 1) * P],
                                 w, start=q == 0, stop=q == len(xs) - 1)
        return last

    def take(copy, c, bank):
        a, n = parts[c]
        return copy(dst(a, n), k.psum[:, bank, 0:n * width].rearrange("p (a b) -> p a b", b=width))

    banked(nc, k, name, len(parts), produce, take)


def typed_linear(nc, k, name, x_t, w_d, out, silu=False):
    s = k.s
    types = w_d.shape[0]
    parts = chunked(s.NP, 512)
    with ExitStack() as ctx:
        w = ctx.enter_context(nc.sbuf_tensor(f"{name}_w", [P, types, D], F32))
        xm = ctx.enter_context(nc.sbuf_tensor(f"{name}_xm", [P, 2, s.NP], F32))
        s_w = ctx.enter_context(signal(nc, f"{name}_s_w"))
        s_xm = ctx.enter_context(signal(nc, f"{name}_s_xm"))
        s_mm = ctx.enter_context(signal(nc, f"{name}_s_mm"))
        s_sig = ctx.enter_context(signal(nc, f"{name}_s_sig"))
        acc = k.psum[:, :, :].rearrange("p a b -> p (a b)")[:, 0:s.NP]
        with nc.Block() as block:
            @block.sync
            def _(sp):
                sp.dma_start(w[:, :, :], w_d.rearrange("t i o -> i t o")).then_inc(s_w, 16)

            @block.vector
            def _(dve):
                for t in range(types):
                    if t >= 2:
                        dve.wait_ge(s_mm, t - 1)
                    dve.scalar_tensor_tensor(xm[:, t % 2, :], k.type_row[:, :], float(t), x_t[:, :],
                                             ALU.is_equal, ALU.mult).then_inc(s_xm, 1)
                if silu:
                    dve.wait_ge(s_sig, 1)
                    dve.tensor_tensor(out[:, :], xm[:, 0, :], acc, ALU.mult)

            @block.tensor
            def _(pe):
                pe.wait_ge(s_w, 16)
                for t in range(types):
                    pe.wait_ge(s_xm, t + 1)
                    for c, (a, n) in enumerate(parts):
                        last = pe.matmul(k.psum[:, c, 0:n], w[:, t, :], xm[:, t % 2, a:a + n],
                                         start=t == 0, stop=t == types - 1)
                    last.then_inc(s_mm, 1)

            @block.scalar
            def _(act):
                act.wait_ge(s_mm, types)
                if silu:
                    act.activation(xm[:, 0, :], acc, ACT.Sigmoid).then_inc(s_sig, 1)
                else:
                    act.activation(out[:, :], acc, ACT.Copy)


def layer_norm(nc, k, name, x, gain=None, shift=None):
    s = k.s
    NT = s.NT
    with ExitStack() as ctx:
        sq = ctx.enter_context(nc.sbuf_tensor(f"{name}_sq", [P, NT, D], F32))
        m = ctx.enter_context(nc.sbuf_tensor(f"{name}_m", [P, NT], F32))
        v = ctx.enter_context(nc.sbuf_tensor(f"{name}_v", [P, NT], F32))
        r = ctx.enter_context(nc.sbuf_tensor(f"{name}_r", [P, NT], F32))
        s_d = ctx.enter_context(signal(nc, f"{name}_s_d"))
        s_x = ctx.enter_context(signal(nc, f"{name}_s_x"))
        s_a = ctx.enter_context(signal(nc, f"{name}_s_a"))
        with nc.Block() as block:
            @block.vector
            def _(dve):
                c = Chain(dve, s_d)
                c.link(dve.tensor_reduce(m[:, :], x[:, :, :], AX.X, ALU.add))
                c.link(dve.tensor_scalar(m[:, :], m[:, :], 1.0 / D, None, ALU.mult))
                dve.tensor_tensor(x[:, :, :], x[:, :, :], over_last(m[:, :], D), ALU.subtract).then_inc(s_x, 1)
                dve.wait_ge(s_a, 1)
                c.link(dve.tensor_reduce(v[:, :], sq[:, :, :], AX.X, ALU.add))
                dve.tensor_scalar(v[:, :], v[:, :], 1.0 / D, LN_EPS, ALU.mult, ALU.add).then_inc(s_x, 1)
                dve.wait_ge(s_a, 2)
                c.link(dve.reciprocal(r[:, :], r[:, :]))
                c.link(dve.tensor_tensor(x[:, :, :], x[:, :, :], over_last(r[:, :], D), ALU.mult))
                if gain is not None:
                    c.link(dve.tensor_tensor(x[:, :, :], x[:, :, :], over_mid(gain, NT), ALU.mult))
                    c.link(dve.tensor_tensor(x[:, :, :], x[:, :, :], over_mid(shift, NT), ALU.add))

            @block.scalar
            def _(act):
                act.wait_ge(s_x, 1)
                act.activation(sq[:, :, :], x[:, :, :], ACT.Square).then_inc(s_a, 1)
                act.wait_ge(s_x, 2)
                act.activation(r[:, :], v[:, :], ACT.Sqrt).then_inc(s_a, 1)


GRP = 4
RND = 4


def tile_registers(eng, n, name):
    return [eng.alloc_register(f"{name}{u}") for u in range(n)]


def load_tiles(eng, order, regs, t0, tiles):
    eng.load(regs, order.tile[0:1, ds(t0, len(regs))])
    return [eng.snap(r, min_val=0, max_val=tiles - 1) for r in regs]


def attend_rows(nc, k, name, order, rows, table, width, score, at, heads, queries, peaks, acc):
    s = k.s
    NT = s.NT
    TG = GRP * RND
    R = s.T // TG
    qw = D if score == "dot" else heads
    lo, hi = at
    F = hi - lo
    FW = F + heads
    W1 = heads + 1
    lanes = TG * heads
    Q_BANK, MAX_BANK, PEAK_BANK, SUM_BANK = 0, 2, 3, 4
    SUBTRACT, WEIGH, ADD = 7, 8, 9
    PEAK, SCATTER = 8, 10
    KEEP, EXP = 3, 10
    AGAIN = 6
    EARLY = 4
    assert R % 2 == 0
    with ExitStack() as ctx:
        def sb(n, shape, dt):
            return ctx.enter_context(nc.sbuf_tensor(f"{name}_{n}", shape, dt))

        def sem(n):
            return ctx.enter_context(signal(nc, f"{name}_{n}"))

        def sems(n):
            return [sem(f"{n}{q}") for q in range(RND)]

        got = sb("got", [P, RND, GRP, width], F32)
        idx = sb("idx", [P, RND, GRP], I32)
        hot_q = sb("hot_q", [P, RND, GRP * P], BF16)
        hot_p = sb("hot_p", [P, RND, GRP * P], BF16)
        hot16 = sb("hot16", [P, 2, TG, P], BF16)
        hot = sb("hot", [P, 2, TG, P], F32)
        msg = sb("msg", [P, 2, RND, GRP, F], F32)
        prod = sb("prod", [P, 2, GRP * qw], F32)
        scores = sb("scores", [P, s.T * heads], F32)
        cut = sb("cut", [P, lanes], F32)
        stat = sb("stat", [P, lanes], F32)
        cut_t = sb("cut_t", [lanes, P], F32)
        run = sb("run", [lanes, P], F32)
        tail = sb("tail", [P, TG * W1], F32)
        tail3 = sb("tail3", [P, 3, TG * W1], BF16)
        gone = sb("gone", [P, TG], F32)
        best = sb("best", [P, TG, heads], F32)
        old = sb("old", [P, NT * heads], F32)
        odd = sb("odd", [P, NT * heads], F32)
        rest = sb("rest", [P, NT * heads], F32)
        gap = sb("gap", [P, NT * heads], F32)
        factor = sb("factor", [P, NT * heads], F32)
        peaks3 = sb("peaks3", [P, 3, NT * heads], BF16)
        diff = sb("diff", [P, RND, GRP * heads], F32)
        below = sb("below", [P, RND, GRP * heads], F32)
        wtd = sb("wtd", [P, RND, GRP, FW], F32)
        s_idx, s_hot, s_again, s_q, s_pk, s_used, s_kept, s_diff, s_exp, s_wtd = (sems(n) for n in (
            "s_idx", "s_hot", "s_again", "s_q", "s_pk", "s_used", "s_kept", "s_diff", "s_exp", "s_wtd"))
        s_sum, s_acc = (sems(n) for n in ("s_sum", "s_acc"))
        s_d, s_scored, s_tr, s_pre, s_cut, s_run, s_back, s_tail, s_mv, s_best, s_rise, s_p3, s_gap, s_fac, s_scaled, \
            s_below, s_wide, s_old, s_hot16 = (sem(n) for n in (
                "s_d", "s_scored", "s_tr", "s_pre", "s_cut", "s_run", "s_back", "s_tail", "s_mv", "s_best", "s_rise",
                "s_p3", "s_gap", "s_fac", "s_scaled", "s_below", "s_wide", "s_old", "s_hot16"))
        s_got, had = k.s_got, k.got
        k.got += R * 16 * GRP

        def back(r, b, q, lag):
            n = q - lag
            return r + n // RND, (b + n // RND) % 2, n % RND

        def here(r):
            return not isinstance(r, int) or 0 <= r < R

        def load_round(eng, regs, r, first):
            if not isinstance(r, int):
                eng.load(regs, order.tile[0:1, ds((r * RND + first) * GRP, TG)])
            else:
                groups = [(q, r * RND + first + q) for q in range(RND)]
                for q, g in groups:
                    if 0 <= g < R * RND:
                        eng.load(regs[q * GRP:(q + 1) * GRP], order.tile[0:1, ds(g * GRP, GRP)])

        def loaded(eng, regs, place, n=GRP):
            return [eng.snap(r, min_val=0, max_val=NT - 1) for r in regs[place * n:(place + 1) * n]]

        def in_rounds(eng, position, behind, links=None):
            for r in range(EARLY):
                for q in range(RND):
                    position(r, r % 2, q)
            if links:
                links[0].enter(0, 2 * links[1])
            with eng.Fori(EARLY // 2, R // 2) as i:
                if links:
                    links[0].offset = (i - EARLY // 2) * (2 * links[1])
                for b in range(2):
                    for q in range(RND):
                        position(i * 2 + b, b, q)
            if links:
                links[0].leave((R - EARLY) // 2)
            for r in range(R, R + behind):
                for q in range(RND):
                    position(r, r % 2, q)

        with nc.Block() as block:
            @block.scalar
            def _(act):
                free(act, *s_exp, s_fac, s_wide)

                def indices(r, q):
                    if here(r):
                        act.wait_ge(s_used[q], r + 1)
                        act.activation(idx[:, q, :], rows[:, ds((r * RND + q) * GRP, GRP)], ACT.Copy).then_inc(s_idx[q], 1)

                def keep(r, b, q):
                    if here(r):
                        act.wait_ge(s_got[q], r * (16 * GRP) + (had + 16 * GRP))
                        act.wait_ge(s_wtd[q], r + 1)
                        act.activation(msg[:, b, q, :, :], got[:, q, :, lo:hi], ACT.Copy).then_inc(s_kept[q], 1)

                def columns(r):
                    if here(r):
                        act.wait_ge(s_scored, r * RND + RND)
                        act.wait_ge(s_tr, r + 1)
                        act.nop(nofuse=True)
                        act.activation(cut[:, :].rearrange("p (a b) -> p a b", b=heads),
                                       over_last(order.cut[:, ds(r * TG, TG)], heads), ACT.Copy)
                        act.activation(stat[:, :], scores[:, ds(r * lanes, lanes)], ACT.Copy).then_inc(s_pre, 1)

                def cuts(r):
                    if here(r):
                        act.wait_ge(s_tr, r + 2)
                        act.wait_ge(s_run, r + 1)
                        act.activation(cut_t[:, :], k.psum[0:lanes, MAX_BANK, 0:P], ACT.Copy).then_inc(s_cut, 1)

                def remember(r):
                    if here(r):
                        act.wait_ge(s_p3, r + 1)
                        act.activation(old[:, :], flat(peaks[:, :, :]), ACT.Copy)
                        act.activation(odd[:, :], flat(peaks[:, :, :]), ACT.Copy).then_inc(s_old, 1)

                def widen(r, b):
                    if here(r):
                        act.wait_ge(s_hot16, r * 16 + 16)
                        if not (isinstance(r, int) and r == 0):
                            act.wait_ge(s_sum[GRP - 1], r * RND)
                        act.activation(hot[:, b, :, :], hot16[:, b, :, :], ACT.Copy).then_inc(s_wide, 1)

                def factors(r):
                    if here(r):
                        act.wait_ge(s_gap, r + 1)
                        act.wait_ge(s_scaled, r * 2 + 1)
                        act.activation(factor[:, :], gap[:, :], ACT.Exp).then_inc(s_fac, 1)

                def weights(r, b, q):
                    if here(r):
                        act.wait_ge(s_diff[q], r + 2)
                        act.activation(below[:, q, :], diff[:, q, :], ACT.Relu, scale=-1.0).then_inc(s_below, 1)
                        act.wait_ge(s_below, r * RND + (q + 1))
                        act.wait_ge(s_sum[GRP - 1], r * RND + (q + 1))
                        act.activation(wtd[:, q, :, F:FW], below[:, q, :].rearrange("p (a b) -> p a b", a=GRP),
                                       ACT.Exp, scale=-1.0).then_inc(s_exp[q], 1)

                def position(r, b, q):
                    if q == RND - 1:
                        columns(r - 1)
                    if q == RND - 2:
                        remember(r - 2)
                        factors(r - 2)
                    indices(r, q)
                    weights(*back(r, b, q, EXP))
                    keep(*back(r, b, q, KEEP))
                    if q == RND - 1:
                        cuts(r - 1)
                        widen(r - 1, 1 - b)

                act.activation(old[:, :], flat(peaks[:, :, :]), ACT.Copy)
                act.activation(odd[:, :], flat(peaks[:, :, :]), ACT.Copy).then_inc(s_old, 1)
                in_rounds(act, position, 3)

            @block.gpsimd
            def _(pool):
                with pool.Fori(0, R) as i:
                    for q in range(RND):
                        pool.wait_ge(s_idx[q], i + 1)
                        pool.wait_ge(s_used[q], i + 1)
                        pool.wait_ge(s_kept[q], i + 1)
                        pool.nop(nofuse=True)
                        for u in range(GRP):
                            pool.indirect_dma_start(
                                got[:, q, u, :], None, table[:, :],
                                bass.IndirectOffsetOnAxis(ap=idx[:, q, u:u + 1], axis=0)).then_inc(s_got[q], 16)

            @block.sync
            def _(sp):
                def one_hots(r, q, buffer, used, ready):
                    if here(r):
                        sp.wait_ge(used[q], r + 1)
                        sp.dma_start(buffer[:, q, :], order.gather[:, ds((r * RND + q) * (GRP * P), GRP * P)])\
                            .then_inc(ready[q], 16)

                def one_hots_by_slot(r, b):
                    if here(r):
                        if not (isinstance(r, int) and r < 2):
                            sp.wait_ge(s_mv, r - 1)
                            sp.wait_ge(s_wide, r)
                        sp.dma_start(flat(hot16[:, b, :, :]), order.scatter[:, ds(r * (TG * P), TG * P)]).then_inc(s_hot16, 16)

                def position(r, b, q):
                    if q == 3:
                        one_hots_by_slot(r, b)
                    one_hots(r, q, hot_q, s_q, s_hot)
                    late, _, place = back(r, b, q, AGAIN)
                    one_hots(late, place, hot_p, s_pk, s_again)

                in_rounds(sp, position, 2)

            @block.tensor
            def _(pe):
                free(pe, *s_q, *s_pk, s_tr)
                free(pe, *s_sum, by=RND)
                q_regs = tile_registers(pe, TG, f"{name}_q")
                p_regs = tile_registers(pe, TG, f"{name}_p")
                def query(r, q):
                    if here(r):
                        tiles = loaded(pe, q_regs, q)
                        pe.wait_ge(s_hot[q], r * 16 + 16)
                        pe.wait_ge(s_used[(q - 2) % RND], r + (2 if q >= 2 else 1))
                        for u in range(GRP):
                            for part in range(3):
                                last = pe.matmul(k.psum[:, Q_BANK + q % 2, u * qw:(u + 1) * qw],
                                                 hot_q[:, q, u * P:(u + 1) * P],
                                                 queries[:, part, ds(tiles[u] * qw, qw)],
                                                 start=part == 0, stop=part == 2)
                        last.then_inc(s_q[q], 1)

                def to_rows(r):
                    if here(r):
                        pe.wait_ge(s_pre, r + 1)
                        pe.wait_ge(s_best, r + 1)
                        pe.nop(nofuse=True)
                        pe.transpose(k.psum[0:lanes, MAX_BANK, 0:P], cut[:, :], k.ident[:, :])
                        pe.transpose(k.psum[0:lanes, MAX_BANK, P:2 * P], stat[:, :], k.ident[:, :]).then_inc(s_tr, 1)

                def to_columns(r):
                    if here(r):
                        pe.wait_ge(s_run, r + 2)
                        pe.nop(nofuse=True)
                        pe.transpose(k.psum[:, MAX_BANK, 2 * P:2 * P + lanes], run[:, :],
                                     k.ident[0:lanes, 0:lanes]).then_inc(s_back, 1)

                def to_nodes(r, b):
                    if here(r):
                        pe.wait_ge(s_hot16, r * 16 + 16)
                        pe.wait_ge(s_tail, r + 1)
                        for u in range(TG):
                            for part in range(3):
                                last = pe.matmul(k.psum[:, MAX_BANK, u * W1:(u + 1) * W1], hot16[:, b, u, :],
                                                 tail3[:, part, u * W1:(u + 1) * W1], start=part == 0, stop=part == 2)
                        last.then_inc(s_mv, 1)

                def peak(r, b, q):
                    if here(r):
                        tiles = loaded(pe, p_regs, q)
                        pe.wait_ge(s_again[q], r * 16 + 16)
                        pe.wait_ge(s_p3, r + 1)
                        pe.wait_ge(s_diff[(q - 1) % RND], r + (2 if q >= 1 else 1))
                        for u in range(GRP):
                            for part in range(3):
                                last = pe.matmul(k.psum[:, PEAK_BANK, u * heads:(u + 1) * heads],
                                                 hot_p[:, q, u * P:(u + 1) * P],
                                                 peaks3[:, part, ds(tiles[u] * heads, heads)],
                                                 start=part == 0, stop=part == 2)
                        last.then_inc(s_pk[q], 1)

                def scatter(r, b, q):
                    if here(r):
                        pe.wait_ge(s_wtd[q], r + 3)
                        pe.wait_ge(s_wide, r + 2)
                        for u in range(GRP):
                            pe.wait_ge(s_acc[u], r * RND + (q + 1))
                            pe.matmul(k.psum[:, SUM_BANK + u, 0:FW], hot[:, b, q * GRP + u, :], wtd[:, q, u, :],
                                      start=True, stop=True).then_inc(s_sum[u], 1)

                def position(r, b, q):
                    if q == 0:
                        load_round(pe, q_regs, r, 0)
                        load_round(pe, p_regs, r, -PEAK)
                        scatter(*back(r, b, q, SCATTER))
                        query(r, q)
                        peak(*back(r, b, q, PEAK))
                    if q == 1:
                        scatter(*back(r, b, q, SCATTER))
                        peak(*back(r, b, q, PEAK))
                        to_rows(r - 1)
                        query(r, q)
                    if q == 2:
                        peak(*back(r, b, q, PEAK))
                        query(r, q)
                        to_columns(r - 1)
                        scatter(*back(r, b, q, SCATTER))
                    if q == 3:
                        to_nodes(r - 1, 1 - b)
                        peak(*back(r, b, q, PEAK))
                        query(r, q)
                        scatter(*back(r, b, q, SCATTER))

                in_rounds(pe, position, 3)

            @block.vector
            def _(dve):
                free(dve, *s_used, *s_kept, *s_diff, *s_acc, s_run, s_best, s_scaled)
                for q in range(RND):
                    dve.sem_inc(s_wtd[q], 2)
                c = Chain(dve, s_d)
                rise_regs = tile_registers(dve, TG, f"{name}_rise")
                add_regs = tile_registers(dve, TG, f"{name}_add")
                tile_of_add = [None]

                def multiplied(r, q):
                    if here(r):
                        dve.wait_ge(s_got[q], r * (16 * GRP) + (had + 16 * GRP))
                        dve.wait_ge(s_q[q], r + 2)
                        ps = k.psum[:, Q_BANK + q % 2, 0:GRP * qw].rearrange("p (a b) -> p a b", a=GRP)
                        pr = prod[:, q % 2, :].rearrange("p (a b) -> p a b", a=GRP)
                        if score == "dot":
                            dve.tensor_tensor(pr, got[:, q, :, 0:D], ps, ALU.mult).then_inc(s_used[q], 1)
                        else:
                            dve.tensor_tensor(pr, got[:, q, :, width - heads:width], ps, ALU.add).then_inc(s_used[q], 1)

                def scored(r, q):
                    if here(r):
                        to = scores[:, ds((r * RND + q) * (GRP * heads), GRP * heads)]
                        pr = prod[:, q % 2, :]
                        dve.wait_ge(s_used[q], r + 2)
                        if score == "dot":
                            last = dve.tensor_reduce(to, pr.rearrange("p (a b) -> p a b", b=D // heads), AX.X, ALU.add)
                        else:
                            last = dve.scalar_tensor_tensor(to, pr, NEG_SLOPE, pr, ALU.mult, ALU.max)
                        last.then_inc(s_scored, 1)

                def scan(r):
                    if here(r):
                        dve.wait_ge(s_tr, r + 2)
                        dve.wait_ge(s_cut, r + 1)
                        dve.tensor_tensor_scan(run[:, :], cut_t[:, :], k.psum[0:lanes, MAX_BANK, P:2 * P], -BIG,
                                               ALU.add, ALU.max).then_inc(s_run, 1)

                def split3(src, rest, parts):
                    for part in range(2):
                        c.link(dve.tensor_copy(parts[:, part, :], src))
                        c.link(dve.tensor_tensor(rest, src, parts[:, part, :], ALU.subtract))
                        src = rest
                    return dve.tensor_copy(parts[:, 2, :], src)

                def tails(r):
                    if here(r):
                        g = ds(r * TG, TG)
                        dve.wait_ge(s_back, r + 1)
                        tail_3d = tail[:, :].rearrange("p (a b) -> p a b", b=W1)
                        dve.tensor_tensor(tail_3d[:, :, 0:heads],
                                          k.psum[:, MAX_BANK, 2 * P:2 * P + lanes].rearrange("p (a b) -> p a b", b=heads),
                                          over_last(order.last[:, g], heads), ALU.mult)
                        c.link(dve.tensor_scalar(tail_3d[:, :, heads:W1], order.last[:, g].unsqueeze(2), 1.0, None, ALU.mult))
                        split3(tail[:, :], tail[:, :], tail3).then_inc(s_tail, 1)

                def moved(r):
                    if here(r):
                        dve.wait_ge(s_mv, r + 1)
                        at_nodes = k.psum[:, MAX_BANK, 0:TG * W1].rearrange("p (a b) -> p a b", b=W1)
                        c.link(dve.tensor_scalar(gone[:, :].unsqueeze(2), at_nodes[:, :, heads:W1], -1.0, BIG,
                                                 ALU.add, ALU.mult))
                        dve.tensor_tensor(best[:, :, :], at_nodes[:, :, 0:heads], over_last(gone[:, :], heads),
                                          ALU.add).then_inc(s_best, 1)
                        dve.wait_ge(s_old, r + 1)
                        dve.wait_ge(s_best, r + 2)

                def rise(r, pair):
                    if here(r):
                        for u in (2 * pair, 2 * pair + 1):
                            node_tile, = loaded(dve, rise_regs, u, 1)
                            to = (flat(peaks[:, :, :]), odd)[u % 2][:, ds(node_tile * heads, heads)]
                            if u > 1:
                                dve.wait_ge(s_rise, r * TG + (u - 1))
                            dve.tensor_tensor(to, to, best[:, u, :], ALU.max).then_inc(s_rise, 1)

                def split(r):
                    if here(r):
                        now = flat(peaks[:, :, :])
                        dve.wait_ge(s_rise, r * TG + TG)
                        c.link(dve.tensor_tensor(now, now, odd[:, :], ALU.max))
                        dve.wait_ge(s_fac, r + 1)
                        dve.tensor_tensor(gap[:, :], old[:, :], now, ALU.subtract).then_inc(s_gap, 1)
                        dve.wait_ge(s_pk[RND - 1], r + 1)
                        split3(now, rest[:, :], peaks3).then_inc(s_p3, 1)

                def rescale(r):
                    if here(r):
                        dve.wait_ge(s_fac, r + 2)
                        dve.wait_ge(s_acc[GRP - 1], r * RND + 1)
                        acc3 = acc.rearrange("p (t c) -> p t c", c=FW)
                        f3 = factor[:, :].rearrange("p (t h) -> p t h", h=heads)
                        dve.tensor_tensor(acc3[:, :, F:FW], acc3[:, :, F:FW], f3, ALU.mult).then_inc(s_scaled, 1)
                        sums = acc3[:, :, 0:F].rearrange("p t (h c) -> p t h c", h=heads)
                        dve.tensor_tensor(sums, sums, f3.unsqueeze(3).to_broadcast([P, NT, heads, F // heads]),
                                          ALU.mult).then_inc(s_scaled, 1)

                def subtract(r, b, q):
                    if here(r):
                        dve.wait_ge(s_pk[q], r + 2)
                        dve.wait_ge(s_exp[q], r + 1)
                        dve.tensor_tensor(diff[:, q, :], scores[:, ds((r * RND + q) * (GRP * heads), GRP * heads)],
                                          k.psum[:, PEAK_BANK, 0:GRP * heads], ALU.subtract).then_inc(s_diff[q], 1)

                def weigh(r, b, q):
                    if here(r):
                        dve.wait_ge(s_exp[q], r + 2)
                        dve.wait_ge(s_kept[q], r + 2)
                        dve.tensor_tensor(
                            wtd[:, q, :, 0:F].rearrange("p g (a b) -> p g a b", a=heads),
                            msg[:, b, q, :, :].rearrange("p g (a b) -> p g a b", a=heads),
                            wtd[:, q, :, F:FW].unsqueeze(3).to_broadcast([P, GRP, heads, F // heads]),
                            ALU.mult).then_inc(s_wtd[q], 1)

                def add(r, q, u):
                    if here(r):
                        if u == 0:
                            tile_of_add[:] = loaded(dve, add_regs, q)
                            dve.wait_ge(s_scaled, r * 2 + 3)
                        to = acc[:, ds(tile_of_add[u] * FW, FW)]
                        dve.wait_ge(s_sum[u], r * RND + (q + RND + 1))
                        dve.wait_ge(s_acc[(u - 1) % GRP], r * RND + (q + 1 if u < 1 else q + 2))
                        dve.tensor_tensor(to, to, k.psum[:, SUM_BANK + u, 0:FW], ALU.add).then_inc(s_acc[u], 1)

                def position(r, b, q):
                    ra, _, qa = back(r, b, q, ADD)

                    def between(pair):
                        if q == 2:
                            rise(r - 1, pair)

                    if q == 1:
                        tails(r - 1)
                    if q == 2:
                        moved(r - 1)
                    if q in (1, 2):
                        subtract(*back(r, b, q, SUBTRACT))
                    between(0)
                    multiplied(r, q)
                    between(1)
                    add(ra, qa, 0)
                    between(2)
                    weigh(*back(r, b, q, WEIGH))
                    between(3)
                    add(ra, qa, 1)
                    between(4)
                    scored(r, q)
                    between(5)
                    add(ra, qa, 2)
                    between(6)
                    if q in (3, 0):
                        subtract(*back(r, b, q, SUBTRACT))
                    add(ra, qa, 3)
                    between(7)
                    if q == 0:
                        scan(r - 1)
                        rescale(r - 2)
                        load_round(dve, add_regs, r, 1 - ADD)
                        load_round(dve, rise_regs, r - 1, 0)
                    if q == 2:
                        split(r - 1)

                in_rounds(dve, position, 3, (c, 11))


def gather_sum(nc, k, name, order, rows, table, width, acc):
    s = k.s
    rounds = s.T // (GRP * RND)
    with ExitStack() as ctx:
        def sb(n, shape, dt):
            return ctx.enter_context(nc.sbuf_tensor(f"{name}_{n}", shape, dt))

        def sems(n, m=RND):
            return [ctx.enter_context(signal(nc, f"{name}_{n}{q}")) for q in range(m)]

        got = sb("got", [P, RND, GRP, width], F32)
        idx = sb("idx", [P, RND, GRP], I32)
        hot = sb("hot", [P, RND, GRP, P], F32)
        s_idx, s_hot, s_used = (sems(n) for n in ("s_idx", "s_hot", "s_used"))
        s_got, had = k.s_got, k.got
        k.got += rounds * 16 * GRP
        s_acc = sems("s_acc", GRP)
        with nc.Block() as block:
            @block.scalar
            def _(act):
                with act.Fori(0, rounds) as i:
                    for q in range(RND):
                        act.wait_ge(s_used[q], i + 1)
                        act.activation(idx[:, q, :], rows[:, ds((i * RND + q) * GRP, GRP)],
                                       ACT.Copy).then_inc(s_idx[q], 1)

            @block.gpsimd
            def _(pool):
                with pool.Fori(0, rounds) as i:
                    for q in range(RND):
                        pool.wait_ge(s_idx[q], i + 1)
                        pool.wait_ge(s_used[q], i + 1)
                        pool.nop(nofuse=True)
                        for u in range(GRP):
                            pool.indirect_dma_start(
                                got[:, q, u, :], None, table[:, :],
                                bass.IndirectOffsetOnAxis(ap=idx[:, q, u:u + 1], axis=0)).then_inc(s_got[q], 16)

            @block.tensor
            def _(pe):
                free(pe, *s_used)
                with pe.Fori(0, rounds) as i:
                    for q in range(RND):
                        pe.wait_ge(s_got[q], i * (16 * GRP) + (had + 16 * GRP))
                        pe.wait_ge(s_hot[q], i + 1)
                        for u in range(GRP):
                            pe.wait_ge(s_acc[u], i * RND + (q + 1))
                            last = pe.matmul(k.psum[:, u, 0:width], hot[:, q, u, :], got[:, q, u, :],
                                             start=True, stop=True)
                        last.then_inc(s_used[q], 1)

            @block.vector
            def _(dve):
                free(dve, *s_acc)
                regs = tile_registers(dve, GRP * RND, f"{name}_dve")
                with dve.Fori(0, rounds) as i:
                    node_tile = load_tiles(dve, order, regs, i * (GRP * RND), s.NT)
                    for q in range(RND):
                        g0 = (i * RND + q) * GRP
                        dve.wait_ge(s_used[q], i + 1)
                        dve.tensor_tensor(hot[:, q, :, :], over_mid(k.iota[:, :], GRP),
                                          over_last(order.local[:, ds(g0, GRP)], P), ALU.is_equal).then_inc(s_hot[q], 1)
                    for q in range(RND):
                        for u in range(GRP):
                            at = acc[:, u % 2, ds(node_tile[q * GRP + u] * width, width)]
                            dve.wait_ge(s_used[q], i + 2)
                            dve.wait_ge(s_acc[(u - 2) % GRP], i * RND + (q + 1 if u < 2 else q + 2))
                            dve.tensor_tensor(at, at, k.psum[:, u, 0:width], ALU.add).then_inc(s_acc[u], 1)


NEG_SLOPE = 0.2


def load_rows(nc, k, name, pairs, fill=()):
    with ExitStack() as ctx:
        s_in = ctx.enter_context(signal(nc, f"{name}_s_in"))
        with nc.Block() as block:
            @block.sync
            def _(sp):
                for dst, src in pairs:
                    sp.dma_start(dst, src).then_inc(s_in, 16)
                sp.wait_ge(s_in, 16 * len(pairs))

            @block.vector
            def _(dve):
                for where, value in fill:
                    dve.memset(where, value)


def row_bcast(vec):
    return vec.unsqueeze(0).to_broadcast([P, vec.shape[0]])


def steps(nc, name, body):
    with ExitStack() as ctx:
        s_d = ctx.enter_context(signal(nc, f"{name}_s_d"))
        with nc.Block() as block:
            @block.vector
            def _(dve):
                body(Chain(dve, s_d).link, dve)


def relation_weights(nc, k, name, w_d, pri_d, out, pri):
    heads, rels, hs = w_d.shape[0], w_d.shape[1], w_d.shape[2]
    with ExitStack() as ctx:
        s_z = ctx.enter_context(signal(nc, f"{name}_s_z"))
        s_in = ctx.enter_context(signal(nc, f"{name}_s_in"))
        s_d = ctx.enter_context(signal(nc, f"{name}_s_d"))
        n_in = 16 * heads * (2 if pri is not None else 1)
        with nc.Block() as block:
            @block.vector
            def _(dve):
                dve.memset(out[:, :, :], 0.0).then_inc(s_z, 1)
                if pri is not None:
                    c = Chain(dve, s_d)
                    dve.wait_ge(s_in, n_in)
                    c.link(dve.tensor_scalar(pri[:, :], pri[:, :], 1.0 / float(np.sqrt(hs)), None, ALU.mult))
                    c.link(dve.tensor_tensor(out[:, :, :], out[:, :, :], over_last(pri[:, :], D), ALU.mult))

            @block.sync
            def _(sp):
                sp.wait_ge(s_z, 1)
                for h in range(heads):
                    at = slice(h * hs, (h + 1) * hs)
                    sp.dma_start(out[at, :, at], w_d[h].rearrange("r i o -> i r o")).then_inc(s_in, 16)
                    if pri is not None:
                        sp.dma_start(pri[at, :], pri_d[h].unsqueeze(0).to_broadcast([hs, rels])).then_inc(s_in, 16)
                sp.wait_ge(s_in, n_in)


def relation_table(nc, k, name, k_t, v_t, wk, wv, table):
    s = k.s
    rels = wk.shape[1]
    half = rels // 2
    rows = table.rearrange("(n r) c -> n r c", r=rels)
    with ExitStack() as ctx:
        out = ctx.enter_context(nc.sbuf_tensor(f"{name}_out", [P, 2, rels, 2 * D], F32))
        s_mm = ctx.enter_context(signal(nc, f"{name}_s_mm"))
        s_a = ctx.enter_context(signal(nc, f"{name}_s_a"))
        s_v = ctx.enter_context(signal(nc, f"{name}_s_v"))
        s_st = [ctx.enter_context(signal(nc, f"{name}_s_st{i}")) for i in range(2)]
        with nc.Block() as block:
            @block.tensor
            def _(pe):
                for j in range(s.NT):
                    if j >= 2:
                        pe.wait_ge(s_a, j - 1)
                        pe.wait_ge(s_v, j - 1)
                    for b in range(4):
                        x, w = ((k_t, wk), (v_t, wv))[b // 2]
                        last = pe.matmul(k.psum[:, 4 * (j % 2) + b, :], x[:, j * P:(j + 1) * P],
                                         flat(w[:, (b % 2) * half:(b % 2 + 1) * half, :]), start=True, stop=True)
                    last.then_inc(s_mm, 1)

            def empty(eng, j, side, copy):
                eng.wait_ge(s_mm, j + 1)
                if j >= 2:
                    eng.wait_ge(s_st[j % 2], 16 * (j // 2))
                b0 = 4 * (j % 2) + 2 * side
                return copy(out[:, j % 2, :, side * D:(side + 1) * D],
                            k.psum[:, b0:b0 + 2, :].rearrange("p a (r c) -> p (a r) c", c=D))

            @block.scalar
            def _(act):
                for j in range(s.NT):
                    empty(act, j, 0, lambda d, x: act.activation(d, x, ACT.Copy)).then_inc(s_a, 1)

            @block.vector
            def _(dve):
                for j in range(s.NT):
                    empty(dve, j, 1, lambda d, x: dve.tensor_copy(d, x)).then_inc(s_v, 1)

            @block.sync
            def _(sp):
                for j in range(s.NT):
                    sp.wait_ge(s_a, j + 1)
                    sp.wait_ge(s_v, j + 1)
                    sp.dma_start(rows[j * P:(j + 1) * P, :, :], out[:, j % 2, :, :]).then_inc(s_st[j % 2], 16)
                sp.wait_ge(s_st[0], 16 * ((s.NT + 1) // 2))
                sp.wait_ge(s_st[1], 16 * (s.NT // 2))


def store_table(nc, k, name, src, table, fill=()):
    load_rows(nc, k, name, [(table.rearrange("(t p) c -> p t c", p=P), src)], fill)


def graph_transformer(nc, k, l, X, order, W, table):
    s = k.s
    NT, NP = s.NT, s.NP
    heads, rels = W["pri"].shape[1], W["pri"].shape[2]
    FW = D + heads
    n = f"g{l}"
    with ExitStack() as outer:
        def sb(nm, shape, dt, where=outer):
            return where.enter_context(nc.sbuf_tensor(f"{n}_{nm}", shape, dt))

        peaks = sb("peaks", [P, NT, heads], F32)
        acc = sb("acc", [P, NT * FW], F32)
        with ExitStack() as ctx:
            q3 = sb("q3", [P, 3, NP], BF16, ctx)
            with ExitStack() as c2:
                x_t = sb("x_t", [P, NP], F32, c2)
                k_t = sb("k_t", [P, NP], F32, c2)
                v_t = sb("v_t", [P, NP], F32, c2)
                transpose_all(nc, k, f"{n}_xt", X, x_t)
                typed_linear(nc, k, f"{n}_k", x_t, W["Wk"][l], k_t)
                typed_linear(nc, k, f"{n}_v", x_t, W["Wv"][l], v_t)
                with ExitStack() as c3:
                    wk = sb("wk", [P, rels, D], F32, c3)
                    wv = sb("wv", [P, rels, D], F32, c3)
                    pri = sb("pri", [P, rels], F32, c3)
                    relation_weights(nc, k, f"{n}_wk", W["Watt"][l], W["pri"][l], wk, pri)
                    relation_weights(nc, k, f"{n}_wv", W["Wmsg"][l], None, wv, None)
                    relation_table(nc, k, f"{n}_tab", k_t, v_t, wk, wv, table)
                typed_linear(nc, k, f"{n}_q", x_t, W["Wq"][l], k_t)
                q = v_t[:, :].rearrange("p (a b) -> p a b", b=D)
                untranspose_all(nc, k, f"{n}_qn", k_t, q)
                steps(nc, f"{n}_q3", lambda link, dve: split3_steps(link, dve, v_t[:, :], [q3[:, j, :] for j in range(3)], k_t[:, :]))

            def clear(link, dve):
                link(dve.memset(peaks[:, :, :], -BIG))
                link(dve.memset(acc[:, :], 0.0))
            steps(nc, f"{n}_clear", clear)
            attend_rows(nc, k, f"{n}_e", order, order.row, table, 2 * D, "dot", (D, 2 * D), heads, q3, peaks, acc)
        with ExitStack() as ctx:
            agg = sb("agg", [P, NT, D], F32, ctx)
            a_t = sb("a_t", [P, NP], F32, ctx)
            o_t = sb("o_t", [P, NP], F32, ctx)
            den = sb("den", [P, NT * heads], F32, ctx)
            al = sb("al", [P, NT], F32, ctx)
            sk = sb("sk", [P, rels], F32, ctx)
            gain = sb("gain", [P, 2, D], F32, ctx)
            load_rows(nc, k, f"{n}_ld", [(sk[:, :], row_bcast(W["skip"][l])), (gain[:, 0, :], row_bcast(W["ln_g"][l])),
                                         (gain[:, 1, :], row_bcast(W["ln_b"][l]))])

            def normalise(link, dve):
                a3 = acc[:, :].rearrange("p (t c) -> p t c", c=FW)
                d3 = den[:, :].rearrange("p (t h) -> p t h", h=heads)
                link(dve.tensor_scalar(d3, a3[:, :, D:FW], 1e-16, None, ALU.add))
                link(dve.reciprocal(den[:, :], den[:, :]))
                link(dve.tensor_tensor(agg[:, :, :].rearrange("p t (h c) -> p t h c", h=heads),
                                       a3[:, :, 0:D].rearrange("p t (h c) -> p t h c", h=heads),
                                       d3.unsqueeze(3).to_broadcast([P, NT, heads, D // heads]), ALU.mult))
            steps(nc, f"{n}_norm", normalise)
            transpose_all(nc, k, f"{n}_at", agg, a_t)
            typed_linear(nc, k, f"{n}_o", a_t, W["Wa"][l], o_t, silu=True)
            untranspose_all(nc, k, f"{n}_on", o_t, agg)
            s_sk = ctx.enter_context(signal(nc, f"{n}_s_sk"))
            s_mix = ctx.enter_context(signal(nc, f"{n}_s_mix"))
            hit = sb("hit", [P, NT], F32, ctx)
            with nc.Block() as block:
                @block.scalar
                def _(act):
                    act.activation(sk[:, :], sk[:, :], ACT.Sigmoid).then_inc(s_sk, 1)

                @block.vector
                def _(dve):
                    link = Chain(dve, s_mix).link
                    dve.wait_ge(s_sk, 1)
                    link(dve.memset(al[:, :], 0.0))
                    for t in range(rels):
                        link(dve.tensor_scalar(hit[:, :], k.type_col[:, :], float(t), sk[:, t:t + 1],
                                               ALU.is_equal, ALU.mult))
                        link(dve.tensor_tensor(al[:, :], al[:, :], hit[:, :], ALU.add))
                    link(dve.tensor_tensor(agg[:, :, :], agg[:, :, :], X[:, :, :], ALU.subtract))
                    link(dve.tensor_tensor(agg[:, :, :], agg[:, :, :], over_last(al[:, :], D), ALU.mult))
                    link(dve.tensor_tensor(X[:, :, :], X[:, :, :], agg[:, :, :], ALU.add))
            layer_norm(nc, k, f"{n}_ln", X, gain[:, 0, :], gain[:, 1, :])


def split3_steps(link, dve, src, parts, rest):
    link(dve.tensor_copy(parts[0], src))
    link(dve.tensor_tensor(rest, src, parts[0], ALU.subtract))
    link(dve.tensor_copy(parts[1], rest))
    link(dve.tensor_tensor(rest, rest, parts[1], ALU.subtract))
    link(dve.tensor_copy(parts[2], rest))


def sage(nc, k, X, order, W, table):
    s = k.s
    NT = s.NT
    width = D + 4
    with ExitStack() as outer:
        def sb(nm, shape, dt, where=outer):
            return where.enter_context(nc.sbuf_tensor(f"sage_{nm}", shape, dt))

        acc = sb("acc", [P, 2, NT * width], F32)
        with ExitStack() as ctx:
            row = sb("row", [P, NT, width], F32, ctx)

            def fill(link, dve):
                link(dve.memset(row[:, :, D:width], 1.0))
                link(dve.tensor_copy(row[:, :, 0:D], X[:, :, :]))
            steps(nc, "sage_fill", fill)
            store_table(nc, k, "sage_store", row[:, :, :], table, [(acc[:, :, :], 0.0)])
        gather_sum(nc, k, "sage_e", order, order.row, table, width, acc)
        mean = sb("mean", [P, NT, D], F32)
        x_t = sb("x_t", [P, s.NP], F32)
        m_t = sb("m_t", [P, s.NP], F32)
        some = sb("some", [P, NT], F32)
        cnt = sb("cnt", [P, NT], F32)
        w = sb("w", [P, 2, D], F32)
        wt = sb("wt", [P, 2, D], F32)
        bias = sb("bias", [P, 2, D], F32)
        y = sb("y", [P, NT, D], F32)
        load_rows(nc, k, "sage_ld", [(w[:, 0, :], W["W_self"]), (w[:, 1, :], W["W_neigh"]),
                                     (bias[:, 0, :], row_bcast(W["b_self"])), (bias[:, 1, :], row_bcast(W["b_neigh"]))])

        def average(link, dve):
            a3 = acc[:, 0, :].rearrange("p (t c) -> p t c", c=width)
            link(dve.tensor_tensor(acc[:, 0, :], acc[:, 0, :], acc[:, 1, :], ALU.add))
            link(dve.tensor_scalar(some[:, :].unsqueeze(2), a3[:, :, D:D + 1], 0.0, None, ALU.is_gt))
            link(dve.tensor_scalar(cnt[:, :].unsqueeze(2), a3[:, :, D:D + 1], 1.0, None, ALU.max))
            link(dve.reciprocal(cnt[:, :], cnt[:, :]))
            link(dve.tensor_tensor(mean[:, :, :], a3[:, :, 0:D], over_last(cnt[:, :], D), ALU.mult))
            link(dve.tensor_tensor(y[:, :, :], over_last(some[:, :], D), over_mid(bias[:, 1, :], NT), ALU.mult))
            link(dve.tensor_tensor(y[:, :, :], y[:, :, :], over_mid(bias[:, 0, :], NT), ALU.add))
        steps(nc, "sage_avg", average)
        transpose_weights(nc, k, "sage_wt", w, wt, 2)
        transpose_all(nc, k, "sage_xt", X, x_t)
        transpose_all(nc, k, "sage_mt", mean, m_t)
        linear(nc, k, "sage_lin", [x_t, m_t], [wt[:, 0, :], wt[:, 1, :]], D, lambda a, m: mean[:, a:a + m, :])

        def finish(link, dve):
            link(dve.tensor_tensor(y[:, :, :], y[:, :, :], mean[:, :, :], ALU.add))
            link(dve.tensor_scalar(y[:, :, :], y[:, :, :], 0.0, None, ALU.max))
            link(dve.tensor_tensor(X[:, :, :], X[:, :, :], y[:, :, :], ALU.add))
        steps(nc, "sage_fin", finish)
    layer_norm(nc, k, "sage_ln", X)


def transpose_weights(nc, k, name, w, wt, n):
    def produce(pe, c, bank):
        return pe.transpose(k.psum[:, bank, 0:D], w[:, c, :], k.ident[:, :])

    banked(nc, k, name, n, produce, lambda copy, c, bank: copy(wt[:, c, :], k.psum[:, bank, 0:D]))


def gated_graph(nc, k, X, order, W, table):
    s = k.s
    NT, NP = s.NT, s.NP
    rounds = W["weight"].shape[0]
    with ExitStack() as outer:
        def sb(nm, shape, dt, where=outer):
            return where.enter_context(nc.sbuf_tensor(f"ggn_{nm}", shape, dt))

        w = sb("w", [P, 7, D], F32)
        wt = sb("wt", [P, 7, D], F32)
        wm = sb("wm", [P, rounds, D], F32)
        bias = sb("bias", [P, 7, D], F32)
        H = sb("H", [P, NT, D], F32)
        h_t = sb("h_t", [P, NP], F32)
        a_t = sb("a_t", [P, NP], F32)
        M = sb("M", [P, NT, D], F32)
        acc = sb("acc", [P, 2, NT * D], F32)
        load_rows(nc, k, "ggn_ld", [
            (w[:, 0:3, :], W["w_ih"].rearrange("(a p) c -> p a c", p=P)),
            (w[:, 3:6, :], W["w_hh"].rearrange("(a p) c -> p a c", p=P)),
            (w[:, 6, :], W["lin_w"]), (wm[:, :, :], W["weight"].rearrange("l i o -> i l o")),
            (flat(bias[:, 0:3, :]), row_bcast(W["b_ih"])), (flat(bias[:, 3:6, :]), row_bcast(W["b_hh"])),
            (bias[:, 6, :], row_bcast(W["lin_b"]))])
        transpose_weights(nc, k, "ggn_wt", w, wt, 7)
        steps(nc, "ggn_b", lambda link, dve: link(
            dve.tensor_tensor(bias[:, 0:2, :], bias[:, 0:2, :], bias[:, 3:5, :], ALU.add)))
        transpose_all(nc, k, "ggn_xt", X, h_t)
        linear(nc, k, "ggn_lin", [h_t], [wt[:, 6, :]], D, lambda a, m: H[:, a:a + m, :])
        steps(nc, "ggn_lb", lambda link, dve: link(
            dve.tensor_tensor(H[:, :, :], H[:, :, :], over_mid(bias[:, 6, :], NT), ALU.add)))
        for r in range(rounds):
            n = f"ggn{r}"
            transpose_all(nc, k, f"{n}_ht", H, h_t)
            linear(nc, k, f"{n}_m", [h_t], [wm[:, r, :]], D, lambda a, m: M[:, a:a + m, :])
            store_table(nc, k, f"{n}_st", M[:, :, :], table, [(acc[:, :, :], 0.0)])
            gather_sum(nc, k, f"{n}_e", order, order.node, table, D, acc)
            steps(nc, f"{n}_s", lambda link, dve: link(
                dve.tensor_tensor(flat(M[:, :, :]), acc[:, 0, :], acc[:, 1, :], ALU.add)))
            transpose_all(nc, k, f"{n}_at", M, a_t)
            gru(nc, k, n, H, h_t, a_t, wt, bias)
        steps(nc, "ggn_fin", lambda link, dve: link(
            dve.tensor_tensor(X[:, :, :], X[:, :, :], H[:, :, :], ALU.add)))
    layer_norm(nc, k, "ggn_ln", X)


def gru(nc, k, n, H, h_t, a_t, wt, bias):
    s = k.s
    parts = chunked(s.NT, 4)
    with ExitStack() as ctx:
        def sb(nm, shape, dt):
            return ctx.enter_context(nc.sbuf_tensor(f"{n}_{nm}", shape, dt))

        g = sb("gates", [P, 2, 4, 4, D], F32)
        t = sb("t", [P, 2, 4, D], F32)
        s_mm, s_g, s_rz, s_n, s_tanh, s_d = (ctx.enter_context(signal(nc, f"{n}_{x}"))
                                             for x in ("s_mm", "s_g", "s_rz", "s_n", "s_tanh", "s_d"))
        with nc.Block() as block:
            @block.tensor
            def _(pe):
                for c, (a, m) in enumerate(parts):
                    if c >= 2:
                        pe.wait_ge(s_g, c - 1)
                    for j in range(m):
                        bank = 4 * (c % 2) + j
                        xa, xh = a_t[:, (a + j) * P:(a + j + 1) * P], h_t[:, (a + j) * P:(a + j + 1) * P]
                        pe.matmul(k.psum[:, bank, 0:2 * D], xa, flat(wt[:, 0:2, :]), start=True, stop=False)
                        pe.matmul(k.psum[:, bank, 0:2 * D], xh, flat(wt[:, 3:5, :]), start=False, stop=True)
                        pe.matmul(k.psum[:, bank, 2 * D:3 * D], xa, wt[:, 2, :], start=True, stop=True)
                        last = pe.matmul(k.psum[:, bank, 3 * D:4 * D], xh, wt[:, 5, :], start=True, stop=True)
                    last.then_inc(s_mm, 1)

            @block.scalar
            def _(act):
                for c, (a, m) in enumerate(parts):
                    act.wait_ge(s_g, c + 1)
                    rz = g[:, c % 2, 0:m, 0:2, :]
                    act.activation(rz, rz, ACT.Sigmoid).then_inc(s_rz, 1)
                    act.wait_ge(s_n, c + 1)
                    act.activation(t[:, c % 2, 0:m, :], t[:, c % 2, 0:m, :], ACT.Tanh).then_inc(s_tanh, 1)

            @block.vector
            def _(dve):
                ch = Chain(dve, s_d)
                brow = bias[:, 0:3, :]
                for c, (a, m) in enumerate(parts):
                    b0 = 4 * (c % 2)
                    dve.wait_ge(s_mm, c + 1)
                    for j in range(m):
                        dve.tensor_tensor(g[:, c % 2, j, 0:3, :], k.psum[:, b0 + j, 0:3 * D].rearrange("p (a b) -> p a b", b=D),
                                          brow, ALU.add)
                        last = dve.tensor_tensor(g[:, c % 2, j, 3, :], k.psum[:, b0 + j, 3 * D:4 * D], bias[:, 5, :], ALU.add)
                    last.then_inc(s_g, 1)
                    dve.wait_ge(s_rz, c + 1)
                    tt = t[:, c % 2, 0:m, :]
                    ch.link(dve.tensor_tensor(tt, g[:, c % 2, 0:m, 0, :], g[:, c % 2, 0:m, 3, :], ALU.mult))
                    dve.tensor_tensor(tt, tt, g[:, c % 2, 0:m, 2, :], ALU.add).then_inc(s_n, 1)
                    dve.wait_ge(s_tanh, c + 1)
                    h = H[:, a:a + m, :]
                    ch.link(dve.tensor_tensor(h, h, tt, ALU.subtract))
                    ch.link(dve.tensor_tensor(h, h, g[:, c % 2, 0:m, 1, :], ALU.mult))
                    ch.link(dve.tensor_tensor(h, h, tt, ALU.add))


def gat(nc, k, n, in_t, ws, heads, width, att_src, att_dst, order, table, out):
    s = k.s
    NT = s.NT
    row = width + heads
    hw = width // heads
    with ExitStack() as outer:
        def sb(nm, shape, dt, where=outer):
            return where.enter_context(nc.sbuf_tensor(f"{n}_{nm}", shape, dt))

        peaks = sb("peaks", [P, NT, heads], F32)
        own = sb("own", [P, NT, heads], F32)
        to = sb("to", [P, NT, heads], F32)
        h = sb("h", [P, NT, row], F32)
        with ExitStack() as ctx:
            att = sb("att", [P, 2, width], F32, ctx)
            prod = sb("prod", [P, NT, width], F32, ctx)
            load_rows(nc, k, f"{n}_ld", [(att[:, 0, :], row_bcast(att_src)), (att[:, 1, :], row_bcast(att_dst))])
            linear(nc, k, f"{n}_h", in_t, ws, width, lambda a, m: h[:, a:a + m, 0:width])

            def node_scores(link, dve):
                for side, dst in ((0, h[:, :, width:row]), (1, to[:, :, :])):
                    link(dve.tensor_tensor(prod[:, :, :], h[:, :, 0:width], over_mid(att[:, side, :], NT), ALU.mult))
                    link(dve.tensor_reduce(dst, prod[:, :, :].rearrange("p t (h c) -> p t h c", c=hw), AX.X, ALU.add))
                link(dve.tensor_tensor(own[:, :, :], h[:, :, width:row], to[:, :, :], ALU.add))
                link(dve.tensor_scalar(peaks[:, :, :], own[:, :, :], NEG_SLOPE, None, ALU.mult))
                link(dve.tensor_tensor(own[:, :, :], own[:, :, :], peaks[:, :, :], ALU.max))
                link(dve.tensor_copy(peaks[:, :, :], own[:, :, :]))
            steps(nc, f"{n}_sc", node_scores)
        store_table(nc, k, f"{n}_st", h[:, :, :], table)
        with ExitStack() as ctx:
            to3 = sb("to3", [P, 3, NT * heads], BF16, ctx)
            rest = sb("rest", [P, NT * heads], F32, ctx)
            steps(nc, f"{n}_to3", lambda link, dve: split3_steps(
                link, dve, flat(to[:, :, :]), [to3[:, j, :] for j in range(3)], rest[:, :]))
            steps(nc, f"{n}_own", lambda link, dve: link(dve.memset(h[:, :, width:row], 1.0)))
            attend_rows(nc, k, f"{n}_e", order, order.node, table, row, "add", (0, width), heads, to3, peaks,
                        flat(h[:, :, :]))

        def normalise(link, dve):
            link(dve.tensor_copy(own[:, :, :], h[:, :, width:row]))
            link(dve.reciprocal(own[:, :, :], own[:, :, :]))
            link(dve.tensor_tensor(out[:, :, :].rearrange("p t (h c) -> p t h c", h=heads),
                                   h[:, :, 0:width].rearrange("p t (h c) -> p t h c", h=heads),
                                   own[:, :, :].unsqueeze(3).to_broadcast([P, NT, heads, hw]), ALU.mult))
        steps(nc, f"{n}_nrm", normalise)


def attention_network(nc, k, X, order, W, table1, table2):
    s = k.s
    NT, NP = s.NT, s.NP
    f1 = W["W1"].shape[1]
    with ExitStack() as outer:
        def sb(nm, shape, dt, where=outer):
            return where.enter_context(nc.sbuf_tensor(f"gat_{nm}", shape, dt))

        wrow = sb("wrow", [P, 2, f1], F32)
        o1 = sb("o1", [P, NT, f1], F32)
        x_t = flat(o1[:, :, :])[:, 0:NP]
        load_rows(nc, k, "gat_ld", [(wrow[:, 0, :], W["W1"])])
        transpose_all(nc, k, "gat_xt", X, x_t)
        gat(nc, k, "ga", [x_t], [wrow[:, 0, :]], W["att_src1"].shape[0], f1,
            W["att_src1"].rearrange("h c -> (h c)"), W["att_dst1"].rearrange("h c -> (h c)"), order, table1, o1)
        h_t = sb("h_t", [P, 2, NP], F32)
        with ExitStack() as ctx:
            b1 = sb("b1", [P, f1], F32, ctx)
            neg = sb("neg", [P, NT, f1], F32, ctx)
            load_rows(nc, k, "gat_lb", [(b1[:, :], row_bcast(W["b1"])),
                                        (wrow[:, :, 0:D], W["W2"].rearrange("(a p) c -> p a c", p=P))])
            s_n, s_e, s_d = (ctx.enter_context(signal(nc, f"gat_{x}")) for x in ("s_n", "s_e", "s_d"))
            with nc.Block() as block:
                @block.vector
                def _(dve):
                    link = Chain(dve, s_d).link
                    link(dve.tensor_tensor(o1[:, :, :], o1[:, :, :], over_mid(b1[:, :], NT), ALU.add))
                    dve.tensor_scalar(neg[:, :, :], o1[:, :, :], 0.0, None, ALU.min).then_inc(s_n, 1)
                    link(dve.tensor_scalar(o1[:, :, :], o1[:, :, :], 0.0, None, ALU.max))
                    dve.wait_ge(s_e, 1)
                    link(dve.tensor_scalar(neg[:, :, :], neg[:, :, :], -1.0, None, ALU.add))
                    link(dve.tensor_tensor(o1[:, :, :], o1[:, :, :], neg[:, :, :], ALU.add))

                @block.scalar
                def _(act):
                    act.wait_ge(s_n, 1)
                    act.activation(neg[:, :, :], neg[:, :, :], ACT.Exp).then_inc(s_e, 1)
            for half in range(2):
                transpose_all(nc, k, f"gat_ot{half}", o1[:, :, half * D:(half + 1) * D], h_t[:, half, :])
        o2 = sb("o2", [P, NT, D], F32)
        gat(nc, k, "gb", [h_t[:, 0, :], h_t[:, 1, :]], [wrow[:, 0, 0:D], wrow[:, 1, 0:D]], 1, D,
            W["att_src2"].rearrange("h c -> (h c)"), W["att_dst2"].rearrange("h c -> (h c)"), order, table2, o2)
        b2 = sb("b2", [P, D], F32)
        load_rows(nc, k, "gat_lb2", [(b2[:, :], row_bcast(W["b2"]))])

        def finish(link, dve):
            link(dve.tensor_tensor(X[:, :, :], X[:, :, :], o2[:, :, :], ALU.add))
            link(dve.tensor_tensor(X[:, :, :], X[:, :, :], over_mid(b2[:, :], NT), ALU.add))
        steps(nc, "gat_fin", finish)
    layer_norm(nc, k, "gat_ln", X)


def load_nodes(nc, k, x, node_type, X):
    s = k.s
    full = s.N // P
    left = s.N - full * P
    with ExitStack() as ctx:
        raw_row = ctx.enter_context(nc.sbuf_tensor("raw_row", [P, s.N], I32))
        raw_col = ctx.enter_context(nc.sbuf_tensor("raw_col", [P, s.NT], I32))
        s_z = ctx.enter_context(signal(nc, "ln_s_z"))
        s_in = ctx.enter_context(signal(nc, "ln_s_in"))
        s_d = ctx.enter_context(signal(nc, "ln_s_d"))
        with nc.Block() as block:
            @block.vector
            def _(dve):
                link = Chain(dve, s_d).link
                dve.memset(X[:, full, :], 0.0)
                dve.memset(raw_col[:, :], -1)
                dve.memset(k.type_row[:, s.N:s.NP], -1.0).then_inc(s_z, 1)
                dve.wait_ge(s_in, 16 * 5)
                link(dve.tensor_copy(k.type_row[:, 0:s.N], raw_row[:, :]))
                link(dve.tensor_copy(k.type_col[:, :], raw_col[:, :]))

            @block.sync
            def _(sp):
                sp.wait_ge(s_z, 1)
                sp.dma_start(X[:, 0:full, :], x[0:full * P, :].rearrange("(t p) c -> p t c", p=P)).then_inc(s_in, 16)
                sp.dma_start(X[0:left, full, :], x[full * P:s.N, :]).then_inc(s_in, 16)
                sp.dma_start(raw_row[:, :], row_bcast(node_type)).then_inc(s_in, 16)
                with nc.allow_non_contiguous_dma("node types by column, once"):
                    sp.dma_start(raw_col[:, 0:full], node_type[0:full * P].rearrange("(t p) -> p t", p=P)).then_inc(s_in, 16)
                    sp.dma_start(raw_col[0:left, full:full + 1], node_type[full * P:s.N].unsqueeze(1)).then_inc(s_in, 16)


def store_nodes(nc, k, X, out):
    s = k.s
    full = s.N // P
    left = s.N - full * P
    with signal(nc, "s_out") as s_out, nc.Block() as block:
        @block.sync
        def _(sp):
            sp.dma_start(out[0:full * P, :].rearrange("(t p) c -> p t c", p=P), X[:, 0:full, :]).then_inc(s_out, 16)
            sp.dma_start(out[full * P:s.N, :], X[0:left, full, :]).then_inc(s_out, 16)
            sp.wait_ge(s_out, 32)


def group(arrays, prefix):
    return {n[len(prefix):]: a for n, a in arrays.items() if n.startswith(prefix)}


def gnn_program(nc, a, out):
    s = Shapes(a["x"].shape[0], a["src"].shape[0])
    turn[:] = range(FIRST_SEMAPHORE, LAST_SEMAPHORE + 1)

    def dram(n, shape):
        return nc.dram_tensor(n, shape, F32, kind="Internal").ap()

    w1 = group(a, "L0_gnn_")
    rels = w1["pri"].shape[2]
    gat_w = group(a, "L3_gnn_")
    heads, f1 = gat_w["att_src1"].shape[0], gat_w["W1"].shape[1]
    with ExitStack() as ctx:
        k = Kit(nc, ctx, s)
        k.type_col = k.sb("type_col", [P, s.NT], F32)
        X = k.sb("X", [P, s.NT, D], F32)
        by_dst = Edges(k.sb, nc, s, "by_dst", True)
        by_src = Edges(k.sb, nc, s, "by_src", False)
        constants(nc, k)
        with nc.sbuf_tensor("pair", [P, s.T, 2], F16) as pair:
            k.pair = pair
            bucket_edges(nc, k, by_dst, a["dst"], a["src"], a["edge_type_8"], "bd", True)
            sort_tiles(nc, k, by_dst)
        bucket_edges(nc, k, by_src, a["src"], a["dst"], None, "bs", False)
        with nc.sbuf_tensor("type_row", [P, s.NP], F32) as type_row, nc.sbuf_tensor("X0", [P, s.NT, D], F32) as X0:
            k.type_row = type_row
            load_nodes(nc, k, a["x"], a["node_type_8"], X)
            steps(nc, "keep", lambda link, dve: link(dve.tensor_copy(X0[:, :, :], X[:, :, :])))
            table = dram("relation_table", [s.NP * rels, 2 * D])
            for l in range(w1["Wk"].shape[0]):
                graph_transformer(nc, k, l, X, by_dst, w1, table)
            with nc.sbuf_tensor("e_t", [P, s.NP], F32) as e_t, nc.sbuf_tensor("wff", [P, 2, D], F32) as wff:
                load_rows(nc, k, "ff_ld", [(wff[:, 0, :], w1["Wff"]), (wff[:, 1, :], row_bcast(w1["bff"]))])
                transpose_all(nc, k, "ff_t", X, e_t)
                linear(nc, k, "ff", [e_t], [wff[:, 0, :]], D, lambda t, m: X[:, t:t + m, :])

                def residual(link, dve):
                    link(dve.tensor_tensor(X[:, :, :], X[:, :, :], over_mid(wff[:, 1, :], s.NT), ALU.add))
                    link(dve.tensor_tensor(X[:, :, :], X[:, :, :], X0[:, :, :], ALU.add))
                steps(nc, "ff_r", residual)
        layer_norm(nc, k, "ff_ln", X)
        sage(nc, k, X, by_src, group(a, "L1_gnn_"), dram("sage_table", [s.NP, D + 4]))
        gated_graph(nc, k, X, by_dst, group(a, "L2_gnn_"), dram("message_table", [s.NP, D]))
        attention_network(nc, k, X, by_dst, gat_w, dram("gat_table1", [s.NP, f1 + heads]),
                          dram("gat_table2", [s.NP, D + 1]))
        store_nodes(nc, k, X, out)


def kernel(**inputs):
    import concourse.bacc as bacc
    from concourse.bass_utils import run_bass_kernel_spmd

    nc = bacc.Bacc("TRN2", target_bir_lowering=False, num_devices=1)
    arrays, aps = {}, {}
    for name, value in inputs.items():
        arrays[f"in_{name}"] = np.ascontiguousarray(value)
        aps[name] = nc.dram_tensor(f"in_{name}", arrays[f"in_{name}"].shape,
                                   mybir.dt.from_np(arrays[f"in_{name}"].dtype), kind="ExternalInput").ap()
    nodes, features = inputs["x"].shape
    out = nc.dram_tensor("out", [nodes, features], F32, kind="ExternalOutput").ap()
    gnn_program(nc, aps, out)
    result = run_bass_kernel_spmd(nc, [arrays], core_ids=[0])
    return result.results[0]["out"]
```
